# Optimizing a Trainium2 kernel written in Bass

```python
import numpy as np
import jax
import jax.numpy as jnp

def _softmax(x, axis=-1):
    return jax.nn.softmax(x, axis=axis)

def _gelu(x):
    return jax.nn.gelu(x, approximate=True)

def _silu(x):
    return jax.nn.silu(x)

def _sigmoid(x):
    return jax.nn.sigmoid(x)

def _layernorm(x, axis=-1, eps=1e-05):
    m = jnp.mean(x, axis=axis, keepdims=True)
    v = jnp.var(x, axis=axis, keepdims=True)
    return (x - m) / jnp.sqrt(v + eps)

def _scatter_add(tgt, idx, src, axis=0):
    return tgt.at[idx].add(src)

def _segment_sum(src, seg, n):
    return jax.ops.segment_sum(src, seg, n)
kernel_name = 'mk_xattn_ffn_d2_seqx_r8_a5570a'

def setup_inputs(seed: int=0):
    np.random.seed(seed)
    _w = jnp.asarray

    def _rec_inputs():
        import jax
        import jax.numpy as jnp
        _rk = jax.random.key(seed)
        x = -0.0003929 + 0.9999 * jax.random.normal(jax.random.fold_in(_rk, 1), (32, 64, 512), jnp.float32)
        _lenS = 64 - jax.random.randint(jax.random.fold_in(_rk, 7), (32,), 0, max(1, 64 // 4) + 1, jnp.int32)
        _lenS2 = 64 - jax.random.randint(jax.random.fold_in(_rk, 8), (32,), 0, max(1, 64 // 4) + 1, jnp.int32)
        _ctx_4096P = jax.random.normal(jax.random.fold_in(_rk, 11), (32, 16, 512), jnp.float32)
        _ctx_4096c = jax.random.dirichlet(jax.random.fold_in(_rk, 511), 0.3 * jnp.ones((16,), jnp.float32), (32, 64))
        _ctx_4096t = jnp.einsum('bsk,bkd->bsd', _ctx_4096c, _ctx_4096P)
        _ctx_4096t = _ctx_4096t * jax.lax.rsqrt(jnp.mean(jnp.square(_ctx_4096t)) + 1e-12) * 0.953939
        ctx_4096 = 2.81802e-05 + 1.00001 * (_ctx_4096t + 0.3 * jax.random.normal(jax.random.fold_in(_rk, 611), (32, 64, 512), jnp.float32))
        return (x, ctx_4096)
    x, ctx_4096 = _rec_inputs()

    def _L0_xattn_setup():
        import jax, jax.numpy as jnp
        import numpy as np
        B, S, F = (2, 256, 512)
        HQ, HKV, D = (32, 8, 128)
        REP = HQ // HKV
        key = jax.random.key(seed)
        ks = jax.random.split(key, 6)
        scale = 0.02
        return {'query': jax.random.normal(ks[0], (B, S, F), jnp.float32), 'value': jax.random.normal(ks[1], (B, S, F), jnp.float32), 'wq': jax.random.normal(ks[2], (F, HQ * D), jnp.float32) * scale, 'wk': jax.random.normal(ks[3], (F, HKV * D), jnp.float32) * scale, 'wv': jax.random.normal(ks[4], (F, HKV * D), jnp.float32) * scale, 'wo': jax.random.normal(ks[5], (HQ * D, F), jnp.float32) * scale}
    _L0_xattn_all = _L0_xattn_setup()
    _L0_xattn_in = {k: v for k, v in _L0_xattn_all.items() if k in ('wq', 'wk', 'wv', 'wo')}
    del _L0_xattn_all

    def _L0_ffn_setup():
        import jax, jax.numpy as jnp
        import numpy as np
        FP8_MAX = 448.0
        CHUNK = 128

        def _quant_dequant_fp8(x):
            M, K = x.shape
            C = K // CHUNK
            xr = x.reshape(M, C, CHUNK)
            amax = jnp.max(jnp.abs(xr), axis=-1, keepdims=True)
            scale = jnp.maximum(amax, 0.0001) / FP8_MAX
            q = (xr / scale).astype(jnp.float8_e4m3fn)
            deq = q.astype(jnp.float32) * scale
            return deq.reshape(M, K)
        key = jax.random.key(seed)
        k0, k1, k2, k3, k4 = jax.random.split(key, 5)
        B, L, H, I = (2, 512, 512, 1792)
        X0 = jax.random.normal(k0, (B, L, H), dtype=jnp.float32)
        W0 = (jax.random.normal(k1, (I, H), dtype=jnp.float32) * 0.02).astype(jnp.bfloat16)
        bias0 = (jax.random.normal(k2, (I,), dtype=jnp.float32) * 0.02).astype(jnp.bfloat16)
        W1 = (jax.random.normal(k3, (H, I), dtype=jnp.float32) * 0.02).astype(jnp.bfloat16)
        bias1 = (jax.random.normal(k4, (H,), dtype=jnp.float32) * 0.02).astype(jnp.bfloat16)
        return {'X0': X0, 'W0': W0, 'bias0': bias0, 'W1': W1, 'bias1': bias1}
    _L0_ffn_all = _L0_ffn_setup()
    _L0_ffn_in = {k: v for k, v in _L0_ffn_all.items() if k in ('W0', 'bias0', 'W1', 'bias1')}
    del _L0_ffn_all

    def _L1_xattn_setup():
        import jax, jax.numpy as jnp
        import numpy as np
        DIM = 512
        NUM_HEADS = 32
        NUM_KV_HEADS = 8
        HEAD_DIM = DIM // NUM_HEADS
        KV_DIM = DIM // (NUM_HEADS // NUM_KV_HEADS)
        B, S = (1, 256)
        key = jax.random.key(seed)
        ks = jax.random.split(key, 7)
        w_scale = DIM ** (-0.5)
        return {'query': jax.random.normal(ks[0], (B, S, DIM), jnp.float32), 'key': jax.random.normal(ks[1], (B, S, DIM), jnp.float32), 'value': jax.random.normal(ks[2], (B, S, DIM), jnp.float32), 'Wq': jax.random.normal(ks[3], (DIM, DIM), jnp.float32) * w_scale, 'Wk': jax.random.normal(ks[4], (DIM, KV_DIM), jnp.float32) * w_scale, 'Wv': jax.random.normal(ks[5], (DIM, KV_DIM), jnp.float32) * w_scale, 'Wo': jax.random.normal(ks[6], (DIM, DIM), jnp.float32) * w_scale}
    _L1_xattn_all = _L1_xattn_setup()
    _L1_xattn_in = {k: v for k, v in _L1_xattn_all.items() if k in ('Wq', 'Wk', 'Wv', 'Wo')}
    del _L1_xattn_all

    def _L1_ffn_setup():
        import jax, jax.numpy as jnp
        import numpy as np
        IN_F = 512
        OUT_F = 512
        N_CLUSTERS = 64
        THRESHOLD = 0.01
        TEMPERATURE = 0.1
        BATCH, SEQ = (4, 256)
        key = jax.random.key(seed)
        k1, k2, k3, k4, k5 = jax.random.split(key, 5)
        s = 1.0 / np.sqrt(IN_F)
        return {'input': jax.random.normal(k1, (BATCH, SEQ, IN_F), dtype=jnp.float32), 'weight': jax.random.normal(k2, (OUT_F, IN_F), dtype=jnp.float32) * s, 'bias': jax.random.uniform(k3, (OUT_F,), dtype=jnp.float32, minval=-s, maxval=s), 'centroids': jax.random.normal(k4, (N_CLUSTERS, IN_F), dtype=jnp.float32) * s, 'assignments': jax.random.randint(k5, (OUT_F,), 0, N_CLUSTERS, dtype=jnp.int32)}
    _L1_ffn_all = _L1_ffn_setup()
    _L1_ffn_in = {k: v for k, v in _L1_ffn_all.items() if k in ('weight', 'bias', 'centroids', 'assignments')}
    del _L1_ffn_all
    return {'x': x, 'ctx_4096': ctx_4096, 'L0_xattn_wq': _L0_xattn_in['wq'], 'L0_xattn_wk': _L0_xattn_in['wk'], 'L0_xattn_wv': _L0_xattn_in['wv'], 'L0_xattn_wo': _L0_xattn_in['wo'], 'L0_ffn_W0': _L0_ffn_in['W0'], 'L0_ffn_bias0': _L0_ffn_in['bias0'], 'L0_ffn_W1': _L0_ffn_in['W1'], 'L0_ffn_bias1': _L0_ffn_in['bias1'], 'L1_xattn_Wq': _L1_xattn_in['Wq'], 'L1_xattn_Wk': _L1_xattn_in['Wk'], 'L1_xattn_Wv': _L1_xattn_in['Wv'], 'L1_xattn_Wo': _L1_xattn_in['Wo'], 'L1_ffn_weight': _L1_ffn_in['weight'], 'L1_ffn_bias': _L1_ffn_in['bias'], 'L1_ffn_centroids': _L1_ffn_in['centroids'], 'L1_ffn_assignments': _L1_ffn_in['assignments']}

def reference(x, ctx_4096, L0_xattn_wq, L0_xattn_wk, L0_xattn_wv, L0_xattn_wo, L0_ffn_W0, L0_ffn_bias0, L0_ffn_W1, L0_ffn_bias1, L1_xattn_Wq, L1_xattn_Wk, L1_xattn_Wv, L1_xattn_Wo, L1_ffn_weight, L1_ffn_bias, L1_ffn_centroids, L1_ffn_assignments):
    import jax
    import jax.numpy as jnp

    def _L0_xattn_ref(query, value, wq, wk, wv, wo):
        import jax, jax.numpy as jnp
        import numpy as np
        B, S, F = (2, 256, 512)
        HQ, HKV, D = (32, 8, 128)
        REP = HQ // HKV
        key = value
        b, tq, _ = query.shape
        tk = key.shape[1]
        q = (query @ wq).reshape(b, tq, HQ, D)
        k = (key @ wk).reshape(b, tk, HKV, D)
        v = (value @ wv).reshape(b, tk, HKV, D)
        k = jnp.repeat(k, REP, axis=2)
        v = jnp.repeat(v, REP, axis=2)
        q = q * (1.0 / jnp.sqrt(jnp.asarray(D, q.dtype)))
        scores = jnp.einsum('bqhd,bkhd->bhqk', q, k)
        probs = jax.nn.softmax(scores, axis=-1)
        out = jnp.einsum('bhqk,bkhd->bqhd', probs, v).reshape(b, tq, HQ * D)
        return out @ wo

    def _L0_ffn_ref(X0, W0, bias0, W1, bias1):
        import jax, jax.numpy as jnp
        import numpy as np
        FP8_MAX = 448.0
        CHUNK = 128

        def _quant_dequant_fp8(x):
            M, K = x.shape
            C = K // CHUNK
            xr = x.reshape(M, C, CHUNK)
            amax = jnp.max(jnp.abs(xr), axis=-1, keepdims=True)
            scale = jnp.maximum(amax, 0.0001) / FP8_MAX
            q = (xr / scale).astype(jnp.float8_e4m3fn)
            deq = q.astype(jnp.float32) * scale
            return deq.reshape(M, K)
        B, L, H = X0.shape
        compute_dtype = W0.dtype
        X = X0.astype(compute_dtype).astype(jnp.float32).reshape(-1, H)
        W0d = _quant_dequant_fp8(W0.astype(jnp.float32))
        W1d = _quant_dequant_fp8(W1.astype(jnp.float32))
        Xd = _quant_dequant_fp8(X)
        D = Xd @ W0d.T + bias0.astype(jnp.float32)
        D = jax.nn.gelu(D, approximate=False)
        D = D.astype(compute_dtype).astype(jnp.float32)
        Dd = _quant_dequant_fp8(D)
        E = Dd @ W1d.T + bias1.astype(jnp.float32)
        return E.astype(compute_dtype).reshape(B, L, H)

    def _L1_xattn_ref(query, key, value, Wq, Wk, Wv, Wo):
        import jax, jax.numpy as jnp
        import numpy as np
        DIM = 512
        NUM_HEADS = 32
        NUM_KV_HEADS = 8
        HEAD_DIM = DIM // NUM_HEADS
        KV_DIM = DIM // (NUM_HEADS // NUM_KV_HEADS)
        B, S = (1, 256)
        b, sq, _ = query.shape
        _, sk, _ = key.shape
        rep = NUM_HEADS // NUM_KV_HEADS
        q = (query @ Wq).reshape(b, sq, NUM_HEADS, HEAD_DIM).transpose(0, 2, 1, 3)
        k = (key @ Wk).reshape(b, sk, NUM_KV_HEADS, HEAD_DIM).transpose(0, 2, 1, 3)
        v = (value @ Wv).reshape(b, sk, NUM_KV_HEADS, HEAD_DIM).transpose(0, 2, 1, 3)
        k = jnp.repeat(k, rep, axis=1)
        v = jnp.repeat(v, rep, axis=1)
        scale = HEAD_DIM ** (-0.5)
        scores = jnp.einsum('bhqd,bhkd->bhqk', q, k) * scale
        probs = jax.nn.softmax(scores, axis=-1)
        out = jnp.einsum('bhqk,bhkd->bhqd', probs, v)
        out = out.transpose(0, 2, 1, 3).reshape(b, sq, DIM)
        return out @ Wo

    def _L1_ffn_ref(input, weight, bias, centroids, assignments):
        import jax, jax.numpy as jnp
        import numpy as np
        IN_F = 512
        OUT_F = 512
        N_CLUSTERS = 64
        THRESHOLD = 0.01
        TEMPERATURE = 0.1
        BATCH, SEQ = (4, 256)
        shape = input.shape
        x = input.reshape(-1, shape[-1])
        dots = jax.nn.softmax(x @ centroids.T / TEMPERATURE, axis=-1)
        hits = dots > THRESHOLD
        query_sel = jnp.any(hits, axis=1)
        cluster_sel = jnp.any(hits, axis=0)
        row_sel = cluster_sel[assignments]
        dense = x @ weight.T + bias
        out = jnp.where(query_sel[:, None] & row_sel[None, :], dense, jnp.zeros((), dense.dtype))
        return out.reshape(*shape[:-1], -1)
    x = x + _L0_xattn_ref(_layernorm(x, axis=-1), ctx_4096, L0_xattn_wq, L0_xattn_wk, L0_xattn_wv, L0_xattn_wo)
    x = x + _L0_ffn_ref(_layernorm(x, axis=-1), L0_ffn_W0, L0_ffn_bias0, L0_ffn_W1, L0_ffn_bias1)
    x = x + _L1_xattn_ref(_layernorm(x, axis=-1), ctx_4096, ctx_4096, L1_xattn_Wq, L1_xattn_Wk, L1_xattn_Wv, L1_xattn_Wo)
    x = x + _L1_ffn_ref(_layernorm(x, axis=-1), L1_ffn_weight, L1_ffn_bias, L1_ffn_centroids, L1_ffn_assignments)
    return x

_drawn_inputs = setup_inputs


def setup_inputs(seed=0):
    import zlib

    import numpy as np

    out = dict(_drawn_inputs(seed))
    spreads = {}
    factors = {'L0_xattn_wq': 2.779,
     'L0_xattn_wk': 2.775,
     'L0_ffn_bias0': 6.194,
     'L0_ffn_bias1': 3.509,
     'L1_ffn_bias': 3.646}
    for name, (base, spread) in spreads.items():
        noise = np.random.default_rng([zlib.crc32(name.encode()), seed]).standard_normal(out[name].shape)
        drawn = base * np.exp(spread * noise) if base else spread * noise
        out[name] = jnp.asarray(drawn.astype(out[name].dtype))
    for name, factor in factors.items():
        out[name] = (out[name] * factor).astype(out[name].dtype)
    return out
```

```python
import concourse.bass as bass
from concourse import mybir
from contextlib import ExitStack

F32 = mybir.dt.float32
F16 = mybir.dt.float16
BF16 = mybir.dt.bfloat16
U32 = mybir.dt.uint32
I32 = mybir.dt.int32
ALU = mybir.AluOpType
ACT = mybir.ActivationFunctionType
AX = mybir.AxisListType

P = 128
BATCH, SEQ, DIM = 32, 64, 512
TOKENS = BATCH * SEQ
TILES = TOKENS // P
KC = DIM // P
BLOCK = 512
BLOCKS = TOKENS // BLOCK
BT = BLOCK // P
BB = BLOCK // SEQ
GROUPS, REP = 8, 4
HEAD0 = 128
HEAD1 = 16
INNER = 1792
IC = INNER // P
NQ = 448
CLUSTERS = 64
THRESHOLD, TEMPERATURE = 0.01, 0.1
EPS = 1e-5
FP8_MAX, AMAX_MIN = 448.0, 1e-4
WEIGHT_SCALE = 64.0
UNSCALE = 1.0 / WEIGHT_SCALE
PASSES = ((0, 0), (0, 1), (1, 0))


SCALE_STEPS = 16
SUBNORMAL = 1.5 * 2.0 ** -6
TO_GRID = 2.0 ** 20


def quant_scales(dve, amax, scale, rec_hi, rec_lo, tmp, step, base):
    u = lambda a: a.bitcast(U32)
    clamped, top, rest, rem, s_hi = (tmp[:, i] for i in range(5))
    stt = lambda o, a, c, b, op0, op1: dve.scalar_tensor_tensor(out=o, in0=a, scalar=c, in1=b, op0=op0, op1=op1)
    ops = (
        lambda: dve.tensor_scalar(clamped, amax, AMAX_MIN, None, ALU.max),
        lambda: dve.tensor_scalar(scale, clamped, 1.0 / FP8_MAX, None, ALU.mult),
        lambda: dve.tensor_scalar(u(top), u(scale), 0xFFFFF000, None, ALU.bitwise_and),
        lambda: dve.tensor_tensor(rest, scale, top, ALU.subtract),
        lambda: stt(rem, top, -FP8_MAX, clamped, ALU.mult, ALU.add),
        lambda: stt(rem, rest, -FP8_MAX, rem, ALU.mult, ALU.add),
        lambda: stt(scale, rem, 1.0 / FP8_MAX, scale, ALU.mult, ALU.add),
        lambda: dve.reciprocal(rest, scale),
        lambda: dve.tensor_scalar(u(rec_hi), u(rest), 0xFFFFFF00, None, ALU.bitwise_and),
        lambda: dve.tensor_scalar(u(s_hi), u(scale), 0xFFFF0000, None, ALU.bitwise_and),
        lambda: dve.tensor_tensor(top, s_hi, rec_hi, ALU.mult),
        lambda: dve.tensor_tensor(s_hi, scale, s_hi, ALU.subtract),
        lambda: dve.tensor_scalar(top, top, -1.0, 1.0, ALU.mult, ALU.add),
        lambda: dve.tensor_tensor(s_hi, s_hi, rec_hi, ALU.mult),
        lambda: dve.tensor_tensor(top, top, s_hi, ALU.subtract),
        lambda: dve.tensor_tensor(rec_lo, top, rest, ALU.mult),
    )
    assert len(ops) == SCALE_STEPS
    for n, op in enumerate(ops):
        if n:
            dve.wait_ge(step, base + n)
        op().then_inc(step, 1)


def to_grid(dve, V, M, src, rec_lo, chunks, sems, at):
    w_done, v_done, bits, m_done, done = sems
    dve.wait_ge(w_done, at)
    for c in range(chunks):
        last = dve.scalar_tensor_tensor(out=V[:, c, :], in0=src[:, c, :], scalar=rec_lo(c), in1=V[:, c, :],
                                        op0=ALU.mult, op1=ALU.add)
    last.then_inc(v_done, 1)
    dve.wait_ge(v_done, at)
    dve.tensor_scalar(M.bitcast(U32), V.bitcast(U32), 0x7F800000, 0x00400000,
                      ALU.bitwise_and, ALU.bitwise_or).then_inc(bits, 1)
    dve.wait_ge(bits, at)
    dve.tensor_scalar(M, M, SUBNORMAL, TO_GRID, ALU.max, ALU.mult).then_inc(m_done, 1)
    dve.wait_ge(m_done, at)
    dve.tensor_tensor(V, V, M, ALU.add).then_inc(done, 1)


def fused_decoder_kernel(nc, x, ctx, wq0, wk0, wv0, wo0, w0, b0, w1, b1,
                         wq1, wk1, wv1, wo1, weight, bias, centroids, assignments, out):
    stack = ExitStack()
    with stack:
        def sb(where, name, shape, dt):
            return where.enter_context(nc.sbuf_tensor(name, shape, dt))

        def pb(where, name, shape=(P, 512)):
            return where.enter_context(nc.psum_tensor(name, list(shape), F32))

        def sem(where, name):
            return where.enter_context(nc.semaphore(name))

        X = sb(stack, "X", [P, TILES, DIM], F32)
        ident = sb(stack, "ident", [P, P], F32)
        CT = sb(stack, "CT", [P, 2, KC, TOKENS], F16)
        rstd = sb(stack, "rstd", [P, TILES], F32)
        nmr = sb(stack, "nmr", [P, TILES], F32)

        bn = sb(stack, "bn", [P, TILES, 6], F32)
        mv = sb(stack, "mv", [P, TILES, 2], F32)
        var_eps, root, guess, work = (sb(stack, n, [P, TILES], F32) for n in ("var_eps", "root", "guess", "ln_work"))
        stat, var_ready, root_ready, ln_step, stats_ready = (
            sem(stack, n) for n in ("stat", "var_ready", "root_ready", "ln_step", "stats_ready"))
        LN_STEPS = 6
        PARTS = {0: BLOCKS, 1: 1, 2: 1, 3: 1}

        def parts_before(use):
            return sum(PARTS[u] for u in range(use))

        def ln_stats_vector(dve, use, loaded=None):
            per = TILES // PARTS[use]
            for part in range(PARTS[use]):
                at = parts_before(use) + part
                s = slice(part * per, (part + 1) * per)
                if loaded is not None:
                    dve.wait_ge(loaded[part], 16)
                for i in range(part * per, (part + 1) * per):
                    dve.bn_stats(bn[:, i, :], X[:, i, :]).then_inc(stat, 1)
                for i in range(part * per, (part + 1) * per):
                    dve.wait_ge(stat, use * TILES + i + 1)
                    last = dve.bn_aggr(mv[:, i, :], bn[:, i, :])
                last.then_inc(ln_step, 1)
                steps = at * LN_STEPS + 1
                dve.wait_ge(ln_step, steps)
                dve.tensor_scalar(var_eps[:, s], mv[:, s, 1], EPS, None, ALU.add).then_inc(var_ready, 1)
                dve.wait_ge(root_ready, at + 1)
                dve.reciprocal(guess[:, s], root[:, s]).then_inc(ln_step, 1)
                for op in (lambda: dve.tensor_tensor(work[:, s], guess[:, s], guess[:, s], ALU.mult),
                           lambda: dve.tensor_tensor(work[:, s], work[:, s], var_eps[:, s], ALU.mult),
                           lambda: dve.tensor_scalar(work[:, s], work[:, s], -0.5, 1.5, ALU.mult, ALU.add),
                           lambda: dve.tensor_tensor(rstd[:, s], work[:, s], guess[:, s], ALU.mult)):
                    steps += 1
                    dve.wait_ge(ln_step, steps)
                    op().then_inc(ln_step, 1)
                steps += 1
                assert steps == (at + 1) * LN_STEPS
                dve.wait_ge(ln_step, steps)
                dve.scalar_tensor_tensor(out=nmr[:, s], in0=mv[:, s, 0], scalar=-1.0, in1=rstd[:, s],
                                         op0=ALU.mult, op1=ALU.mult).then_inc(stats_ready, 1)

        def ln_stats_scalar(act, use):
            per = TILES // PARTS[use]
            for part in range(PARTS[use]):
                s = slice(part * per, (part + 1) * per)
                act.wait_ge(var_ready, parts_before(use) + part + 1)
                act.activation(root[:, s], var_eps[:, s], ACT.Sqrt).then_inc(root_ready, 1)

        ln = (ln_stats_vector, ln_stats_scalar, stats_ready, parts_before)

        xt_scope = stack.enter_context(ExitStack())
        XT = sb(xt_scope, "XT", [P, 2, KC, TOKENS], F16)
        w0t = nc.dram_tensor("w0t", [P, 2 * KC * INNER], F16, kind="Internal").ap()
        w1t = nc.dram_tensor("w1t", [P, 2 * IC * DIM], F16, kind="Internal").ap()
        with ExitStack() as ph:
            CS = sb(ph, "CS", [P, TILES, DIM], F32)
            XN = sb(ph, "XN", [P, 2, DIM], F32)
            tp = [pb(ph, f"p0_tp{i}") for i in range(4)]
            x_ld = [sem(ph, f"x_ld{i}") for i in range(BLOCKS)]
            c_ld = [sem(ph, f"c_ld{i}") for i in range(BLOCKS)]
            ident_ready = sem(ph, "ident_ready")
            xn_ready = sem(ph, "xn_ready")
            tp_done = sem(ph, "p0_tp_done")
            hi_done = sem(ph, "p0_hi_done")
            lo_done = sem(ph, "p0_lo_done")
            block = ph.enter_context(nc.Block())

            @block.sync
            def _(sp):
                for i in range(BLOCKS):
                    rows = slice(i * BLOCK, (i + 1) * BLOCK)
                    sp.dma_start(CS[:, i * BT:(i + 1) * BT, :],
                                 ctx[rows, :].rearrange("(t p) d -> p t d", p=P)).then_inc(c_ld[i], 16)
                    sp.dma_start(X[:, i * BT:(i + 1) * BT, :],
                                 x[rows, :].rearrange("(t p) d -> p t d", p=P)).then_inc(x_ld[i], 16)

            @block.gpsimd
            def _(pool):
                pool.memset(ident[:, :], 0.0).then_inc(ident_ready, 1)
                pool.wait_ge(ident_ready, 1)
                pool.affine_select(out=ident[:, :], in_=ident[:, :], compare_op=ALU.not_equal, fill=1.0,
                                   base=0, pattern=[[-1, P]], channel_multiplier=1).then_inc(ident_ready, 1)

            @block.tensor
            def _(pe):
                pe.wait_ge(ident_ready, 2)
                for n in range(2 * TILES):
                    if n < TILES:
                        if n % BT == 0:
                            pe.wait_ge(c_ld[n // BT], 16)
                        src = CS[:, n, :]
                    else:
                        pe.wait_ge(xn_ready, n - TILES + 1)
                        src = XN[:, n % 2, :]
                    if n >= 4:
                        pe.wait_ge(lo_done, n - 3)
                    for k in range(KC):
                        last = pe.transpose(tp[n % 4][:, k * P:(k + 1) * P], src[:, k * P:(k + 1) * P], ident[:, :])
                    last.then_inc(tp_done, 1)

            def dst(n, part):
                to = (CT, XT)[n // TILES]
                i = n % TILES
                return to[:, part, :, i * P:(i + 1) * P]

            def bank(n):
                return tp[n % 4][:, :].rearrange("p (k t) -> p k t", k=KC)

            @block.scalar
            def _(act):
                for n in range(2 * TILES):
                    if n == 4:
                        ln_stats_scalar(act, 0)
                    act.wait_ge(tp_done, n + 1)
                    act.activation(dst(n, 0), bank(n), ACT.Copy).then_inc(hi_done, 1)

            @block.vector
            def _(dve):
                def low(n):
                    dve.wait_ge(hi_done, n + 1)
                    dve.tensor_tensor(dst(n, 1), bank(n), dst(n, 0), ALU.subtract).then_inc(lo_done, 1)

                for n in range(4):
                    low(n)
                ln_stats_vector(dve, 0, x_ld)
                for n in range(4, TILES):
                    low(n)
                for i in range(TILES):
                    dve.wait_ge(stats_ready, i // BT + 1)
                    if i >= 2:
                        dve.wait_ge(tp_done, TILES + i - 1)
                    dve.tensor_scalar(XN[:, i % 2, :], X[:, i, :], rstd[:, i:i + 1], nmr[:, i:i + 1],
                                      ALU.mult, ALU.add).then_inc(xn_ready, 1)
                    if i >= 1:
                        low(TILES + i - 1)
                low(2 * TILES - 1)

        attention0(nc, sb, pb, sem, X, ident, XT, CT, wq0, wk0, wv0, wo0, w0, w1, w0t, w1t)
        xt_scope.close()
        ffn0(nc, sb, pb, sem, X, ident, rstd, nmr, ln, w0t, w1t, b0, b1)
        attention1(nc, sb, pb, sem, X, ident, CT, rstd, nmr, ln, wq1, wk1, wv1, wo1)
        ffn1(nc, sb, pb, sem, X, ident, rstd, nmr, ln, weight, bias, centroids, assignments, out)


def attention0(nc, sb, pb, sem, X, ident, XT, CT, wq, wk, wv, wo, w0, w1, w0t_dram, w1t_dram):
    NQH = REP * HEAD0
    exp_scale = float(HEAD0) ** -0.5
    with ExitStack() as ph:
        SQ = sb(ph, "SQ", [P, KC, NQH], F32)
        SKV = sb(ph, "SKV", [P, KC, 2, HEAD0], F32)
        SO = sb(ph, "SO", [P, REP, DIM], F32)
        WQ = sb(ph, "WQ", [P, 2, KC, NQH], F16)
        WKV = sb(ph, "WKV", [P, 2, KC, 2, HEAD0], F16)
        WO = sb(ph, "WO", [P, 2, REP, DIM], F16)
        QT = sb(ph, "QT", [P, 2, BB, REP, SEQ], F16)
        KT = sb(ph, "KT", [P, 2, BB, SEQ], F16)
        V = sb(ph, "V", [P, 2, BT, 2, HEAD0], F16)
        E = sb(ph, "E", [P, 2, BB, SEQ], F32)
        ST = sb(ph, "ST", [P, 3, 2, BB], F32)
        PT = sb(ph, "PT", [P, 2, BT, REP * SEQ], F16)
        OT = sb(ph, "OT", [P, 2, REP, BLOCK], F16)
        WB = sb(ph, "WB", [P, 16, P], BF16)
        VW = sb(ph, "VW", [P, 8, P], F32)
        MW = sb(ph, "MW", [P, 8, P], F32)
        wa, ws, wh, wl = (sb(ph, "w" + n, [P, 16], F32) for n in ("amax", "scale", "rec_hi", "rec_lo"))
        wtmp = sb(ph, "wtmp", [P, 5, 16], F32)
        WS0 = sb(ph, "WS0", [P, 2, KC, 2 * P], F16)
        WS1 = sb(ph, "WS1", [P, 2, 2, DIM], F16)
        sc = [pb(ph, f"sc{i}") for i in range(2)]
        pj = [pb(ph, f"pj{i}") for i in range(2)]
        tv = [pb(ph, f"tv{i}") for i in range(2)]
        xp = [pb(ph, f"xp{i}") for i in range(2)]
        names = ("zeroed sq_ld skv_ld so_ld qkv_hi qkv_lo o_hi o_lo sc_done pj_done tp_done pv_done xp_done "
                 "exp_done pj_hi tp_hi ot_hi max_done sub_done sum_done rcp_done p_done pj_lo tp_lo ot_lo x_acc "
                 "wb_ld wa_done wstep ww_done wv_done wbits wm_done wsum wqs_done wq_done wt_done wt_hi wt_lo w_st")
        S = {n: sem(ph, "a0_" + n) for n in names.split()}
        block = ph.enter_context(nc.Block())
        SPG = BLOCKS
        PREP = ((1, 0, 4), (2, 4, 12), (3, 12, 16))

        def n_of(g, t, per, c):
            return g * (SPG * per) + (t * per + c)

        @block.sync
        def _(sp):
            def load_qkv(g):
                sp.dma_start(SQ[:, :, :], wq[:, bass.ds(g * NQH, NQH)].rearrange("(c p) n -> p c n", p=P)).then_inc(S["sq_ld"], 16)
                for i, w in enumerate((wk, wv)):
                    sp.dma_start(SKV[:, :, i, :], w[:, bass.ds(g * HEAD0, HEAD0)].rearrange("(c p) n -> p c n", p=P)).then_inc(S["skv_ld"], 16)

            def load_o(g):
                sp.dma_start(SO[:, :, :], wo[bass.ds(g * NQH, NQH), :].rearrange("(j p) n -> p j n", p=P)).then_inc(S["so_ld"], 16)

            load_qkv(0)
            load_o(0)
            with sp.Fori(0, GROUPS - 1) as g:
                sp.dma_start(WB[:, 0:8, :].rearrange("p (t c) k -> p t (c k)", t=2),
                             w0[bass.ds(g * 256, 256), :].rearrange("(t p) k -> p t k", p=P)).then_inc(S["wb_ld"], 16)
                sp.dma_start(WB[:, 8:16, :].rearrange("p (t c) k -> p t (c k)", t=4),
                             w1[:, bass.ds(g * 256, 256)].rearrange("(t p) k -> p t k", p=P)).then_inc(S["wb_ld"], 16)
                sp.wait_ge(S["qkv_lo"], g * 2 + 2)
                load_qkv(g + 1)
                sp.wait_ge(S["wt_lo"], g * 4 + 4)
                sp.dma_start(w0t_dram.rearrange("p (s c n) -> p s c n", s=2, c=KC)[:, :, :, bass.ds(g * 256, 256)],
                             WS0[:, :, :, :]).then_inc(S["w_st"], 16)
                sp.dma_start(w1t_dram.rearrange("p (s c n) -> p s c n", s=2, c=IC)[:, :, bass.ds(g * 2, 2), :],
                             WS1[:, :, :, :]).then_inc(S["w_st"], 16)
                sp.wait_ge(S["w_st"], g * 32 + 32)
                sp.wait_ge(S["o_lo"], g + 1)
                load_o(g + 1)

        @block.gpsimd
        def _(pool):
            pool.memset(V[:, :, :, :, :], 0.0).then_inc(S["zeroed"], 1)
            with pool.Fori(0, GROUPS - 1) as g:
                for n, (t, lo, hi) in enumerate(PREP):
                    v = VW[:, 0:hi - lo, :]
                    pool.wait_ge(S["wsum"], g * 3 + (n + 1))
                    pool.tensor_tensor(v, v, MW[:, 0:hi - lo, :], ALU.subtract).then_inc(S["wq_done"], 1)
                    pool.wait_ge(S["wq_done"], g * 3 + (n + 1))
                    pool.tensor_tensor(v, v, ws[:, lo:hi].unsqueeze(2).to_broadcast([P, hi - lo, P]), ALU.mult).then_inc(S["wqs_done"], 1)

        @block.tensor
        def _(pe):
            def project(g, t, units):
                for u in units:
                    bank = pj[u % 2]
                    if u == 0:
                        pe.wait_ge(S["qkv_lo"], g * 2 + 2)
                    if not (isinstance(g, int) and g == 0 and t == 0 and u < 2):
                        pe.wait_ge(S["pj_lo"], n_of(g, t, 6, u - 1))
                    tokens = slice(t * BLOCK, (t + 1) * BLOCK)
                    if u < 5:
                        for n, (k, (a, b)) in enumerate([(k, ab) for ab in PASSES for k in range(KC)]):
                            w = WQ[:, a, k, u * HEAD0:(u + 1) * HEAD0] if u < 4 else WKV[:, a, k, 0, :]
                            src = XT if u < 4 else CT
                            last = pe.matmul(bank[:, :], w, src[:, b, k, tokens], start=n == 0, stop=n == 3 * KC - 1)
                    else:
                        for i in range(BT):
                            for n, (k, (a, b)) in enumerate([(k, ab) for ab in PASSES for k in range(KC)]):
                                own = slice(t * BLOCK + i * P, t * BLOCK + (i + 1) * P)
                                last = pe.matmul(bank[:, i * P:(i + 1) * P], CT[:, a, k, own], WKV[:, b, k, 1, :],
                                                 start=n == 0, stop=n == 3 * KC - 1)
                    last.then_inc(S["pj_done"], 1)

            def scores(g, t):
                pe.wait_ge(S["pj_lo"], n_of(g, t, 6, 5))
                for jp in range(2):
                    for b in range(BB):
                        for n, (qa, ka) in enumerate(PASSES):
                            last = pe.matmul(sc[jp][:, b * SEQ:(b + 1) * SEQ], QT[:, qa, b, 2 * jp:2 * jp + 2, :],
                                             KT[:, ka, b, :], start=n == 0, stop=n == 2)
                    last.then_inc(S["sc_done"], 1)

            def transpose_probs(g, t):
                pe.wait_ge(S["p_done"], n_of(g, t, 2, 2))
                for i in range(BT):
                    for jp in range(2):
                        at = (i % 2) * 256 + jp * P
                        last = pe.transpose(tv[i // 2][:, at:at + P],
                                            E[:, jp, 2 * i:2 * i + 2, :], ident[:, :])
                    if i % 2:
                        last.then_inc(S["tp_done"], 1)

            def weigh_values(g, t):
                pe.wait_ge(S["pj_lo"], n_of(g, t, 6, 6))
                for i in range(BT):
                    if i < 2:
                        pe.wait_ge(S["tp_lo"], n_of(g, t, 2, 2))
                    else:
                        pe.wait_ge(S["ot_lo"], n_of(g, t, 4, i - 1))
                    for h in range(2):
                        for n, (a, b) in enumerate(PASSES):
                            last = pe.matmul(tv[i % 2][:, h * 256:(h + 1) * 256], V[:, a, i, h, :], PT[:, b, i, :],
                                             start=n == 0, stop=n == 2)
                    last.then_inc(S["pv_done"], 1)

            def project_out(g, t):
                pe.wait_ge(S["o_lo"], g + 1)
                for i in range(BT):
                    pe.wait_ge(S["ot_lo"], n_of(g, t, 4, i + 1))
                    if i >= 2:
                        pe.wait_ge(S["x_acc"], n_of(g, t, 4, i - 1))
                    for n, (j, (a, b)) in enumerate([(j, ab) for j in range(REP) for ab in PASSES]):
                        last = pe.matmul(xp[i % 2][:, :], OT[:, a, j, i * P:(i + 1) * P], WO[:, b, j, :],
                                         start=n == 0, stop=n == 3 * REP - 1)
                    last.then_inc(S["xp_done"], 1)

            def transpose_weights(g, n, lo, hi):
                pe.wait_ge(S["wqs_done"], g * 3 + (n + 1))
                for u in range(lo // 4, hi // 4):
                    pe.wait_ge(S["x_acc"], n_of(g, PREP[n][0], 4, 3 + u - lo // 4))
                    for i in range(4):
                        slot = i if u < 2 else (i % 2) * 2 + i // 2
                        last = pe.transpose(xp[u - lo // 4][:, slot * P:(slot + 1) * P], VW[:, 4 * u + i - lo, :], ident[:, :])
                    last.then_inc(S["wt_done"], 1)

            def group(g, last):
                for t in range(SPG):
                    nxt = (g, t + 1) if t < SPG - 1 else (g + 1, 0)
                    more = not (last and t == SPG - 1)
                    scores(g, t)
                    if more:
                        project(*nxt, range(4))
                    transpose_probs(g, t)
                    if more:
                        project(*nxt, (4,))
                    weigh_values(g, t)
                    if more:
                        project(*nxt, (5,))
                    project_out(g, t)
                    if not last:
                        for n, (at, lo, hi) in enumerate(PREP):
                            if at == t:
                                transpose_weights(g, n, lo, hi)

            pe.sem_inc(S["xp_done"], 1)
            pe.wait_ge(S["zeroed"], 1)
            project(0, 0, range(6))
            with pe.Fori(0, GROUPS - 1) as g:
                group(g, False)
            group(GROUPS - 1, True)

        def q_bank(u):
            return pj[u % 2][:, :].rearrange("p (b t) -> p b t", b=BB)

        def v_bank(h):
            return pj[1][h * 64:(h + 1) * 64, :].rearrange("p (i d) -> p i d", i=BT)

        def o_bank(i):
            return tv[i % 2][:, :].rearrange("p (b j t) -> p b j t", b=2, j=REP)

        def o_out(part, i):
            return OT[:, part, :, i * P:(i + 1) * P].rearrange("p j (b t) -> p b j t", b=2)

        def w_bank(u, lo):
            return xp[u - lo // 4][:, :].rearrange("p (c n) -> p c n", c=4 if u < 2 else 2)

        def w_out(part, u):
            return WS0[:, part, :, u * P:(u + 1) * P] if u < 2 else WS1[:, part, :, (u - 2) * 256:(u - 1) * 256]

        @block.scalar
        def _(act):
            def weights_times_rec(g, n, lo, hi):
                act.wait_ge(S["wstep"], g * SCALE_STEPS + SCALE_STEPS)
                for c in range(lo, hi):
                    last = act.activation(VW[:, c - lo, :], WB[:, c, :], ACT.Copy, scale=wh[:, c:c + 1])
                last.then_inc(S["ww_done"], 1)

            def high_weights(g, n, lo, hi):
                for u in range(lo // 4, hi // 4):
                    act.wait_ge(S["wt_done"], g * 4 + (u + 1))
                    act.activation(w_out(0, u), w_bank(u, lo), ACT.Copy, scale=WEIGHT_SCALE).then_inc(S["wt_hi"], 1)

            def high(g, t, units):
                for u in units:
                    act.wait_ge(S["pj_done"], n_of(g, t, 6, u + 1))
                    if u < 4:
                        act.activation(QT[:, 0, :, u, :], q_bank(u), ACT.Copy, scale=UNSCALE).then_inc(S["pj_hi"], 1)
                    elif u == 4:
                        act.activation(KT[:, 0, :, :], q_bank(u), ACT.Copy, scale=UNSCALE).then_inc(S["pj_hi"], 1)
                    else:
                        act.activation(V[0:64, 0, :, 0, :], v_bank(0), ACT.Copy, scale=UNSCALE)
                        act.activation(V[64:128, 0, :, 1, :], v_bank(1), ACT.Copy, scale=UNSCALE).then_inc(S["pj_hi"], 1)

            def split_qkv(g):
                act.wait_ge(S["sq_ld"], g * 16 + 16)
                act.activation(WQ[:, 0, :, :], SQ[:, :, :], ACT.Copy, scale=WEIGHT_SCALE).then_inc(S["qkv_hi"], 1)
                act.wait_ge(S["skv_ld"], g * 32 + 32)
                act.activation(WKV[:, 0, :, :, :], SKV[:, :, :, :], ACT.Copy, scale=WEIGHT_SCALE).then_inc(S["qkv_hi"], 1)

            def group(g, last):
                for t in range(SPG):
                    nxt = (g, t + 1) if t < SPG - 1 else (g + 1, 0)
                    more = not (last and t == SPG - 1)
                    for jp in range(2):
                        act.wait_ge(S["sub_done"], n_of(g, t, 2, jp + 1))
                        act.activation(E[:, jp, :, :], E[:, jp, :, :], ACT.Exp, scale=exp_scale).then_inc(S["exp_done"], 1)
                    prep = [] if last else [(n, lo, hi) for n, (at, lo, hi) in enumerate(PREP) if at == t]
                    if more:
                        high(*nxt, range(2))
                    for p in prep:
                        weights_times_rec(g, *p)
                    if more:
                        high(*nxt, range(2, 4))
                    for i in range(2):
                        act.wait_ge(S["tp_done"], n_of(g, t, 2, i + 1))
                        act.activation(PT[:, 0, 2 * i:2 * i + 2, :], tv[i][:, :].rearrange("p (i n) -> p i n", i=2),
                                       ACT.Copy).then_inc(S["tp_hi"], 1)
                    if t == 0:
                        act.wait_ge(S["so_ld"], g * 16 + 16)
                        act.wait_ge(S["xp_done"], g * (SPG * 4) + 1)
                        act.activation(WO[:, 0, :, :], SO[:, :, :], ACT.Copy, scale=WEIGHT_SCALE).then_inc(S["o_hi"], 1)
                    if more:
                        high(*nxt, (4,))
                    for i in range(BT):
                        act.wait_ge(S["pv_done"], n_of(g, t, 4, i + 1))
                        act.activation(o_out(0, i), o_bank(i), ACT.Copy).then_inc(S["ot_hi"], 1)
                    if more:
                        high(*nxt, (5,))
                    for p in prep:
                        high_weights(g, *p)
                    if t == SPG - 2 and not last:
                        split_qkv(g + 1)

            split_qkv(0)
            high(0, 0, range(5))
            act.wait_ge(S["zeroed"], 1)
            high(0, 0, (5,))
            with act.Fori(0, GROUPS - 1) as g:
                group(g, False)
            group(GROUPS - 1, True)

        @block.vector
        def _(dve):
            def low(g, t, u):
                dve.wait_ge(S["pj_hi"], n_of(g, t, 6, u + 1))
                if u < 5:
                    to = (QT[:, 1, :, u, :], QT[:, 0, :, u, :]) if u < 4 else (KT[:, 1, :, :], KT[:, 0, :, :])
                    dve.scalar_tensor_tensor(out=to[0], in0=q_bank(u), scalar=UNSCALE, in1=to[1],
                                             op0=ALU.mult, op1=ALU.subtract).then_inc(S["pj_lo"], 1)
                else:
                    for h in range(2):
                        rows = slice(h * 64, (h + 1) * 64)
                        last = dve.scalar_tensor_tensor(out=V[rows, 1, :, h, :], in0=v_bank(h), scalar=UNSCALE,
                                                        in1=V[rows, 0, :, h, :], op0=ALU.mult, op1=ALU.subtract)
                    last.then_inc(S["pj_lo"], 1)

            def scale_weights(g):
                dve.wait_ge(S["wb_ld"], g * 32 + 32)
                dve.tensor_reduce(wa[:, :], WB[:, :, :], AX.X, ALU.max, apply_absolute_value=True).then_inc(S["wa_done"], 1)
                dve.wait_ge(S["wa_done"], g + 1)
                quant_scales(dve, wa[:, :], ws[:, :], wh[:, :], wl[:, :], wtmp, S["wstep"], g * SCALE_STEPS)

            def weights_to_grid(g, n, lo, hi):
                to_grid(dve, VW[:, 0:hi - lo, :], MW[:, 0:hi - lo, :], WB[:, lo:hi, :], lambda c: wl[:, lo + c:lo + c + 1],
                        hi - lo, [S[x] for x in ("ww_done", "wv_done", "wbits", "wm_done", "wsum")], g * 3 + (n + 1))

            def low_weights(g, n, lo, hi):
                for u in range(lo // 4, hi // 4):
                    dve.wait_ge(S["wt_hi"], g * 4 + (u + 1))
                    dve.scalar_tensor_tensor(out=w_out(1, u), in0=w_bank(u, lo), scalar=WEIGHT_SCALE, in1=w_out(0, u),
                                             op0=ALU.mult, op1=ALU.subtract).then_inc(S["wt_lo"], 1)

            def split_qkv(g):
                dve.wait_ge(S["qkv_hi"], g * 2 + 1)
                dve.scalar_tensor_tensor(out=WQ[:, 1, :, :], in0=SQ[:, :, :], scalar=WEIGHT_SCALE, in1=WQ[:, 0, :, :],
                                         op0=ALU.mult, op1=ALU.subtract).then_inc(S["qkv_lo"], 1)
                dve.wait_ge(S["qkv_hi"], g * 2 + 2)
                dve.scalar_tensor_tensor(out=WKV[:, 1, :, :, :], in0=SKV[:, :, :, :], scalar=WEIGHT_SCALE, in1=WKV[:, 0, :, :, :],
                                         op0=ALU.mult, op1=ALU.subtract).then_inc(S["qkv_lo"], 1)

            def scores_less_max(g, t, jp):
                s3 = sc[jp][:, :].rearrange("p (b k) -> p b k", b=BB)
                dve.wait_ge(S["sc_done"], n_of(g, t, 2, jp + 1))
                dve.reduce_max(ST[:, 0, jp, :], s3, AX.X).then_inc(S["max_done"], 1)
                dve.wait_ge(S["max_done"], n_of(g, t, 2, jp + 1))
                dve.tensor_tensor(E[:, jp, :, :], s3, ST[:, 0, jp, :].unsqueeze(2).to_broadcast([P, BB, SEQ]),
                                  ALU.subtract).then_inc(S["sub_done"], 1)

            def normalise(g, t, jp):
                at = n_of(g, t, 2, jp + 1)
                dve.wait_ge(S["exp_done"], at)
                dve.reduce_sum(ST[:, 1, jp, :], E[:, jp, :, :], AX.X).then_inc(S["sum_done"], 1)
                dve.wait_ge(S["sum_done"], at)
                dve.reciprocal(ST[:, 2, jp, :], ST[:, 1, jp, :]).then_inc(S["rcp_done"], 1)
                dve.wait_ge(S["rcp_done"], at)
                dve.tensor_tensor(E[:, jp, :, :], E[:, jp, :, :], ST[:, 2, jp, :].unsqueeze(2).to_broadcast([P, BB, SEQ]),
                                  ALU.mult).then_inc(S["p_done"], 1)

            def group(g, last):
                for t in range(SPG):
                    nxt = (g, t + 1) if t < SPG - 1 else (g + 1, 0)
                    more = not (last and t == SPG - 1)
                    scores_less_max(g, t, 0)
                    scores_less_max(g, t, 1)
                    if more:
                        low(*nxt, 0)
                    normalise(g, t, 0)
                    if more:
                        low(*nxt, 1)
                    normalise(g, t, 1)
                    if more:
                        low(*nxt, 2)
                        low(*nxt, 3)
                    for i in range(2):
                        dve.wait_ge(S["tp_hi"], n_of(g, t, 2, i + 1))
                        dve.tensor_tensor(PT[:, 1, 2 * i:2 * i + 2, :], tv[i][:, :].rearrange("p (i n) -> p i n", i=2),
                                          PT[:, 0, 2 * i:2 * i + 2, :], ALU.subtract).then_inc(S["tp_lo"], 1)
                    if t == 0:
                        dve.wait_ge(S["o_hi"], g + 1)
                        dve.scalar_tensor_tensor(out=WO[:, 1, :, :], in0=SO[:, :, :], scalar=WEIGHT_SCALE, in1=WO[:, 0, :, :],
                                                 op0=ALU.mult, op1=ALU.subtract).then_inc(S["o_lo"], 1)
                    if more:
                        low(*nxt, 4)
                    for i in range(BT):
                        dve.wait_ge(S["ot_hi"], n_of(g, t, 4, i + 1))
                        dve.tensor_tensor(o_out(1, i), o_bank(i), o_out(0, i), ALU.subtract).then_inc(S["ot_lo"], 1)
                    if more:
                        low(*nxt, 5)
                    prep = [] if last else [(n, lo, hi) for n, (at, lo, hi) in enumerate(PREP) if at == t]
                    for p in prep:
                        weights_to_grid(g, *p)
                    for i in range(BT):
                        if t == 0 and i == 2 and not last:
                            scale_weights(g)
                        dve.wait_ge(S["xp_done"], n_of(g, t, 4, i + 2))
                        xt = X[:, t * BT + i, :]
                        dve.scalar_tensor_tensor(out=xt, in0=xp[i % 2][:, :], scalar=UNSCALE, in1=xt,
                                                 op0=ALU.mult, op1=ALU.add).then_inc(S["x_acc"], 1)
                    for p in prep:
                        low_weights(g, *p)
                    if t == SPG - 2 and not last:
                        split_qkv(g + 1)

            split_qkv(0)
            for u in range(6):
                low(0, 0, u)
            with dve.Fori(0, GROUPS - 1) as g:
                group(g, False)
            group(GROUPS - 1, True)


def ffn0(nc, sb, pb, sem, X, ident, rstd, nmr, ln, w0t_dram, w1t_dram, b0, b1):
    with ExitStack() as ph:
        W0T = sb(ph, "W0T", [P, 2, KC, INNER], F16)
        W1T = sb(ph, "W1T", [P, 2, IC, DIM], F16)
        B0 = sb(ph, "B0", [P, INNER], BF16)
        B1 = sb(ph, "B1", [P, DIM], BF16)
        XB = sb(ph, "XB", [P, TILES, KC, P], BF16)
        xa = sb(ph, "xamax", [P, TILES, KC], F32)
        xs, xh, xl = (sb(ph, "x" + n, [P, TILES, KC], F32) for n in ("scale", "rec_hi", "rec_lo"))
        xtmp = sb(ph, "xtmp", [P, 5, TILES, KC], F32)
        VX = sb(ph, "VX", [P, KC, P], F32)
        MX = sb(ph, "MX", [P, KC, P], F32)
        QX = sb(ph, "QX", [P, KC, P], F32)
        XD = sb(ph, "XD", [P, 2, 2, KC, P], F16)
        DP = sb(ph, "DP", [P, INNER], F32)
        DB = sb(ph, "DB", [P, 2, IC, P], BF16)
        da = sb(ph, "damax", [P, IC], F32)
        ds_, dh, dl = (sb(ph, "d" + n, [P, 2, IC], F32) for n in ("scale", "rec_hi", "rec_lo"))
        dtmp = sb(ph, "dtmp", [P, 5, IC], F32)
        VD = sb(ph, "VD", [P, IC, P], F32)
        MD = sb(ph, "MD", [P, IC, P], F32)
        QD = sb(ph, "QD", [P, 2, IC, P], F32)
        DT = sb(ph, "DT", [P, 2, IC, P], F16)
        EB = sb(ph, "EB", [P, 2, DIM], BF16)
        db = [pb(ph, f"db{i}") for i in range(4)]
        et = [pb(ph, f"et{i}") for i in range(2)]
        xt = pb(ph, "xt")
        eb = pb(ph, "eb")
        names = ("w0_ld w1_ld b_ld xb_done xa_done xstep xw_done xv_done xbits xm_done xsum xq_done xqs_done "
                 "xt_done xt_hi xt_lo d_done bias_done gelu_done da_done dstep dw_done dv_done dbits dm_done dsum "
                 "dq_done dqs_done et_done et_hi et_lo e_done eb_done x_done")
        S = {n: sem(ph, "f0_" + n) for n in names.split()}
        stats_vector, stats_scalar, stats_ready, parts_before = ln
        block = ph.enter_context(nc.Block())
        GROUP_OF = [(0, 4), (4, 8), (8, 12), (12, 14)]

        def n_of(p, r, per, c):
            return p * (2 * per) + (r * per + c)

        @block.sync
        def _(sp):
            sp.dma_start(W0T[:, :, :, :], w0t_dram.rearrange("p (s c n) -> p s c n", s=2, c=KC)).then_inc(S["w0_ld"], 16)
            sp.dma_start(B0[:, :], b0.partition_broadcast(P)).then_inc(S["b_ld"], 16)
            sp.dma_start(B1[:, :], b1.partition_broadcast(P)).then_inc(S["b_ld"], 16)
            sp.dma_start(W1T[:, :, :, :], w1t_dram.rearrange("p (s c n) -> p s c n", s=2, c=IC)).then_inc(S["w1_ld"], 16)

        @block.tensor
        def _(pe):
            def first_product(p, r):
                pe.wait_ge(S["xt_lo"], n_of(p, r, 1, 1))
                for q in range(4):
                    if not (isinstance(p, int) and p == 0 and r == 0):
                        pe.wait_ge(S["bias_done"], n_of(p, r, 4, q - 3))
                    for n, (k, (a, b)) in enumerate([(k, ab) for ab in PASSES for k in range(KC)]):
                        last = pe.matmul(db[q][:, 0:NQ], XD[:, r, a, k, :], W0T[:, b, k, q * NQ:(q + 1) * NQ],
                                         start=n == 0, stop=n == 3 * KC - 1)
                    last.then_inc(S["d_done"], 1)

            def transpose_x(p, r):
                pe.wait_ge(S["xqs_done"], n_of(p, r, 1, 1))
                for k in range(KC):
                    last = pe.transpose(xt[:, k * P:(k + 1) * P], QX[:, k, :], ident[:, :])
                last.then_inc(S["xt_done"], 1)

            def second_product(p, r):
                def transposes(n):
                    if n >= 2:
                        pe.wait_ge(S["et_lo"], n_of(p, r, 4, n - 1))
                    for c in range(*GROUP_OF[n]):
                        last = pe.transpose(et[n % 2][:, (c % 4) * P:(c % 4 + 1) * P], QD[:, r, c, :], ident[:, :])
                    last.then_inc(S["et_done"], 1)

                pe.wait_ge(S["dqs_done"], n_of(p, r, 1, 1))
                transposes(0)
                transposes(1)
                for n in range(4):
                    pe.wait_ge(S["et_lo"], n_of(p, r, 4, n + 1))
                    for c in range(*GROUP_OF[n]):
                        for a, b in PASSES:
                            last = pe.matmul(eb[:, :], DT[:, a, c, :], W1T[:, b, c, :],
                                             start=c == 0 and (a, b) == PASSES[0], stop=c == IC - 1 and (a, b) == PASSES[-1])
                    if n < 2:
                        transposes(n + 2)
                last.then_inc(S["e_done"], 1)

            transpose_x(0, 0)
            pe.wait_ge(S["w0_ld"], 16)
            for r in range(2):
                first_product(0, r)
                transpose_x(0, 1) if r == 0 else transpose_x(1, 0)
            pe.wait_ge(S["w1_ld"], 16)
            with pe.Fori(1, TILES // 2 - 1) as p:
                first_product(p, 0)
                transpose_x(p, 1)
                second_product(p - 1, 0)
                first_product(p, 1)
                transpose_x(p + 1, 0)
                second_product(p - 1, 1)
            p = TILES // 2 - 1
            first_product(p, 0)
            transpose_x(p, 1)
            second_product(p - 1, 0)
            first_product(p, 1)
            second_product(p - 1, 1)
            second_product(p, 0)
            second_product(p, 1)

        def et_bank(n):
            a, b = GROUP_OF[n]
            return et[n % 2][:, 0:(b - a) * P].rearrange("p (c t) -> p c t", c=b - a)

        @block.scalar
        def _(act):
            def x_times_rec(p, r, i):
                for k in range(KC):
                    last = act.activation(VX[:, k, :], XB[:, i, k, :], ACT.Copy, scale=xh[:, i, k:k + 1])
                last.then_inc(S["xw_done"], 1)

            def d_times_rec(p, r):
                act.wait_ge(S["dstep"], n_of(p, r, SCALE_STEPS, SCALE_STEPS))
                if not (isinstance(p, int) and p == 0 and r == 0):
                    act.wait_ge(S["dqs_done"], n_of(p, r, 1, 0))
                for c in range(IC):
                    last = act.activation(VD[:, c, :], DB[:, r, c, :], ACT.Copy, scale=dh[:, r, c:c + 1])
                last.then_inc(S["dw_done"], 1)

            def gelu(p, r):
                for q in range(4):
                    act.wait_ge(S["bias_done"], n_of(p, r, 4, q + 1))
                    last = act.activation(DB[:, r, :, :].rearrange("p c t -> p (c t)")[:, q * NQ:(q + 1) * NQ],
                                          DP[:, q * NQ:(q + 1) * NQ], ACT.Gelu)
                last.then_inc(S["gelu_done"], 1)

            def high_x(p, r):
                act.wait_ge(S["xt_done"], n_of(p, r, 1, 1))
                act.activation(XD[:, r, 0, :, :], xt[:, :].rearrange("p (k t) -> p k t", k=KC), ACT.Copy).then_inc(S["xt_hi"], 1)

            def high_e(p, r):
                for n, (a, b) in enumerate(GROUP_OF):
                    act.wait_ge(S["et_done"], n_of(p, r, 4, n + 1))
                    act.activation(DT[:, 0, a:b, :], et_bank(n), ACT.Copy).then_inc(S["et_hi"], 1)

            def tile(p, r, quant_d, next_x, second):
                if next_x is not None:
                    act.wait_ge(S["xqs_done"], n_of(p, r, 1, 1))
                    x_times_rec(*next_x)
                if quant_d is not None:
                    d_times_rec(*quant_d)
                gelu(p, r)
                if next_x is not None:
                    high_x(*next_x[:2])
                if second is not None:
                    high_e(*second)

            stats_scalar(act, 1)
            act.wait_ge(S["xstep"], SCALE_STEPS)
            x_times_rec(0, 0, 0)
            high_x(0, 0)
            tile(0, 0, None, (0, 1, 1), None)
            tile(0, 1, (0, 0), (1, 0, 2), None)
            with act.Fori(1, TILES // 2 - 1) as p:
                tile(p, 0, (p - 1, 1), (p, 1, 2 * p + 1), (p - 1, 0))
                tile(p, 1, (p, 0), (p + 1, 0, 2 * p + 2), (p - 1, 1))
            p = TILES // 2 - 1
            tile(p, 0, (p - 1, 1), (p, 1, 2 * p + 1), (p - 1, 0))
            tile(p, 1, (p, 0), None, (p - 1, 1))
            d_times_rec(p, 1)
            high_e(p, 0)
            high_e(p, 1)

        @block.vector
        def _(dve):
            def quant_x(p, r, i):
                to_grid(dve, VX[:, :, :], MX[:, :, :], XB[:, i, :, :], lambda c: xl[:, i, c:c + 1], KC,
                        [S[n] for n in ("xw_done", "xv_done", "xbits", "xm_done", "xsum")], n_of(p, r, 1, 1))

            def scales_d(p, r):
                dve.wait_ge(S["gelu_done"], n_of(p, r, 1, 1))
                dve.tensor_reduce(da[:, :], DB[:, r, :, :], AX.X, ALU.max, apply_absolute_value=True).then_inc(S["da_done"], 1)
                dve.wait_ge(S["da_done"], n_of(p, r, 1, 1))
                quant_scales(dve, da[:, :], ds_[:, r, :], dh[:, r, :], dl[:, r, :], dtmp, S["dstep"], n_of(p, r, SCALE_STEPS, 0))

            def quant_d(p, r):
                to_grid(dve, VD[:, :, :], MD[:, :, :], DB[:, r, :, :], lambda c: dl[:, r, c:c + 1], IC,
                        [S[n] for n in ("dw_done", "dv_done", "dbits", "dm_done", "dsum")], n_of(p, r, 1, 1))

            def add_bias(p, r, qs):
                for q in qs:
                    dve.wait_ge(S["d_done"], n_of(p, r, 4, q + 1))
                    dve.scalar_tensor_tensor(out=DP[:, q * NQ:(q + 1) * NQ], in0=db[q][:, 0:NQ], scalar=UNSCALE,
                                             in1=B0[:, q * NQ:(q + 1) * NQ], op0=ALU.mult, op1=ALU.add).then_inc(S["bias_done"], 1)

            def low_x(p, r):
                dve.wait_ge(S["xt_hi"], n_of(p, r, 1, 1))
                dve.tensor_tensor(XD[:, r, 1, :, :], xt[:, :].rearrange("p (k t) -> p k t", k=KC), XD[:, r, 0, :, :],
                                  ALU.subtract).then_inc(S["xt_lo"], 1)

            def low_e(p, r):
                for n, (a, b) in enumerate(GROUP_OF):
                    dve.wait_ge(S["et_hi"], n_of(p, r, 4, n + 1))
                    dve.tensor_tensor(DT[:, 1, a:b, :], et_bank(n), DT[:, 0, a:b, :], ALU.subtract).then_inc(S["et_lo"], 1)
                dve.wait_ge(S["e_done"], n_of(p, r, 1, 1))
                dve.scalar_tensor_tensor(out=EB[:, r, :], in0=eb[:, :], scalar=UNSCALE, in1=B1[:, :],
                                         op0=ALU.mult, op1=ALU.add).then_inc(S["eb_done"], 1)

            def tile(p, r, hidden, next_x, second):
                if hidden is not None:
                    scales_d(*hidden)
                if next_x is not None:
                    quant_x(*next_x)
                add_bias(p, r, (0, 1))
                if hidden is not None:
                    quant_d(*hidden)
                add_bias(p, r, (2, 3))
                if next_x is not None:
                    low_x(*next_x[:2])
                if second is not None:
                    low_e(*second)

            stats_vector(dve, 1)
            dve.wait_ge(stats_ready, parts_before(1) + 1)
            for i in range(TILES):
                dve.tensor_scalar(XB[:, i, :, :].rearrange("p c t -> p (c t)"), X[:, i, :], rstd[:, i:i + 1], nmr[:, i:i + 1],
                                  ALU.mult, ALU.add).then_inc(S["xb_done"], 1)
            for i in range(TILES):
                dve.wait_ge(S["xb_done"], i + 1)
                last = dve.tensor_reduce(xa[:, i, :], XB[:, i, :, :], AX.X, ALU.max, apply_absolute_value=True)
            last.then_inc(S["xa_done"], 1)
            dve.wait_ge(S["xa_done"], 1)
            quant_scales(dve, xa[:, :, :], xs[:, :, :], xh[:, :, :], xl[:, :, :], xtmp, S["xstep"], 0)
            quant_x(0, 0, 0)
            low_x(0, 0)
            dve.wait_ge(S["b_ld"], 32)
            tile(0, 0, None, (0, 1, 1), None)
            tile(0, 1, (0, 0), (1, 0, 2), None)
            with dve.Fori(1, TILES // 2 - 1) as p:
                tile(p, 0, (p - 1, 1), (p, 1, 2 * p + 1), (p - 1, 0))
                tile(p, 1, (p, 0), (p + 1, 0, 2 * p + 2), (p - 1, 1))
            p = TILES // 2 - 1
            tile(p, 0, (p - 1, 1), (p, 1, 2 * p + 1), (p - 1, 0))
            tile(p, 1, (p, 0), None, (p - 1, 1))
            scales_d(p, 1)
            quant_d(p, 1)
            low_e(p, 0)
            low_e(p, 1)

        @block.gpsimd
        def _(pool):
            def dequant(V, M, Q, scale, chunks, S_, at):
                done, q_done, qs_done = S_
                pool.wait_ge(done, at)
                pool.tensor_tensor(V, V, M, ALU.subtract).then_inc(q_done, 1)
                pool.wait_ge(q_done, at)
                pool.tensor_tensor(Q, V, scale.unsqueeze(2).to_broadcast([P, chunks, P]), ALU.mult).then_inc(qs_done, 1)

            def quant_x(p, r, i):
                if not (isinstance(p, int) and p == 0 and r == 0):
                    pool.wait_ge(S["xt_done"], n_of(p, r, 1, 0))
                dequant(VX[:, :, :], MX[:, :, :], QX[:, :, :], xs[:, i, :], KC,
                        [S[n] for n in ("xsum", "xq_done", "xqs_done")], n_of(p, r, 1, 1))

            def quant_d(p, r):
                dequant(VD[:, :, :], MD[:, :, :], QD[:, r, :, :], ds_[:, r, :], IC,
                        [S[n] for n in ("dsum", "dq_done", "dqs_done")], n_of(p, r, 1, 1))

            def add_x(p, r, i):
                pool.wait_ge(S["eb_done"], n_of(p, r, 1, 1))
                pool.tensor_tensor(X[:, i, :], X[:, i, :], EB[:, r, :], ALU.add).then_inc(S["x_done"], 1)

            quant_x(0, 0, 0)
            quant_x(0, 1, 1)
            quant_x(1, 0, 2)
            quant_d(0, 0)
            with pool.Fori(1, TILES // 2 - 1) as p:
                quant_x(p, 1, 2 * p + 1)
                quant_d(p - 1, 1)
                add_x(p - 1, 0, 2 * p - 2)
                quant_x(p + 1, 0, 2 * p + 2)
                quant_d(p, 0)
                add_x(p - 1, 1, 2 * p - 1)
            p = TILES // 2 - 1
            quant_x(p, 1, 2 * p + 1)
            quant_d(p - 1, 1)
            add_x(p - 1, 0, 2 * p - 2)
            quant_d(p, 0)
            add_x(p - 1, 1, 2 * p - 1)
            quant_d(p, 1)
            add_x(p, 0, 2 * p)
            add_x(p, 1, 2 * p + 1)


def attention1(nc, sb, pb, sem, X, ident, CT, rstd, nmr, ln, wq, wk, wv, wo):
    exp_scale = float(HEAD1) ** -0.5
    HALF = TILES // 2
    with ExitStack() as ph:
        QT = sb(ph, "QT1", [P, 2, BATCH, REP, SEQ], F16)
        KT = sb(ph, "KT1", [P, 2, TOKENS], F16)
        V = sb(ph, "V1", [P, 2, TILES, P], F16)
        WQ = sb(ph, "WQ1", [P, 2, KC, REP, GROUPS, HEAD1], F16)
        WKV = sb(ph, "WKV1", [P, 2, KC, 2, P], F16)
        WO = sb(ph, "WO1", [P, 2, REP, DIM], F16)
        with ExitStack() as part:
            XT = sb(part, "XT1", [P, 2, KC, TOKENS], F16)
            SQ = sb(part, "SQ1", [P, KC, DIM], F32)
            SKV = sb(part, "SKV1", [P, KC, 2, P], F32)
            SO = sb(part, "SO1", [P, REP, DIM], F32)
            XN = sb(part, "XN1", [P, 2, DIM], F32)
            tp = [pb(part, f"n1_tp{i}") for i in range(2)]
            pj = [pb(part, f"n1_pj{i}") for i in range(2)]
            names = ("sq_ld skv_ld so_ld qkv_hi qkv_lo xn_done tp_done tp_hi tp_lo pj_done pj_hi pj_lo")
            S = {n: sem(part, "n1_" + n) for n in names.split()}
            stats_vector, stats_scalar, stats_ready, parts_before = ln
            block = part.enter_context(nc.Block())

            @block.sync
            def _(sp):
                sp.dma_start(SQ[:, :, :], wq.rearrange("(c p) n -> p c n", p=P)).then_inc(S["sq_ld"], 16)
                for i, w in enumerate((wk, wv)):
                    sp.dma_start(SKV[:, :, i, :], w.rearrange("(c p) n -> p c n", p=P)).then_inc(S["skv_ld"], 16)
                for g in range(GROUPS):
                    sp.dma_start(SO[g * HEAD1:(g + 1) * HEAD1, :, :],
                                 wo[g * REP * HEAD1:(g + 1) * REP * HEAD1, :].rearrange("(j d) n -> d j n", d=HEAD1)).then_inc(S["so_ld"], 16)

            @block.tensor
            def _(pe):
                def transposes(blk):
                    for i in range(BT):
                        pe.wait_ge(S["xn_done"], blk * BT + (i + 1))
                        if not (isinstance(blk, int) and blk == 0 and i < 2):
                            pe.wait_ge(S["tp_lo"], blk * BT + (i - 1))
                        for k in range(KC):
                            last = pe.transpose(tp[i % 2][:, k * P:(k + 1) * P], XN[:, i % 2, k * P:(k + 1) * P], ident[:, :])
                        last.then_inc(S["tp_done"], 1)

                def project(blk, units):
                    for u in units:
                        if not (isinstance(blk, int) and blk == 0 and u < 2):
                            pe.wait_ge(S["pj_lo"], blk * 6 + (u - 1))
                        if u == 0:
                            pe.wait_ge(S["tp_lo"], blk * BT + BT)
                        steps = [(k, ab) for ab in PASSES for k in range(KC)]
                        if u < 5:
                            for n, (k, (a, b)) in enumerate(steps):
                                if u < 4:
                                    w = WQ[:, a, k, u, :, :]
                                else:
                                    w = WKV[:, a, k, 0, :]
                                last = pe.matmul(pj[u % 2][:, :], w, (XT if u < 4 else CT)[:, b, k, bass.ds(blk * BLOCK, BLOCK)],
                                                 start=n == 0, stop=n == len(steps) - 1)
                        else:
                            for i in range(BT):
                                for n, (k, (a, b)) in enumerate(steps):
                                    last = pe.matmul(pj[1][:, i * P:(i + 1) * P], CT[:, a, k, bass.ds(blk * BLOCK + i * P, P)],
                                                     WKV[:, b, k, 1, :], start=n == 0, stop=n == len(steps) - 1)
                        last.then_inc(S["pj_done"], 1)

                transposes(0)
                pe.wait_ge(S["qkv_lo"], 3)
                project(0, range(4))
                transposes(1)
                project(0, (4, 5))
                with pe.Fori(1, BLOCKS - 1) as blk:
                    project(blk, range(4))
                    transposes(blk + 1)
                    project(blk, (4, 5))
                project(BLOCKS - 1, range(6))

            def q_columns(j):
                return SQ[:, :, :].rearrange("p k (g j d) -> p k j g d", g=GROUPS, j=REP)[:, :, j, :, :]

            def tp_bank(i):
                return tp[i % 2][:, :].rearrange("p (k t) -> p k t", k=KC)

            def x_out(part_, blk, i):
                return XT[:, part_, :, bass.ds(blk * BLOCK + i * P, P)]

            def pj_views(part_, blk, u):
                if u < 4:
                    return (QT[:, part_, bass.ds(blk * BB, BB), u, :], pj[u % 2][:, :].rearrange("p (b t) -> p b t", b=BB))
                if u == 4:
                    return KT[:, part_, bass.ds(blk * BLOCK, BLOCK)], pj[0][:, :]
                return V[:, part_, bass.ds(blk * BT, BT), :], pj[1][:, :].rearrange("p (i d) -> p i d", i=BT)

            @block.scalar
            def _(act):
                def high_x(blk):
                    for i in range(BT):
                        act.wait_ge(S["tp_done"], blk * BT + (i + 1))
                        act.activation(x_out(0, blk, i), tp_bank(i), ACT.Copy).then_inc(S["tp_hi"], 1)

                def high(blk, units):
                    for u in units:
                        act.wait_ge(S["pj_done"], blk * 6 + (u + 1))
                        to, bank = pj_views(0, blk, u)
                        act.activation(to, bank, ACT.Copy, scale=UNSCALE).then_inc(S["pj_hi"], 1)

                act.wait_ge(S["sq_ld"], 16)
                for j in range(REP):
                    last = act.activation(WQ[:, 0, :, j, :, :], q_columns(j), ACT.Copy, scale=WEIGHT_SCALE)
                last.then_inc(S["qkv_hi"], 1)
                act.wait_ge(S["skv_ld"], 32)
                act.activation(WKV[:, 0, :, :, :], SKV[:, :, :, :], ACT.Copy, scale=WEIGHT_SCALE).then_inc(S["qkv_hi"], 1)
                act.wait_ge(S["so_ld"], 16 * GROUPS)
                act.activation(WO[:, 0, :, :], SO[:, :, :], ACT.Copy, scale=WEIGHT_SCALE).then_inc(S["qkv_hi"], 1)
                stats_scalar(act, 2)
                high_x(0)
                with act.Fori(0, BLOCKS - 1) as blk:
                    high(blk, range(4))
                    high_x(blk + 1)
                    high(blk, (4, 5))
                high(BLOCKS - 1, range(6))

            @block.vector
            def _(dve):
                def norm(blk, i):
                    if not (isinstance(blk, int) and blk == 0 and i < 2):
                        dve.wait_ge(S["tp_done"], blk * BT + (i - 1))
                    t = blk * BT + i
                    dve.tensor_scalar(XN[:, i % 2, :], X[:, t, :], rstd[:, bass.ds(t, 1)], nmr[:, bass.ds(t, 1)],
                                      ALU.mult, ALU.add).then_inc(S["xn_done"], 1)

                def low_x(blk, i):
                    dve.wait_ge(S["tp_hi"], blk * BT + (i + 1))
                    dve.tensor_tensor(x_out(1, blk, i), tp_bank(i), x_out(0, blk, i), ALU.subtract).then_inc(S["tp_lo"], 1)

                def low(blk, units):
                    for u in units:
                        dve.wait_ge(S["pj_hi"], blk * 6 + (u + 1))
                        to, bank = pj_views(1, blk, u)
                        dve.scalar_tensor_tensor(out=to, in0=bank, scalar=UNSCALE, in1=pj_views(0, blk, u)[0],
                                                 op0=ALU.mult, op1=ALU.subtract).then_inc(S["pj_lo"], 1)

                def norm_block(blk):
                    norm(blk, 0)
                    norm(blk, 1)
                    for i in range(BT):
                        low_x(blk, i)
                        if i < 2:
                            norm(blk, i + 2)

                stats_vector(dve, 2)
                dve.wait_ge(stats_ready, parts_before(2) + 1)
                norm_block(0)
                dve.wait_ge(S["qkv_hi"], 1)
                for j in range(REP):
                    for k in range(KC):
                        last = dve.scalar_tensor_tensor(out=WQ[:, 1, k, j, :, :], in0=q_columns(j)[:, k, :, :], scalar=WEIGHT_SCALE,
                                                        in1=WQ[:, 0, k, j, :, :], op0=ALU.mult, op1=ALU.subtract)
                last.then_inc(S["qkv_lo"], 1)
                for n, (w, raw) in enumerate(((WKV, SKV), (WO, SO))):
                    dve.wait_ge(S["qkv_hi"], n + 2)
                    full = (slice(None),) * (len(raw.shape) - 1)
                    dve.scalar_tensor_tensor(out=w[(slice(None), 1) + full], in0=raw[(slice(None),) + full],
                                             scalar=WEIGHT_SCALE, in1=w[(slice(None), 0) + full],
                                             op0=ALU.mult, op1=ALU.subtract).then_inc(S["qkv_lo"], 1)
                with dve.Fori(0, BLOCKS - 1) as blk:
                    low(blk, range(4))
                    norm_block(blk + 1)
                    low(blk, (4, 5))
                low(BLOCKS - 1, range(6))

        with ExitStack() as part:
            mask = sb(part, "mask", [P, GROUPS], F16)
            KM = sb(part, "KM", [P, 2, 2, GROUPS, 2, SEQ], F16)
            VM = sb(part, "VM", [P, 2, 2, 2, 640], F16)
            E = sb(part, "E1", [P, 2, 4, GROUPS, SEQ], F32)
            ST = sb(part, "ST1", [P, 3, 4, GROUPS], F32)
            PT = sb(part, "PT1", [P, 2, 4, 2, 256], F16)
            OT = sb(part, "OT1", [P, 2, 2, REP, P], F16)
            sc = [pb(part, f"sc1_{i}") for i in range(4)]
            tp = [pb(part, f"a1_tp{i}") for i in range(2)]
            ob = pb(part, "ob1")
            xp = pb(part, "a1_xp")
            names = ("mask zeroed km_done vm_done sc_done max_done sub_done exp_done sum_done rcp_done p_done tp_done "
                     "tp_hi tp_lo ot_done ot_hi ot_lo xp_done x_acc")
            S = {n: sem(part, "a1_" + n) for n in names.split()}
            block = part.enter_context(nc.Block())

            def n_of(p, r, per, c):
                return p * (2 * per) + (r * per + c)

            def first(p, r):
                return isinstance(p, int) and p == 0 and r == 0

            @block.gpsimd
            def _(pool):
                pool.memset(mask[:, :], 1.0).then_inc(S["mask"], 1)
                pool.memset(VM[:, :, :, :, :], 0.0).then_inc(S["zeroed"], 1)
                for n, (step, base, cm) in enumerate(((-HEAD1, 0, 1), (HEAD1, HEAD1 - 1, -1))):
                    pool.wait_ge(S["mask"], n + 1)
                    pool.affine_select(out=mask[:, :], in_=mask[:, :], compare_op=ALU.is_ge, fill=0.0, base=base,
                                       pattern=[[step, GROUPS]], channel_multiplier=cm).then_inc(S["mask"], 1)

                def block_keys(p, r, t):
                    if not (isinstance(p, int) and p == 0):
                        pool.wait_ge(S["sc_done"], n_of(p - 1, r, 4, 4))
                    for s in range(2):
                        pool.tensor_tensor(KM[:, r, s, :, :, :].rearrange("p g b k -> p g (b k)"),
                                          KT[:, s, bass.ds(t * P, P)].unsqueeze(1).to_broadcast([P, GROUPS, P]),
                                          mask[:, :].unsqueeze(2).to_broadcast([P, GROUPS, P]), ALU.mult).then_inc(S["km_done"], 1)

                def normalise(p, r, us):
                    for u in us:
                        pool.wait_ge(S["rcp_done"], n_of(p, r, 4, u + 1))
                        e = E[:, r, u, :, :]
                        pool.tensor_tensor(e, e, ST[:, 2, u, :].unsqueeze(2).to_broadcast([P, GROUPS, SEQ]),
                                           ALU.mult).then_inc(S["p_done"], 1)

                pool.wait_ge(S["mask"], 3)
                block_keys(0, 0, 0)
                block_keys(0, 1, 1)
                for r in range(2):
                    normalise(0, r, range(4))
                    block_keys(1, r, 2 + r)
                with pool.Fori(1, HALF - 1) as p:
                    for r in range(2):
                        normalise(p, r, range(4))
                        block_keys(p + 1, r, 2 * p + 2 + r)
                for r in range(2):
                    normalise(HALF - 1, r, range(4))

            @block.tensor
            def _(pe):
                def scores(p, r, t, us):
                    for u in us:
                        b, jp = u // 2, u % 2
                        pe.wait_ge(S["km_done"], n_of(p, r, 2, 2))
                        if not first(p, r):
                            pe.wait_ge(S["sub_done"], n_of(p, r, 4, u - 3))
                        for n, (qa, ka) in enumerate(PASSES):
                            last = pe.matmul(sc[u][:, :], QT[:, qa, 2 * t + b, 2 * jp:2 * jp + 2, :], KM[:, r, ka, :, b, :],
                                             start=n == 0, stop=n == 2)
                        last.then_inc(S["sc_done"], 1)

                def transpose_probs(p, r, b):
                    pe.wait_ge(S["p_done"], n_of(p, r, 4, 2 * b + 2))
                    for h in range(2):
                        u = 2 * b + h
                        if u >= 2:
                            pe.wait_ge(S["tp_lo"], n_of(p, r, 4, u - 1))
                        for q in range(2):
                            for jp in range(2):
                                g = 4 * h + 2 * q
                                last = pe.transpose(tp[h][:, q * 256 + jp * P:q * 256 + (jp + 1) * P],
                                                    E[:, r, 2 * b + jp, g:g + 2, :], ident[:, :])
                        last.then_inc(S["tp_done"], 1)

                def weigh_values(p, r, b):
                    if b == 0:
                        pe.wait_ge(S["vm_done"], n_of(p, r, 1, 1))
                        if not first(p, r):
                            pe.wait_ge(S["ot_lo"], n_of(p, r, 1, 0))
                    n = 0
                    for h in range(2):
                        pe.wait_ge(S["tp_lo"], n_of(p, r, 4, 2 * b + h + 1))
                        for q in range(2):
                            gp = 2 * h + q
                            for va, pa in PASSES:
                                last = pe.matmul(ob[:, b * 256:(b + 1) * 256], VM[:, r, va, b, gp * P:(gp + 1) * P],
                                                 PT[:, pa, 2 * b + h, q, :], start=n == 0, stop=n == 11)
                                n += 1
                    if b == 1:
                        last.then_inc(S["ot_done"], 1)

                def project_out(p, r):
                    pe.wait_ge(S["ot_lo"], n_of(p, r, 1, 1))
                    if not first(p, r):
                        pe.wait_ge(S["x_acc"], n_of(p, r, 1, 0))
                    for n, (j, (a, b)) in enumerate([(j, ab) for j in range(REP) for ab in PASSES]):
                        last = pe.matmul(xp[:, :], OT[:, r, a, j, :], WO[:, b, j, :], start=n == 0, stop=n == 3 * REP - 1)
                    last.then_inc(S["xp_done"], 1)

                def tile(cur, old, out):
                    if old:
                        transpose_probs(*old, 0)
                    if cur:
                        scores(*cur, (0, 1))
                    if old:
                        transpose_probs(*old, 1)
                        weigh_values(*old, 0)
                    if cur:
                        scores(*cur, (2, 3))
                    if old:
                        weigh_values(*old, 1)
                    if out:
                        project_out(*out)

                tile((0, 0, 0), None, None)
                tile((0, 1, 1), (0, 0), None)
                with pe.Fori(1, HALF) as p:
                    tile((p, 0, 2 * p), (p - 1, 1), (p - 1, 0))
                    tile((p, 1, 2 * p + 1), (p, 0), (p - 1, 1))
                tile(None, (HALF - 1, 1), (HALF - 1, 0))
                project_out(HALF - 1, 1)

            def t_bank(u):
                return tp[u % 2][:, :].rearrange("p (q n) -> p q n", q=2)

            def o_bank():
                return ob[:, :].rearrange("p (b j t) -> p b j t", b=2, j=REP)

            def o_out(r, part_):
                return OT[:, r, part_, :, :].rearrange("p j (b t) -> p b j t", b=2)

            @block.scalar
            def _(act):
                def place_values(p, r, t):
                    if not (isinstance(p, int) and p == 0):
                        act.wait_ge(S["ot_done"], n_of(p - 1, r, 1, 1))
                    for b in range(2):
                        for h in range(2):
                            src = V[b * 64:(b + 1) * 64, :, t, :].rearrange("p s (q h d) -> p s q h d", q=4, h=2)[:, :, :, h, :]
                            to = VM[h * 64:(h + 1) * 64, r, :, b, :].rearrange("p s (q c) -> p s q c", q=4)[:, :, :, h * HEAD1:(h + 1) * HEAD1]
                            last = act.activation(to, src, ACT.Copy)
                    last.then_inc(S["vm_done"], 1)

                def exp(p, r, u):
                    act.wait_ge(S["sub_done"], n_of(p, r, 4, u + 1))
                    act.activation(E[:, r, u, :, :], E[:, r, u, :, :], ACT.Exp, scale=exp_scale).then_inc(S["exp_done"], 1)

                def high(p, r, u):
                    act.wait_ge(S["tp_done"], n_of(p, r, 4, u + 1))
                    act.activation(PT[:, 0, u, :, :], t_bank(u), ACT.Copy).then_inc(S["tp_hi"], 1)

                def tile(cur, old, place=None):
                    if old:
                        for u in range(4):
                            high(*old, u)
                    if cur:
                        exp(*cur, 0)
                        exp(*cur, 1)
                    if old:
                        act.wait_ge(S["ot_done"], n_of(*old, 1, 1))
                        act.activation(o_out(old[1], 0), o_bank(), ACT.Copy).then_inc(S["ot_hi"], 1)
                    if cur:
                        exp(*cur, 2)
                        exp(*cur, 3)
                    if place:
                        place_values(*place)

                act.wait_ge(S["zeroed"], 1)
                place_values(0, 0, 0)
                place_values(0, 1, 1)
                tile((0, 0), None)
                tile((0, 1), (0, 0))
                with act.Fori(1, HALF) as p:
                    tile((p, 0), (p - 1, 1), (p, 0, 2 * p))
                    tile((p, 1), (p, 0), (p, 1, 2 * p + 1))
                tile(None, (HALF - 1, 1))

            @block.vector
            def _(dve):
                def scores_less_max(p, r, us):
                    s3 = [sc[u][:, :].rearrange("p (g k) -> p g k", g=GROUPS) for u in range(4)]
                    for u in us:
                        dve.wait_ge(S["sc_done"], n_of(p, r, 4, u + 1))
                        dve.reduce_max(ST[:, 0, u, :], s3[u], AX.X).then_inc(S["max_done"], 1)
                    if not (isinstance(p, int) and p == 0):
                        dve.wait_ge(S["tp_done"], n_of(p - 1, r, 4, 4))
                    for u in us:
                        dve.wait_ge(S["max_done"], n_of(p, r, 4, u + 1))
                        dve.tensor_tensor(E[:, r, u, :, :], s3[u], ST[:, 0, u, :].unsqueeze(2).to_broadcast([P, GROUPS, SEQ]),
                                          ALU.subtract).then_inc(S["sub_done"], 1)

                def sums(p, r, us):
                    for u in us:
                        dve.wait_ge(S["exp_done"], n_of(p, r, 4, u + 1))
                        dve.reduce_sum(ST[:, 1, u, :], E[:, r, u, :, :], AX.X).then_inc(S["sum_done"], 1)
                    for u in us:
                        dve.wait_ge(S["sum_done"], n_of(p, r, 4, u + 1))
                        if not first(p, r):
                            dve.wait_ge(S["p_done"], n_of(p, r, 4, u - 3))
                        dve.reciprocal(ST[:, 2, u, :], ST[:, 1, u, :]).then_inc(S["rcp_done"], 1)

                def low(p, r, u):
                    dve.wait_ge(S["tp_hi"], n_of(p, r, 4, u + 1))
                    dve.tensor_tensor(PT[:, 1, u, :, :], t_bank(u), PT[:, 0, u, :, :], ALU.subtract).then_inc(S["tp_lo"], 1)

                def low_o(p, r):
                    dve.wait_ge(S["ot_hi"], n_of(p, r, 1, 1))
                    dve.tensor_tensor(o_out(r, 1), o_bank(), o_out(r, 0), ALU.subtract).then_inc(S["ot_lo"], 1)

                def add_x(p, r, t):
                    dve.wait_ge(S["xp_done"], n_of(p, r, 1, 1))
                    dve.scalar_tensor_tensor(out=X[:, t, :], in0=xp[:, :], scalar=UNSCALE, in1=X[:, t, :],
                                             op0=ALU.mult, op1=ALU.add).then_inc(S["x_acc"], 1)

                def tile(cur, old, out):
                    if old:
                        low(*old, 0)
                        low(*old, 1)
                    if cur:
                        scores_less_max(*cur, (0, 1))
                    if old:
                        low(*old, 2)
                        low(*old, 3)
                    if cur:
                        sums(*cur, (0, 1))
                        scores_less_max(*cur, (2, 3))
                    if old:
                        low_o(*old)
                    if out:
                        add_x(*out)
                    if cur:
                        sums(*cur, (2, 3))

                tile((0, 0), None, None)
                tile((0, 1), (0, 0), None)
                with dve.Fori(1, HALF) as p:
                    tile((p, 0), (p - 1, 1), (p - 1, 0, 2 * p - 2))
                    tile((p, 1), (p, 0), (p - 1, 1, 2 * p - 1))
                tile(None, (HALF - 1, 1), (HALF - 1, 0, TILES - 2))
                add_x(HALF - 1, 1, TILES - 1)


def ffn1(nc, sb, pb, sem, X, ident, rstd, nmr, ln, weight, bias, centroids, assignments, out):
    with ExitStack() as ph:
        SW = sb(ph, "SW", [P, 4, DIM], F32)
        SC = sb(ph, "SC", [CLUSTERS, DIM], F32)
        WT = sb(ph, "WT", [P, 2, KC, DIM], F16)
        CTT = sb(ph, "CTT", [P, 2, KC, CLUSTERS], F16)
        BI = sb(ph, "BI", [P, DIM], F32)
        AS = sb(ph, "AS", [CLUSTERS, DIM], I32)
        OH = sb(ph, "OH", [CLUSTERS, DIM], F16)
        cid = sb(ph, "cid", [CLUSTERS, 1], F32)
        cidi = sb(ph, "cidi", [CLUSTERS, 1], I32)
        ones = sb(ph, "ones", [P, P], F16)
        XN = sb(ph, "XN2", [P, 2, DIM], F32)
        XT = sb(ph, "XT2", [P, 2, 2, KC, P], F16)
        DN = sb(ph, "DN", [P, TILES, DIM], F32)
        EX = sb(ph, "EX", [P, 2, CLUSTERS], F32)
        cs = sb(ph, "cs", [P, 2, 4], F32)
        HT = sb(ph, "HT", [P, 2, CLUSTERS], F32)
        HA = sb(ph, "HA", [P, CLUSTERS], F16)
        QS = sb(ph, "QS", [P, TILES], F32)
        CSEL = sb(ph, "CSEL", [CLUSTERS, P], F16)
        RSEL = sb(ph, "RSEL", [P, DIM], F32)
        OM = sb(ph, "OM", [P, 2, DIM], F32)
        tp = [pb(ph, f"t2_{i}") for i in range(2)]
        dn = [pb(ph, f"dn{i}") for i in range(2)]
        lg = [pb(ph, f"lg{i}") for i in range(2)]
        rs = [pb(ph, f"rs{i}") for i in range(2)]
        names = ("w_ld c_ld b_ld a_ld ones_done cid_done oh_done ha_done xn_done tp_done tp_hi tp_lo dn_done lg_done dn_out "
                 "max_done nmax_done exp_done rcp_done hit_done any_done qs_done count_done csel_done row_done rsel_done om_done x_done stored")
        S = {n: sem(ph, "f1_" + n) for n in names.split()}
        stats_vector, stats_scalar, stats_ready, parts_before = ln
        block = ph.enter_context(nc.Block())
        HALF = TILES // 2
        FIRST = 5
        LOGIT = UNSCALE / TEMPERATURE

        def w_bank(u):
            if u < 4:
                return tp[u % 2][:, :].rearrange("p (k t) -> p k t", k=KC)
            return tp[0][:, 0:KC * CLUSTERS].rearrange("p (k t) -> p k t", k=KC)

        def w_out(part, u):
            return WT[:, part, :, u * P:(u + 1) * P] if u < 4 else CTT[:, part, :, :]

        def x_bank(r):
            return tp[(FIRST + r) % 2][:, :].rearrange("p (k t) -> p k t", k=KC)

        @block.sync
        def _(sp):
            sp.dma_start(SW[:, :, :], weight.rearrange("(t p) k -> p t k", p=P)).then_inc(S["w_ld"], 16)
            sp.dma_start(SC[:, :], centroids).then_inc(S["c_ld"], 16)
            sp.dma_start(BI[:, :], bias.partition_broadcast(P)).then_inc(S["b_ld"], 16)
            sp.dma_start(AS[:, :], assignments.partition_broadcast(CLUSTERS)).then_inc(S["a_ld"], 16)
            for i in range(TILES):
                sp.wait_ge(S["x_done"], i + 1)
                sp.dma_start(out[i * P:(i + 1) * P, :], X[:, i, :]).then_inc(S["stored"], 16)
            sp.wait_ge(S["stored"], 16 * TILES)

        @block.gpsimd
        def _(pool):
            pool.memset(ones[:, :], 1.0).then_inc(S["ones_done"], 1)
            pool.memset(HA[:, :], 0.0).then_inc(S["ones_done"], 1)
            pool.iota(cidi[:, :], pattern=[[0, 1]], base=0, channel_multiplier=1).then_inc(S["cid_done"], 1)
            pool.wait_ge(S["cid_done"], 1)
            pool.tensor_copy(cid[:, :], cidi[:, :]).then_inc(S["cid_done"], 1)
            for i in range(TILES):
                pool.wait_ge(S["om_done"], i + 1)
                pool.tensor_tensor(X[:, i, :], X[:, i, :], OM[:, i % 2, :], ALU.add).then_inc(S["x_done"], 1)

        @block.tensor
        def _(pe):
            pe.wait_ge(S["w_ld"], 16)
            for u in range(4):
                if u >= 2:
                    pe.wait_ge(S["tp_lo"], u - 1)
                for k in range(KC):
                    last = pe.transpose(tp[u % 2][:, k * P:(k + 1) * P], SW[:, u, k * P:(k + 1) * P], ident[:, :])
                last.then_inc(S["tp_done"], 1)
            pe.wait_ge(S["c_ld"], 16)
            pe.wait_ge(S["tp_lo"], 3)
            for k in range(KC):
                last = pe.transpose(tp[0][:, k * CLUSTERS:(k + 1) * CLUSTERS], SC[:, k * P:(k + 1) * P],
                                    ident[0:CLUSTERS, 0:CLUSTERS])
            last.then_inc(S["tp_done"], 1)

            def transposes(p, r):
                pe.wait_ge(S["xn_done"], p * 2 + (r + 1))
                pe.wait_ge(S["tp_lo"], p * 2 + (FIRST + r - 1))
                for k in range(KC):
                    last = pe.transpose(tp[(FIRST + r) % 2][:, k * P:(k + 1) * P], XN[:, r, k * P:(k + 1) * P], ident[:, :])
                last.then_inc(S["tp_done"], 1)

            def products(p, r):
                pe.wait_ge(S["tp_lo"], p * 2 + (FIRST + r + 1))
                if not (isinstance(p, int) and p == 0):
                    pe.wait_ge(S["dn_out"], p * 2 + (r - 1))
                    pe.wait_ge(S["exp_done"], p * 2 + (r - 1))
                for n, (k, (a, b)) in enumerate([(k, ab) for k in range(KC) for ab in PASSES]):
                    last = pe.matmul(lg[r][:, 0:CLUSTERS], XT[:, r, a, k, :], CTT[:, b, k, :], start=n == 0, stop=n == 3 * KC - 1)
                last.then_inc(S["lg_done"], 1)
                for n, (k, (a, b)) in enumerate([(k, ab) for k in range(KC) for ab in PASSES]):
                    last = pe.matmul(dn[r][:, :], XT[:, r, a, k, :], WT[:, b, k, :], start=n == 0, stop=n == 3 * KC - 1)
                last.then_inc(S["dn_done"], 1)

            transposes(0, 0)
            transposes(0, 1)
            products(0, 0)
            transposes(1, 0)
            products(0, 1)
            transposes(1, 1)
            products(1, 0)
            with pe.Fori(2, HALF) as p:
                transposes(p, 0)
                products(p - 1, 1)
                transposes(p, 1)
                products(p, 0)
            products(HALF - 1, 1)
            pe.wait_ge(S["any_done"], TILES)
            pe.matmul(rs[0][0:CLUSTERS, 0:P], HA[:, :], ones[:, :], start=True, stop=True).then_inc(S["count_done"], 1)
            pe.wait_ge(S["csel_done"], 1)
            pe.wait_ge(S["oh_done"], 1)
            pe.matmul(rs[1][:, :], CSEL[:, :], OH[:, :], start=True, stop=True).then_inc(S["row_done"], 1)

        @block.scalar
        def _(act):
            for u in range(FIRST):
                act.wait_ge(S["tp_done"], u + 1)
                act.activation(w_out(0, u), w_bank(u), ACT.Copy, scale=WEIGHT_SCALE).then_inc(S["tp_hi"], 1)
            stats_scalar(act, 3)

            def high(p, r):
                act.wait_ge(S["tp_done"], p * 2 + (FIRST + r + 1))
                act.activation(XT[:, r, 0, :, :], x_bank(r), ACT.Copy).then_inc(S["tp_hi"], 1)

            def exps(p, r):
                act.wait_ge(S["nmax_done"], p * 2 + (r + 1))
                act.activation(EX[:, r, :], lg[r][:, 0:CLUSTERS], ACT.Exp, bias=cs[:, r, 1:2], scale=LOGIT,
                               accum_out=cs[:, r, 2:3]).then_inc(S["exp_done"], 1)

            high(0, 0)
            high(0, 1)
            exps(0, 0)
            with act.Fori(1, HALF) as p:
                high(p, 0)
                exps(p - 1, 1)
                high(p, 1)
                exps(p, 0)
            exps(HALF - 1, 1)

        @block.vector
        def _(dve):
            for u in range(FIRST):
                dve.wait_ge(S["tp_hi"], u + 1)
                dve.scalar_tensor_tensor(out=w_out(1, u), in0=w_bank(u), scalar=WEIGHT_SCALE, in1=w_out(0, u),
                                         op0=ALU.mult, op1=ALU.subtract).then_inc(S["tp_lo"], 1)
            stats_vector(dve, 3)
            dve.wait_ge(stats_ready, parts_before(3) + 1)
            dve.wait_ge(S["ones_done"], 2)
            dve.wait_ge(S["b_ld"], 16)
            dve.wait_ge(S["a_ld"], 16)
            dve.wait_ge(S["cid_done"], 2)
            dve.tensor_scalar(OH[:, :], AS[:, :], cid[:, 0:1], None, ALU.is_equal).then_inc(S["oh_done"], 1)

            def norm(p, r):
                t = 2 * p + r
                if not (isinstance(p, int) and p == 0):
                    dve.wait_ge(S["tp_done"], p * 2 + (FIRST + r - 1))
                dve.tensor_scalar(XN[:, r, :], X[:, t, :], rstd[:, bass.ds(t, 1)], nmr[:, bass.ds(t, 1)],
                                  ALU.mult, ALU.add).then_inc(S["xn_done"], 1)

            def low(p, r):
                dve.wait_ge(S["tp_hi"], p * 2 + (FIRST + r + 1))
                dve.tensor_tensor(XT[:, r, 1, :, :], x_bank(r), XT[:, r, 0, :, :], ALU.subtract).then_inc(S["tp_lo"], 1)

            def maxima(p, r):
                at = p * 2 + (r + 1)
                dve.wait_ge(S["lg_done"], at)
                dve.reduce_max(cs[:, r, 0:1], lg[r][:, 0:CLUSTERS], AX.X).then_inc(S["max_done"], 1)
                dve.wait_ge(S["max_done"], at)
                dve.tensor_scalar(cs[:, r, 1:2], cs[:, r, 0:1], -LOGIT, None, ALU.mult).then_inc(S["nmax_done"], 1)

            def dense_out(p, r):
                dve.wait_ge(S["dn_done"], p * 2 + (r + 1))
                dve.scalar_tensor_tensor(out=DN[:, 2 * p + r, :], in0=dn[r][:, :], scalar=UNSCALE, in1=BI[:, :],
                                         op0=ALU.mult, op1=ALU.add).then_inc(S["dn_out"], 1)

            def hits(p, r):
                at = p * 2 + (r + 1)
                dve.wait_ge(S["exp_done"], at)
                dve.reciprocal(cs[:, r, 3:4], cs[:, r, 2:3]).then_inc(S["rcp_done"], 1)
                dve.wait_ge(S["rcp_done"], at)
                dve.tensor_scalar(HT[:, r, :], EX[:, r, :], cs[:, r, 3:4], THRESHOLD, ALU.mult, ALU.is_gt).then_inc(S["hit_done"], 1)
                dve.wait_ge(S["hit_done"], at)
                dve.reduce_max(QS[:, bass.ds(2 * p + r, 1)], HT[:, r, :], AX.X).then_inc(S["qs_done"], 1)
                dve.tensor_tensor(HA[:, :], HA[:, :], HT[:, r, :], ALU.max).then_inc(S["any_done"], 1)

            norm(0, 0)
            norm(0, 1)
            low(0, 0)
            low(0, 1)
            maxima(0, 0)
            with dve.Fori(1, HALF) as p:
                norm(p, 0)
                low(p, 0)
                maxima(p - 1, 1)
                hits(p - 1, 0)
                dense_out(p - 1, 0)
                norm(p, 1)
                low(p, 1)
                maxima(p, 0)
                hits(p - 1, 1)
                dense_out(p - 1, 1)
            p = HALF - 1
            maxima(p, 1)
            hits(p, 0)
            dense_out(p, 0)
            hits(p, 1)
            dense_out(p, 1)
            dve.wait_ge(S["count_done"], 1)
            dve.tensor_scalar(CSEL[:, :], rs[0][0:CLUSTERS, 0:P], 0.0, None, ALU.is_gt).then_inc(S["csel_done"], 1)
            dve.wait_ge(S["row_done"], 1)
            dve.tensor_scalar(RSEL[:, :], rs[1][:, :], 0.0, None, ALU.is_gt).then_inc(S["rsel_done"], 1)
            dve.wait_ge(S["rsel_done"], 1)
            dve.wait_ge(S["qs_done"], TILES)
            for i in range(TILES):
                if i >= 2:
                    dve.wait_ge(S["x_done"], i - 1)
                dve.scalar_tensor_tensor(out=OM[:, i % 2, :], in0=DN[:, i, :], scalar=QS[:, i:i + 1], in1=RSEL[:, :],
                                         op0=ALU.mult, op1=ALU.mult).then_inc(S["om_done"], 1)


_INS = ["x", "ctx_4096", "L0_xattn_wq", "L0_xattn_wk", "L0_xattn_wv", "L0_xattn_wo",
        "L0_ffn_W0", "L0_ffn_bias0", "L0_ffn_W1", "L0_ffn_bias1",
        "L1_xattn_Wq", "L1_xattn_Wk", "L1_xattn_Wv", "L1_xattn_Wo",
        "L1_ffn_weight", "L1_ffn_bias", "L1_ffn_centroids", "L1_ffn_assignments"]


def kernel(**inputs):
    import numpy as _np
    import concourse.bacc as _bacc
    from concourse import mybir as _mybir
    from concourse.bass_utils import run_bass_kernel_spmd as _run

    nc = _bacc.Bacc("TRN2", target_bir_lowering=False, num_devices=1)
    arrays, args = {}, []
    for name in _INS:
        a = _np.ascontiguousarray(inputs[name])
        if name in ("x", "ctx_4096"):
            a = a.reshape(TOKENS, DIM)
        arrays[f"in_{name}"] = a
        args.append(nc.dram_tensor(f"in_{name}", a.shape, _mybir.dt.from_np(a.dtype), kind="ExternalInput").ap())
    args.append(nc.dram_tensor("out_0", (TOKENS, DIM), _mybir.dt.float32, kind="ExternalOutput").ap())
    fused_decoder_kernel(nc, *args)
    r = _run(nc, [arrays], core_ids=[0])
    return r.results[0]["out_0"].reshape(BATCH, SEQ, DIM)
```

```python
import math

import concourse.bass as bass
from concourse import mybir
from contextlib import ExitStack

F32 = mybir.dt.float32
F16 = mybir.dt.float16
BF16 = mybir.dt.bfloat16
U32 = mybir.dt.uint32
I32 = mybir.dt.int32
ALU = mybir.AluOpType
ACT = mybir.ActivationFunctionType
AX = mybir.AxisListType

P = 128
BATCH, SEQ, DIM = 32, 64, 512
TOKENS = BATCH * SEQ
TILES = TOKENS // P
KC = DIM // P
BLOCK = 512
BLOCKS = TOKENS // BLOCK
BT = BLOCK // P
BB = BLOCK // SEQ
GROUPS, REP = 8, 4
HEAD0 = 128
HEAD1 = 16
INNER = 1792
IC = INNER // P
NQ = 448
CLUSTERS = 64
THRESHOLD, TEMPERATURE = 0.01, 0.1
EPS = 1e-5
FP8_MAX, AMAX_MIN = 448.0, 1e-4
WEIGHT_SCALE = 64.0
UNSCALE = 1.0 / WEIGHT_SCALE
PASSES = ((0, 0), (0, 1), (1, 0))


SCALE_STEPS = 16
SUBNORMAL = 1.5 * 2.0 ** -6
TO_GRID = 2.0 ** 20


def quant_scales(dve, amax, scale, rec_hi, rec_lo, tmp, step, base):
    u = lambda a: a.bitcast(U32)
    clamped, top, rest, rem, s_hi = (tmp[:, i] for i in range(5))
    stt = lambda o, a, c, b, op0, op1: dve.scalar_tensor_tensor(out=o, in0=a, scalar=c, in1=b, op0=op0, op1=op1)
    ops = (
        lambda: dve.tensor_scalar(clamped, amax, AMAX_MIN, None, ALU.max),
        lambda: dve.tensor_scalar(scale, clamped, 1.0 / FP8_MAX, None, ALU.mult),
        lambda: dve.tensor_scalar(u(top), u(scale), 0xFFFFF000, None, ALU.bitwise_and),
        lambda: dve.tensor_tensor(rest, scale, top, ALU.subtract),
        lambda: stt(rem, top, -FP8_MAX, clamped, ALU.mult, ALU.add),
        lambda: stt(rem, rest, -FP8_MAX, rem, ALU.mult, ALU.add),
        lambda: stt(scale, rem, 1.0 / FP8_MAX, scale, ALU.mult, ALU.add),
        lambda: dve.reciprocal(rest, scale),
        lambda: dve.tensor_scalar(u(rec_hi), u(rest), 0xFFFFFF00, None, ALU.bitwise_and),
        lambda: dve.tensor_scalar(u(s_hi), u(scale), 0xFFFF0000, None, ALU.bitwise_and),
        lambda: dve.tensor_tensor(top, s_hi, rec_hi, ALU.mult),
        lambda: dve.tensor_tensor(s_hi, scale, s_hi, ALU.subtract),
        lambda: dve.tensor_scalar(top, top, -1.0, 1.0, ALU.mult, ALU.add),
        lambda: dve.tensor_tensor(s_hi, s_hi, rec_hi, ALU.mult),
        lambda: dve.tensor_tensor(top, top, s_hi, ALU.subtract),
        lambda: dve.tensor_tensor(rec_lo, top, rest, ALU.mult),
    )
    assert len(ops) == SCALE_STEPS
    for n, op in enumerate(ops):
        if n:
            dve.wait_ge(step, base + n)
        op().then_inc(step, 1)


def round_to_grid(dve, V, M, sems, at):
    bits, m_done, done = sems
    dve.tensor_scalar(M.bitcast(U32), V.bitcast(U32), 0x7F800000, 0x00400000,
                      ALU.bitwise_and, ALU.bitwise_or).then_inc(bits, 1)
    dve.wait_ge(bits, at)
    dve.tensor_scalar(M, M, SUBNORMAL, TO_GRID, ALU.max, ALU.mult).then_inc(m_done, 1)
    dve.wait_ge(m_done, at)
    dve.tensor_tensor(V, V, M, ALU.add).then_inc(done, 1)


def to_grid(dve, V, M, src, rec_lo, chunks, sems, at):
    w_done, v_done = sems[:2]
    dve.wait_ge(w_done, at)
    for c in range(chunks):
        last = dve.scalar_tensor_tensor(out=V[:, c, :], in0=src[:, c, :], scalar=rec_lo(c), in1=V[:, c, :],
                                        op0=ALU.mult, op1=ALU.add)
    last.then_inc(v_done, 1)
    dve.wait_ge(v_done, at)
    round_to_grid(dve, V, M, sems[2:], at)


def fused_decoder_kernel(nc, x, ctx, wq0, wk0, wv0, wo0, w0, b0, w1, b1,
                         wq1, wk1, wv1, wo1, weight, bias, centroids, assignments, out):
    stack = ExitStack()
    with stack:
        def sb(where, name, shape, dt):
            return where.enter_context(nc.sbuf_tensor(name, shape, dt))

        def pb(where, name, shape=(P, 512)):
            return where.enter_context(nc.psum_tensor(name, list(shape), F32))

        def sem(where, name):
            return where.enter_context(nc.semaphore(name))

        X = sb(stack, "X", [P, TILES, DIM], F32)
        ident = sb(stack, "ident", [P, P], F32)
        CT = sb(stack, "CT", [P, 2, KC, TOKENS], F16)
        rstd = sb(stack, "rstd", [P, TILES], F32)
        nmr = sb(stack, "nmr", [P, TILES], F32)

        bn = sb(stack, "bn", [P, TILES, 6], F32)
        mv = sb(stack, "mv", [P, TILES, 2], F32)
        var_eps, root, guess, work = (sb(stack, n, [P, TILES], F32) for n in ("var_eps", "root", "guess", "ln_work"))
        stat, var_ready, root_ready, ln_step, stats_ready = (
            sem(stack, n) for n in ("stat", "var_ready", "root_ready", "ln_step", "stats_ready"))
        LN_STEPS = 6
        PARTS = {0: BLOCKS, 1: BLOCKS, 2: 1, 3: TILES // 2}

        def parts_before(use):
            return sum(PARTS[u] for u in range(use))

        def ln_part(use, part):
            per = TILES // PARTS[use]
            return per, bass.ds(part * per, per), part + parts_before(use)

        def ln_moments(dve, use, part):
            per, s, at = ln_part(use, part)
            for i in range(per):
                dve.bn_stats(bn[:, i, :], X[:, part * per + i, :]).then_inc(stat, 1)
            if not (isinstance(at, int) and at == 0):
                dve.wait_ge(stats_ready, at)
            for i in range(per):
                dve.wait_ge(stat, part * per + (use * TILES + i + 1))
                last = dve.bn_aggr(mv[:, i, :], bn[:, i, :])
            last.then_inc(ln_step, 1)
            dve.wait_ge(ln_step, at * LN_STEPS + 1)
            dve.tensor_scalar(var_eps[:, s], mv[:, 0:per, 1], EPS, None, ALU.add).then_inc(var_ready, 1)

        def ln_scales(dve, use, part):
            per, s, at = ln_part(use, part)
            dve.wait_ge(root_ready, at + 1)
            dve.reciprocal(guess[:, s], root[:, s]).then_inc(ln_step, 1)
            for n, op in enumerate((lambda: dve.tensor_tensor(work[:, s], guess[:, s], guess[:, s], ALU.mult),
                       lambda: dve.tensor_tensor(work[:, s], work[:, s], var_eps[:, s], ALU.mult),
                       lambda: dve.tensor_scalar(work[:, s], work[:, s], -0.5, 1.5, ALU.mult, ALU.add),
                       lambda: dve.tensor_tensor(rstd[:, s], work[:, s], guess[:, s], ALU.mult))):
                dve.wait_ge(ln_step, at * LN_STEPS + (n + 2))
                op().then_inc(ln_step, 1)
            dve.wait_ge(ln_step, at * LN_STEPS + LN_STEPS)
            dve.scalar_tensor_tensor(out=nmr[:, s], in0=mv[:, 0:per, 0], scalar=-1.0, in1=rstd[:, s],
                                     op0=ALU.mult, op1=ALU.mult).then_inc(stats_ready, 1)

        def ln_stats_vector(dve, use, parts, loaded=None):
            for part in parts:
                if loaded is not None:
                    dve.wait_ge(loaded[part], 16)
                ln_moments(dve, use, part)
                ln_scales(dve, use, part)

        def ln_stats_scalar(act, use, parts):
            for part in parts:
                per, s, at = ln_part(use, part)
                act.wait_ge(var_ready, at + 1)
                act.activation(root[:, s], var_eps[:, s], ACT.Sqrt).then_inc(root_ready, 1)

        ln = (ln_stats_vector, ln_stats_scalar, stats_ready, parts_before)

        ffn0_scope = stack.enter_context(ExitStack())
        W0T = sb(ffn0_scope, "W0T", [P, 2, KC, INNER], F16)
        XB = sb(ffn0_scope, "XB", [P, TILES, KC, P], BF16)
        xa = sb(ffn0_scope, "xamax", [P, TILES, KC], F32)
        xs, xh, xl = (sb(ffn0_scope, "x" + n, [P, TILES, KC], F32) for n in ("scale", "rec_hi", "rec_lo"))
        xtmp = sb(ffn0_scope, "xtmp", [P, 5, BT, KC], F32)
        xb_done, xa_done, xstep, w0_ld = (sem(stack, n) for n in ("xb_done", "xa_done", "xstep", "w0_ld"))

        def norm_x(dve, part):
            dve.wait_ge(stats_ready, parts_before(1) + part + 1)
            for i in range(part * BT, (part + 1) * BT):
                dve.tensor_scalar(XB[:, i, :, :].rearrange("p c t -> p (c t)"), X[:, i, :], rstd[:, i:i + 1], nmr[:, i:i + 1],
                                  ALU.mult, ALU.add).then_inc(xb_done, 1)

        def amax_x(dve, part):
            for i in range(part * BT, (part + 1) * BT):
                dve.wait_ge(xb_done, i + 1)
                last = dve.tensor_reduce(xa[:, i, :], XB[:, i, :, :], AX.X, ALU.max, apply_absolute_value=True)
            last.then_inc(xa_done, 1)

        def scales_x(dve, part):
            dve.wait_ge(xa_done, part + 1)
            s = slice(part * BT, (part + 1) * BT)
            quant_scales(dve, xa[:, s, :], xs[:, s, :], xh[:, s, :], xl[:, s, :], xtmp, xstep, part * SCALE_STEPS)

        x_pieces = (lambda dve, part: ln_moments(dve, 1, part), lambda dve, part: ln_scales(dve, 1, part), norm_x, amax_x, scales_x)
        ahead_of_ffn0 = (W0T, XB, w0_ld, x_pieces, lambda act, part: ln_stats_scalar(act, 1, (part,)))
        NQH = REP * HEAD0

        def bits16(buffer):
            return buffer[:, :, :, :].rearrange("p a b c -> p (a b c)")

        def piece(memory, at, shape, dt):
            size = math.prod(shape) * mybir.dt.size(dt) // 2
            names = "abcd"[:len(shape)]
            flat = memory[:, at:at + size].bitcast(dt)
            return flat.rearrange(f"p ({' '.join(names)}) -> p {' '.join(names)}", **dict(zip(names, shape))), at + size

        xt_scope = stack.enter_context(ExitStack())
        SQ, at = piece(bits16(W0T), 0, (KC, NQH), F32)
        SKV, at = piece(bits16(W0T), at, (KC, 2, HEAD0), F32)
        SO, at = piece(bits16(W0T), at, (REP, DIM), F32)
        WS1, at = piece(bits16(W0T), at, (2, 2, DIM), F16)
        WQ = sb(xt_scope, "WQ", [P, 2, KC, NQH], F16)
        WKV = sb(xt_scope, "WKV", [P, 2, KC, 2, HEAD0], F16)
        weights0 = (SQ, SKV, SO, WQ, WKV, WS1)
        weight_sems0 = {n: sem(stack, "a0_" + n) for n in "sq_ld skv_ld so_ld qkv_hi qkv_lo".split()}
        W = weight_sems0

        def load_qkv(sp, g):
            sp.dma_start(SQ[:, :, :], wq0[:, bass.ds(g * NQH, NQH)].rearrange("(c p) n -> p c n", p=P)).then_inc(W["sq_ld"], 16)
            for i, w in enumerate((wk0, wv0)):
                sp.dma_start(SKV[:, :, i, :], w[:, bass.ds(g * HEAD0, HEAD0)].rearrange("(c p) n -> p c n", p=P)).then_inc(W["skv_ld"], 16)

        def load_o(sp, g):
            sp.dma_start(SO[:, :, :], wo0[bass.ds(g * NQH, NQH), :].rearrange("(j p) n -> p j n", p=P)).then_inc(W["so_ld"], 16)

        def high_q(act, g):
            act.wait_ge(W["sq_ld"], g * 16 + 16)
            act.activation(WQ[:, 0, :, :], SQ[:, :, :], ACT.Copy, scale=WEIGHT_SCALE).then_inc(W["qkv_hi"], 1)

        def high_kv(act, g):
            act.wait_ge(W["skv_ld"], g * 32 + 32)
            act.activation(WKV[:, 0, :, :, :], SKV[:, :, :, :], ACT.Copy, scale=WEIGHT_SCALE).then_inc(W["qkv_hi"], 1)

        def low_q(dve, g):
            dve.wait_ge(W["qkv_hi"], g * 2 + 1)
            dve.scalar_tensor_tensor(out=WQ[:, 1, :, :], in0=SQ[:, :, :], scalar=WEIGHT_SCALE, in1=WQ[:, 0, :, :],
                                     op0=ALU.mult, op1=ALU.subtract).then_inc(W["qkv_lo"], 1)

        def low_kv(dve, g):
            dve.wait_ge(W["qkv_hi"], g * 2 + 2)
            dve.scalar_tensor_tensor(out=WKV[:, 1, :, :, :], in0=SKV[:, :, :, :], scalar=WEIGHT_SCALE, in1=WKV[:, 0, :, :, :],
                                     op0=ALU.mult, op1=ALU.subtract).then_inc(W["qkv_lo"], 1)

        XT = sb(xt_scope, "XT", [P, 2, KC, TOKENS], F16)
        w0t = nc.dram_tensor("w0t", [P, 2 * KC * INNER], F16, kind="Internal").ap()
        w1t = nc.dram_tensor("w1t", [P, 2 * IC * DIM], F16, kind="Internal").ap()
        with ExitStack() as ph:
            CS = sb(ph, "CS", [P, TILES, DIM], F32)
            XN = sb(ph, "XN", [P, 2, DIM], F32)
            tp = [pb(ph, f"p0_tp{i}") for i in range(4)]
            x_ld = [sem(ph, f"x_ld{i}") for i in range(BLOCKS)]
            c_ld = [sem(ph, f"c_ld{i}") for i in range(BLOCKS)]
            ident_ready = sem(ph, "ident_ready")
            xn_ready = sem(ph, "xn_ready")
            tp_done = sem(ph, "p0_tp_done")
            hi_done = sem(ph, "p0_hi_done")
            lo_done = sem(ph, "p0_lo_done")
            UNITS = [(x_too, i * BT + j) for i in range(BLOCKS) for x_too in range(2) for j in range(BT)]
            block = ph.enter_context(nc.Block())

            @block.sync
            def _(sp):
                for i in range(BLOCKS):
                    rows = slice(i * BLOCK, (i + 1) * BLOCK)
                    sp.dma_start(CS[:, i * BT:(i + 1) * BT, :],
                                 ctx[rows, :].rearrange("(t p) d -> p t d", p=P)).then_inc(c_ld[i], 16)
                    sp.dma_start(X[:, i * BT:(i + 1) * BT, :],
                                 x[rows, :].rearrange("(t p) d -> p t d", p=P)).then_inc(x_ld[i], 16)
                    if i == 1:
                        load_qkv(sp, 0)
                load_o(sp, 0)

            @block.gpsimd
            def _(pool):
                pool.memset(ident[:, :], 0.0).then_inc(ident_ready, 1)
                pool.wait_ge(ident_ready, 1)
                pool.affine_select(out=ident[:, :], in_=ident[:, :], compare_op=ALU.not_equal, fill=1.0,
                                   base=0, pattern=[[-1, P]], channel_multiplier=1).then_inc(ident_ready, 1)
                for i in range(TILES):
                    pool.wait_ge(stats_ready, i // BT + 1)
                    if i >= 2:
                        pool.wait_ge(tp_done, UNITS.index((1, i - 2)) + 1)
                    pool.tensor_scalar(XN[:, i % 2, :], X[:, i, :], rstd[:, i:i + 1], nmr[:, i:i + 1],
                                       ALU.mult, ALU.add).then_inc(xn_ready, 1)

            @block.tensor
            def _(pe):
                pe.wait_ge(ident_ready, 2)
                for n, (x_too, i) in enumerate(UNITS):
                    if not x_too:
                        if i % BT == 0:
                            pe.wait_ge(c_ld[i // BT], 16)
                        src = CS[:, i, :]
                    else:
                        pe.wait_ge(xn_ready, i + 1)
                        src = XN[:, i % 2, :]
                    if n >= 4:
                        pe.wait_ge(lo_done, n - 3)
                    for k in range(KC):
                        last = pe.transpose(tp[n % 4][:, k * P:(k + 1) * P], src[:, k * P:(k + 1) * P], ident[:, :])
                    last.then_inc(tp_done, 1)

            def dst(n, part):
                x_too, i = UNITS[n]
                return (CT, XT)[x_too][:, part, :, i * P:(i + 1) * P]

            def bank(n):
                return tp[n % 4][:, :].rearrange("p (k t) -> p k t", k=KC)

            @block.scalar
            def _(act):
                for n in range(2 * TILES):
                    if n % (2 * BT) == 0:
                        ln_stats_scalar(act, 0, (n // (2 * BT),))
                    act.wait_ge(tp_done, n + 1)
                    act.activation(dst(n, 0), bank(n), ACT.Copy).then_inc(hi_done, 1)
                high_q(act, 0)
                high_kv(act, 0)

            @block.vector
            def _(dve):
                for n in range(2 * TILES):
                    if n % (2 * BT) == 0:
                        ln_stats_vector(dve, 0, (n // (2 * BT),), x_ld)
                    dve.wait_ge(hi_done, n + 1)
                    dve.tensor_tensor(dst(n, 1), bank(n), dst(n, 0), ALU.subtract).then_inc(lo_done, 1)
                low_q(dve, 0)
                low_kv(dve, 0)

        attention0(nc, sb, pb, sem, X, ident, XT, CT, w0, w1, w0t, w1t, ahead_of_ffn0,
                   weights0, weight_sems0, (load_qkv, load_o), (high_q, high_kv, low_q, low_kv), piece, bits16)
        xt_scope.close()
        ffn0(nc, sb, pb, sem, X, ident, ahead_of_ffn0, (xs, xh, xl, xstep), w1t, b0, b1)
        ffn0_scope.close()
        attention1(nc, sb, pb, sem, X, ident, CT, rstd, nmr, ln, wq1, wk1, wv1, wo1)
        ffn1(nc, sb, pb, sem, X, ident, rstd, nmr, (ln_moments, ln_scales) + ln[1:], weight, bias, centroids, assignments, out)


def attention0(nc, sb, pb, sem, X, ident, XT, CT, w0, w1, w0t_dram, w1t_dram, ahead_of_ffn0,
               weights, weight_sems, loads, splits, piece, bits16):
    exp_scale = float(HEAD0) ** -0.5
    with ExitStack() as ph:
        W0T, XB, w0_ld, x_pieces, stats_x = ahead_of_ffn0
        SQ, SKV, SO, WQ, WKV, WS1 = weights
        load_qkv, load_o = loads
        high_q, high_kv, low_q, low_kv = splits
        WO = sb(ph, "WO", [P, 2, REP, DIM], F16)
        QT = sb(ph, "QT", [P, 2, BB, REP, SEQ], F16)
        KT = sb(ph, "KT", [P, 2, BB, SEQ], F16)
        V = sb(ph, "V", [P, 2, BT, 2, HEAD0], F16)
        E = sb(ph, "E", [P, 2, BB, SEQ], F32)
        ST = sb(ph, "ST", [P, 3, 2, BB], F32)
        PT = sb(ph, "PT", [P, 2, BT, REP * SEQ], F16)
        OT = sb(ph, "OT", [P, 2, REP, BLOCK], F16)
        words = bits16(XB)
        WB, at = piece(words, 0, (16, P), BF16)
        VW = sb(ph, "VW", [P, 2, 8, P], F32)
        MW, at = piece(words, at, (8, P), F32)
        WS0, at = piece(words, at, (2, KC, 2 * P), F16)
        wa, ws, wh, wl = (sb(ph, "w" + n, [P, 16], F32) for n in ("amax", "scale", "rec_hi", "rec_lo"))
        wtmp = sb(ph, "wtmp", [P, 5, 16], F32)
        sc = [pb(ph, f"sc{i}") for i in range(2)]
        pj = [pb(ph, f"pj{i}") for i in range(2)]
        tv = [pb(ph, f"tv{i}") for i in range(2)]
        xp = [pb(ph, f"xp{i}") for i in range(2)]
        names = ("zeroed o_hi o_lo sc_done pj_done tp_done pv_done xp_done "
                 "exp_done pj_hi tp_hi ot_hi max_done sub_done sum_done rcp_done p_done pj_lo tp_lo ot_lo x_acc "
                 "wb_ld wa_done wstep ww_done wv_done wbits wm_done wsum wqs_done wq_done wt_done wt_hi wt_lo w_st")
        S = {n: sem(ph, "a0_" + n) for n in names.split()} | weight_sems
        block = ph.enter_context(nc.Block())
        SPG = BLOCKS
        PREP = ((1, 0, 8), (2, 8, 16))

        def prepared(t, last):
            return [] if last else [(n, lo, hi) for n, (at, lo, hi) in enumerate(PREP) if at == t]

        def n_of(g, t, per, c):
            return g * (SPG * per) + (t * per + c)

        @block.sync
        def _(sp):
            with sp.Fori(0, GROUPS - 1) as g:
                sp.dma_start(WB[:, 0:8, :].rearrange("p (t c) k -> p t (c k)", t=2),
                             w0[bass.ds(g * 256, 256), :].rearrange("(t p) k -> p t k", p=P)).then_inc(S["wb_ld"], 16)
                sp.dma_start(WB[:, 8:16, :].rearrange("p (t c) k -> p t (c k)", t=4),
                             w1[:, bass.ds(g * 256, 256)].rearrange("(t p) k -> p t k", p=P)).then_inc(S["wb_ld"], 16)
                sp.wait_ge(S["qkv_lo"], g * 2 + 2)
                load_qkv(sp, g + 1)
                sp.wait_ge(S["wt_lo"], g * 4 + 4)
                sp.dma_start(w0t_dram.rearrange("p (s c n) -> p s c n", s=2, c=KC)[:, :, :, bass.ds(g * 256, 256)],
                             WS0[:, :, :, :]).then_inc(S["w_st"], 16)
                sp.dma_start(w1t_dram.rearrange("p (s c n) -> p s c n", s=2, c=IC)[:, :, bass.ds(g * 2, 2), :],
                             WS1[:, :, :, :]).then_inc(S["w_st"], 16)
                sp.wait_ge(S["w_st"], g * 32 + 32)
                sp.wait_ge(S["o_lo"], g + 1)
                load_o(sp, g + 1)
            sp.wait_ge(S["qkv_lo"], 2 * GROUPS)
            sp.wait_ge(S["o_lo"], GROUPS)
            sp.dma_start(W0T[:, :, :, :], w0t_dram.rearrange("p (s c n) -> p s c n", s=2, c=KC)).then_inc(w0_ld, 16)

        @block.gpsimd
        def _(pool):
            pool.memset(V[:, :, :, :, :], 0.0).then_inc(S["zeroed"], 1)
            with pool.Fori(0, GROUPS - 1) as g:
                for n, (t, lo, hi) in enumerate(PREP):
                    v = VW[:, n, 0:hi - lo, :]
                    pool.wait_ge(S["wsum"], g * 2 + (n + 1))
                    pool.tensor_tensor(v, v, MW[:, 0:hi - lo, :], ALU.subtract).then_inc(S["wq_done"], 1)
                    pool.wait_ge(S["wq_done"], g * 2 + (n + 1))
                    pool.tensor_tensor(v, v, ws[:, lo:hi].unsqueeze(2).to_broadcast([P, hi - lo, P]), ALU.mult).then_inc(S["wqs_done"], 1)

        @block.tensor
        def _(pe):
            def project(g, t, units):
                for u in units:
                    bank = pj[u % 2]
                    if u == 0:
                        pe.wait_ge(S["qkv_lo"], g * 2 + 2)
                    if not (isinstance(g, int) and g == 0 and t == 0 and u < 2):
                        pe.wait_ge(S["pj_lo"], n_of(g, t, 6, u - 1))
                    tokens = slice(t * BLOCK, (t + 1) * BLOCK)
                    if u < 5:
                        for n, (k, (a, b)) in enumerate([(k, ab) for ab in PASSES for k in range(KC)]):
                            w = WQ[:, a, k, u * HEAD0:(u + 1) * HEAD0] if u < 4 else WKV[:, a, k, 0, :]
                            src = XT if u < 4 else CT
                            last = pe.matmul(bank[:, :], w, src[:, b, k, tokens], start=n == 0, stop=n == 3 * KC - 1)
                    else:
                        for i in range(BT):
                            for n, (k, (a, b)) in enumerate([(k, ab) for ab in PASSES for k in range(KC)]):
                                own = slice(t * BLOCK + i * P, t * BLOCK + (i + 1) * P)
                                last = pe.matmul(bank[:, i * P:(i + 1) * P], CT[:, a, k, own], WKV[:, b, k, 1, :],
                                                 start=n == 0, stop=n == 3 * KC - 1)
                    last.then_inc(S["pj_done"], 1)

            def scores(g, t):
                pe.wait_ge(S["pj_lo"], n_of(g, t, 6, 5))
                for jp in range(2):
                    for b in range(BB):
                        for n, (qa, ka) in enumerate(PASSES):
                            last = pe.matmul(sc[jp][:, b * SEQ:(b + 1) * SEQ], QT[:, qa, b, 2 * jp:2 * jp + 2, :],
                                             KT[:, ka, b, :], start=n == 0, stop=n == 2)
                    last.then_inc(S["sc_done"], 1)

            def transpose_probs(g, t):
                pe.wait_ge(S["p_done"], n_of(g, t, 2, 2))
                for i in range(BT):
                    for jp in range(2):
                        at = (i % 2) * 256 + jp * P
                        last = pe.transpose(tv[i // 2][:, at:at + P],
                                            E[:, jp, 2 * i:2 * i + 2, :], ident[:, :])
                    if i % 2:
                        last.then_inc(S["tp_done"], 1)

            def weigh_values(g, t):
                pe.wait_ge(S["pj_lo"], n_of(g, t, 6, 6))
                for i in range(BT):
                    if i < 2:
                        pe.wait_ge(S["tp_lo"], n_of(g, t, 2, 2))
                    else:
                        pe.wait_ge(S["ot_lo"], n_of(g, t, 4, i - 1))
                    for h in range(2):
                        for n, (a, b) in enumerate(PASSES):
                            last = pe.matmul(tv[i % 2][:, h * 256:(h + 1) * 256], V[:, a, i, h, :], PT[:, b, i, :],
                                             start=n == 0, stop=n == 2)
                    last.then_inc(S["pv_done"], 1)

            def project_out(g, t):
                pe.wait_ge(S["o_lo"], g + 1)
                for i in range(BT):
                    pe.wait_ge(S["ot_lo"], n_of(g, t, 4, i + 1))
                    if i >= 2:
                        pe.wait_ge(S["x_acc"], n_of(g, t, 4, i - 1))
                    for n, (j, (a, b)) in enumerate([(j, ab) for j in range(REP) for ab in PASSES]):
                        last = pe.matmul(xp[i % 2][:, :], OT[:, a, j, i * P:(i + 1) * P], WO[:, b, j, :],
                                         start=n == 0, stop=n == 3 * REP - 1)
                    last.then_inc(S["xp_done"], 1)

            def transpose_weights(g, n, lo, hi):
                pe.wait_ge(S["wqs_done"], g * 2 + (n + 1))
                for u in range(lo // 4, hi // 4):
                    pe.wait_ge(S["x_acc"], n_of(g, PREP[n][0], 4, 3 + u - lo // 4))
                    for i in range(4):
                        slot = i if u < 2 else (i % 2) * 2 + i // 2
                        last = pe.transpose(xp[u - lo // 4][:, slot * P:(slot + 1) * P], VW[:, n, 4 * u + i - lo, :], ident[:, :])
                    last.then_inc(S["wt_done"], 1)

            def group(g, last):
                for t in range(SPG):
                    nxt = (g, t + 1) if t < SPG - 1 else (g + 1, 0)
                    more = not (last and t == SPG - 1)
                    scores(g, t)
                    if more:
                        project(*nxt, range(4))
                    transpose_probs(g, t)
                    split = prepared(t - 1, last)
                    for p in split:
                        transpose_weights(g, *p)
                    if more:
                        project(*nxt, (4,))
                    weigh_values(g, t)
                    if more:
                        project(*nxt, (5,))
                    for n, lo, hi in split:
                        pe.wait_ge(S["wt_lo"], g * 4 + hi // 4)
                    project_out(g, t)

            pe.sem_inc(S["xp_done"], 1)
            pe.wait_ge(S["zeroed"], 1)
            project(0, 0, range(6))
            with pe.Fori(0, GROUPS - 1) as g:
                group(g, False)
            group(GROUPS - 1, True)

        def q_bank(u):
            return pj[u % 2][:, :].rearrange("p (b t) -> p b t", b=BB)

        def v_bank(h):
            return pj[1][h * 64:(h + 1) * 64, :].rearrange("p (i d) -> p i d", i=BT)

        def o_bank(i):
            return tv[i % 2][:, :].rearrange("p (b j t) -> p b j t", b=2, j=REP)

        def o_out(part, i):
            return OT[:, part, :, i * P:(i + 1) * P].rearrange("p j (b t) -> p b j t", b=2)

        def w_bank(u, lo):
            return xp[u - lo // 4][:, :].rearrange("p (c n) -> p c n", c=4 if u < 2 else 2)

        def w_out(part, u):
            return WS0[:, part, :, u * P:(u + 1) * P] if u < 2 else WS1[:, part, :, (u - 2) * 256:(u - 1) * 256]

        @block.scalar
        def _(act):
            def weights_times_rec(g, n, lo, hi):
                act.wait_ge(S["wstep"], g * SCALE_STEPS + SCALE_STEPS)
                for c in range(lo, hi):
                    last = act.activation(VW[:, n, c - lo, :], WB[:, c, :], ACT.Copy, scale=wh[:, c:c + 1])
                last.then_inc(S["ww_done"], 1)

            def high_weights(g, n, lo, hi):
                for u in range(lo // 4, hi // 4):
                    act.wait_ge(S["wt_done"], g * 4 + (u + 1))
                    act.activation(w_out(0, u), w_bank(u, lo), ACT.Copy, scale=WEIGHT_SCALE).then_inc(S["wt_hi"], 1)

            def high(g, t, units):
                for u in units:
                    act.wait_ge(S["pj_done"], n_of(g, t, 6, u + 1))
                    if u < 4:
                        act.activation(QT[:, 0, :, u, :], q_bank(u), ACT.Copy, scale=UNSCALE).then_inc(S["pj_hi"], 1)
                    elif u == 4:
                        act.activation(KT[:, 0, :, :], q_bank(u), ACT.Copy, scale=UNSCALE).then_inc(S["pj_hi"], 1)
                    else:
                        act.activation(V[0:64, 0, :, 0, :], v_bank(0), ACT.Copy, scale=UNSCALE)
                        act.activation(V[64:128, 0, :, 1, :], v_bank(1), ACT.Copy, scale=UNSCALE).then_inc(S["pj_hi"], 1)

            def group(g, last):
                for t in range(SPG):
                    nxt = (g, t + 1) if t < SPG - 1 else (g + 1, 0)
                    more = not (last and t == SPG - 1)
                    for jp in range(2):
                        act.wait_ge(S["sub_done"], n_of(g, t, 2, jp + 1))
                        act.activation(E[:, jp, :, :], E[:, jp, :, :], ACT.Exp, scale=exp_scale).then_inc(S["exp_done"], 1)
                    if more:
                        high(*nxt, range(2))
                    for p in prepared(t, last):
                        weights_times_rec(g, *p)
                    if more:
                        high(*nxt, range(2, 4))
                    if last and t in (1, 2):
                        stats_x(act, t - 1)
                    for i in range(2):
                        act.wait_ge(S["tp_done"], n_of(g, t, 2, i + 1))
                        act.activation(PT[:, 0, 2 * i:2 * i + 2, :], tv[i][:, :].rearrange("p (i n) -> p i n", i=2),
                                       ACT.Copy).then_inc(S["tp_hi"], 1)
                    for p in prepared(t - 1, last):
                        high_weights(g, *p)
                    if t == SPG - 2 and not last:
                        high_q(act, g + 1)
                    if t == 0:
                        act.wait_ge(S["so_ld"], g * 16 + 16)
                        act.wait_ge(S["xp_done"], g * (SPG * 4) + 1)
                        act.activation(WO[:, 0, :, :], SO[:, :, :], ACT.Copy, scale=WEIGHT_SCALE).then_inc(S["o_hi"], 1)
                    if more:
                        high(*nxt, (4,))
                    for i in range(BT):
                        act.wait_ge(S["pv_done"], n_of(g, t, 4, i + 1))
                        act.activation(o_out(0, i), o_bank(i), ACT.Copy).then_inc(S["ot_hi"], 1)
                    if more:
                        high(*nxt, (5,))
                    if t == SPG - 2 and not last:
                        high_kv(act, g + 1)

            high(0, 0, range(5))
            act.wait_ge(S["zeroed"], 1)
            high(0, 0, (5,))
            with act.Fori(0, GROUPS - 1) as g:
                group(g, False)
            group(GROUPS - 1, True)

        @block.vector
        def _(dve):
            def low(g, t, u):
                dve.wait_ge(S["pj_hi"], n_of(g, t, 6, u + 1))
                if u < 5:
                    to = (QT[:, 1, :, u, :], QT[:, 0, :, u, :]) if u < 4 else (KT[:, 1, :, :], KT[:, 0, :, :])
                    dve.scalar_tensor_tensor(out=to[0], in0=q_bank(u), scalar=UNSCALE, in1=to[1],
                                             op0=ALU.mult, op1=ALU.subtract).then_inc(S["pj_lo"], 1)
                else:
                    for h in range(2):
                        rows = slice(h * 64, (h + 1) * 64)
                        last = dve.scalar_tensor_tensor(out=V[rows, 1, :, h, :], in0=v_bank(h), scalar=UNSCALE,
                                                        in1=V[rows, 0, :, h, :], op0=ALU.mult, op1=ALU.subtract)
                    last.then_inc(S["pj_lo"], 1)

            def scale_weights(g):
                dve.wait_ge(S["wb_ld"], g * 32 + 32)
                dve.tensor_reduce(wa[:, :], WB[:, :, :], AX.X, ALU.max, apply_absolute_value=True).then_inc(S["wa_done"], 1)
                dve.wait_ge(S["wa_done"], g + 1)
                quant_scales(dve, wa[:, :], ws[:, :], wh[:, :], wl[:, :], wtmp, S["wstep"], g * SCALE_STEPS)

            def weights_add_rest(g, n, lo, hi):
                dve.wait_ge(S["ww_done"], g * 2 + (n + 1))
                for c in range(hi - lo):
                    last = dve.scalar_tensor_tensor(out=VW[:, n, c, :], in0=WB[:, lo + c, :], scalar=wl[:, lo + c:lo + c + 1],
                                                    in1=VW[:, n, c, :], op0=ALU.mult, op1=ALU.add)
                last.then_inc(S["wv_done"], 1)

            def weights_to_grid(g, n, lo, hi):
                dve.wait_ge(S["wv_done"], g * 2 + (n + 1))
                round_to_grid(dve, VW[:, n, 0:hi - lo, :], MW[:, 0:hi - lo, :],
                              [S[x] for x in ("wbits", "wm_done", "wsum")], g * 2 + (n + 1))

            def low_weights(g, n, lo, hi):
                for u in range(lo // 4, hi // 4):
                    dve.wait_ge(S["wt_hi"], g * 4 + (u + 1))
                    dve.scalar_tensor_tensor(out=w_out(1, u), in0=w_bank(u, lo), scalar=WEIGHT_SCALE, in1=w_out(0, u),
                                             op0=ALU.mult, op1=ALU.subtract).then_inc(S["wt_lo"], 1)

            def scores_less_max(g, t, jp):
                s3 = sc[jp][:, :].rearrange("p (b k) -> p b k", b=BB)
                dve.wait_ge(S["sc_done"], n_of(g, t, 2, jp + 1))
                dve.reduce_max(ST[:, 0, jp, :], s3, AX.X).then_inc(S["max_done"], 1)
                dve.wait_ge(S["max_done"], n_of(g, t, 2, jp + 1))
                dve.tensor_tensor(E[:, jp, :, :], s3, ST[:, 0, jp, :].unsqueeze(2).to_broadcast([P, BB, SEQ]),
                                  ALU.subtract).then_inc(S["sub_done"], 1)

            def normalise(g, t, jp):
                at = n_of(g, t, 2, jp + 1)
                dve.wait_ge(S["exp_done"], at)
                dve.reduce_sum(ST[:, 1, jp, :], E[:, jp, :, :], AX.X).then_inc(S["sum_done"], 1)
                dve.wait_ge(S["sum_done"], at)
                dve.reciprocal(ST[:, 2, jp, :], ST[:, 1, jp, :]).then_inc(S["rcp_done"], 1)
                dve.wait_ge(S["rcp_done"], at)
                dve.tensor_tensor(E[:, jp, :, :], E[:, jp, :, :], ST[:, 2, jp, :].unsqueeze(2).to_broadcast([P, BB, SEQ]),
                                  ALU.mult).then_inc(S["p_done"], 1)

            def group(g, last):
                for t in range(SPG):
                    nxt = (g, t + 1) if t < SPG - 1 else (g + 1, 0)
                    more = not (last and t == SPG - 1)

                    def x_ahead(n):
                        if last and t in (1, 2):
                            x_pieces[n](dve, t - 1)

                    scores_less_max(g, t, 0)
                    scores_less_max(g, t, 1)
                    if more:
                        low(*nxt, 0)
                    normalise(g, t, 0)
                    if more:
                        low(*nxt, 1)
                    normalise(g, t, 1)
                    if more:
                        low(*nxt, 2)
                    x_ahead(0)
                    if more:
                        low(*nxt, 3)
                    x_ahead(1)
                    for i in range(2):
                        dve.wait_ge(S["tp_hi"], n_of(g, t, 2, i + 1))
                        dve.tensor_tensor(PT[:, 1, 2 * i:2 * i + 2, :], tv[i][:, :].rearrange("p (i n) -> p i n", i=2),
                                          PT[:, 0, 2 * i:2 * i + 2, :], ALU.subtract).then_inc(S["tp_lo"], 1)
                    for p in prepared(t - 1, last):
                        low_weights(g, *p)
                    if more:
                        low(*nxt, 4)
                    x_ahead(2)
                    for i in range(BT):
                        dve.wait_ge(S["ot_hi"], n_of(g, t, 4, i + 1))
                        dve.tensor_tensor(o_out(1, i), o_bank(i), o_out(0, i), ALU.subtract).then_inc(S["ot_lo"], 1)
                    if t == 0:
                        dve.wait_ge(S["o_hi"], g + 1)
                        dve.scalar_tensor_tensor(out=WO[:, 1, :, :], in0=SO[:, :, :], scalar=WEIGHT_SCALE, in1=WO[:, 0, :, :],
                                                 op0=ALU.mult, op1=ALU.subtract).then_inc(S["o_lo"], 1)
                    if t == SPG - 2 and not last:
                        low_q(dve, g + 1)
                    for p in prepared(t, last):
                        weights_add_rest(g, *p)
                    x_ahead(3)
                    if more:
                        low(*nxt, 5)
                    for p in prepared(t, last):
                        weights_to_grid(g, *p)
                    for i in range(BT):
                        if t == 0 and i == 2 and not last:
                            scale_weights(g)
                        dve.wait_ge(S["xp_done"], n_of(g, t, 4, i + 2))
                        xt = X[:, t * BT + i, :]
                        dve.scalar_tensor_tensor(out=xt, in0=xp[i % 2][:, :], scalar=UNSCALE, in1=xt,
                                                 op0=ALU.mult, op1=ALU.add).then_inc(S["x_acc"], 1)
                        if i == 0:
                            x_ahead(4)
                        if i == 1 and t == SPG - 2 and not last:
                            low_kv(dve, g + 1)

            for u in range(6):
                low(0, 0, u)
            with dve.Fori(0, GROUPS - 1) as g:
                group(g, False)
            group(GROUPS - 1, True)


def ffn0(nc, sb, pb, sem, X, ident, ahead_of_ffn0, x_scales, w1t_dram, b0, b1):
    with ExitStack() as ph:
        W0T, XB, w0_ld, x_pieces, stats_x = ahead_of_ffn0
        xs, xh, xl, xstep = x_scales
        W1T = sb(ph, "W1T", [P, 2, IC, DIM], F16)
        B0 = sb(ph, "B0", [P, INNER], BF16)
        B1 = sb(ph, "B1", [P, DIM], BF16)
        VX = sb(ph, "VX", [P, KC, P], F32)
        MX = sb(ph, "MX", [P, KC, P], F32)
        QX = sb(ph, "QX", [P, KC, P], F32)
        XD = sb(ph, "XD", [P, 2, 2, KC, P], F16)
        DP = sb(ph, "DP", [P, INNER], F32)
        DB = sb(ph, "DB", [P, 2, IC, P], BF16)
        da = sb(ph, "damax", [P, IC], F32)
        ds_, dh, dl = (sb(ph, "d" + n, [P, 2, IC], F32) for n in ("scale", "rec_hi", "rec_lo"))
        dtmp = sb(ph, "dtmp", [P, 5, IC], F32)
        VD = sb(ph, "VD", [P, 2, IC, P], F32)
        MD = sb(ph, "MD", [P, IC, P], F32)
        QD = sb(ph, "QD", [P, IC, P], F32)
        DT = sb(ph, "DT", [P, 2, IC, P], F16)
        EB = sb(ph, "EB", [P, 2, DIM], BF16)
        db = [pb(ph, f"db{i}") for i in range(4)]
        et = [pb(ph, f"et{i}") for i in range(2)]
        xt = pb(ph, "xt")
        eb = pb(ph, "eb")
        names = ("w1_ld b_ld xw_done xv_done xbits xm_done xsum xq_done xqs_done "
                 "xt_done xt_hi xt_lo d_done bias_done gelu_done da_done dstep dw_done dv_done dbits dm_done dsum "
                 "dq_done dqs_done et_done et_hi et_lo e_done eb_done x_done")
        S = {n: sem(ph, "f0_" + n) for n in names.split()}
        block = ph.enter_context(nc.Block())
        X2_STEP, X3_STEPS = -1, (2, 3, 3, 4, 5)
        THIRDS = [(0, 4), (4, 8), (8, 14)]
        GROUP_OF = [(0, 4), (4, 8), (8, 12), (12, 14)]

        def ahead(tile, by):
            return tile[0], tile[1] + by

        def fixed(tile):
            return 2 * tile[0] + tile[1] if isinstance(tile[0], int) else None

        def live(tile):
            return fixed(tile) is None or 0 <= fixed(tile) < TILES

        def nr(tile):
            return 2 * tile[0] + tile[1]

        def count(tile, per, c):
            return tile[0] * (2 * per) + (tile[1] * per + c)

        def steps(engine, step):
            for i in range(-2, 6):
                step((0, i))
            with engine.Fori(3, TILES // 2 - 1) as p:
                step((p, 0))
                step((p, 1))
            for i in range(TILES - 2, TILES + 3):
                step((0, i))

        @block.sync
        def _(sp):
            sp.dma_start(B0[:, :], b0.partition_broadcast(P)).then_inc(S["b_ld"], 16)
            sp.dma_start(B1[:, :], b1.partition_broadcast(P)).then_inc(S["b_ld"], 16)
            sp.dma_start(W1T[:, :, :, :], w1t_dram.rearrange("p (s c n) -> p s c n", s=2, c=IC)).then_inc(S["w1_ld"], 16)

        @block.tensor
        def _(pe):
            def first_product(i, qs):
                for q in qs:
                    if q == 0:
                        pe.wait_ge(S["xt_lo"], count(i, 1, 1))
                    if live(ahead(i, -1)):
                        pe.wait_ge(S["bias_done"], count(i, 4, q - 3))
                    for n, (k, (a, b)) in enumerate([(k, ab) for ab in PASSES for k in range(KC)]):
                        last = pe.matmul(db[q][:, 0:NQ], XD[:, i[1] % 2, a, k, :], W0T[:, b, k, q * NQ:(q + 1) * NQ],
                                         start=n == 0, stop=n == 3 * KC - 1)
                    last.then_inc(S["d_done"], 1)

            def transpose_x(i):
                pe.wait_ge(S["xqs_done"], count(i, 1, 1))
                for k in range(KC):
                    last = pe.transpose(xt[:, k * P:(k + 1) * P], QX[:, k, :], ident[:, :])
                last.then_inc(S["xt_done"], 1)

            def transpose_hidden(i, n):
                if n < 3:
                    pe.wait_ge(S["dqs_done"], count(i, 3, n + 1))
                if n >= 2 or live(ahead(i, -1)):
                    pe.wait_ge(S["et_lo"], count(i, 4, n - 1))
                for c in range(*GROUP_OF[n]):
                    last = pe.transpose(et[n % 2][:, (c % 4) * P:(c % 4 + 1) * P], QD[:, c, :], ident[:, :])
                last.then_inc(S["et_done"], 1)

            def second_product(i):
                if live(ahead(i, -1)):
                    pe.wait_ge(S["eb_done"], count(i, 1, 0))
                for n in range(4):
                    pe.wait_ge(S["et_lo"], count(i, 4, n + 1))
                    for c in range(*GROUP_OF[n]):
                        for a, b in PASSES:
                            last = pe.matmul(eb[:, :], DT[:, a, c, :], W1T[:, b, c, :],
                                             start=c == 0 and (a, b) == PASSES[0], stop=c == IC - 1 and (a, b) == PASSES[-1])
                    if n == 0:
                        transpose_hidden(i, 3)
                last.then_inc(S["e_done"], 1)

            def step(i):
                old, nxt = ahead(i, -2), ahead(i, 1)
                if live(old):
                    transpose_hidden(old, 0)
                    transpose_hidden(old, 1)
                if fixed(i) == 0:
                    pe.wait_ge(w0_ld, 16)
                if live(i):
                    first_product(i, (0, 1, 2))
                if live(old):
                    transpose_hidden(old, 2)
                if live(nxt):
                    transpose_x(nxt)
                if live(i):
                    first_product(i, (3,))
                if live(old):
                    if fixed(i) == 2:
                        pe.wait_ge(S["w1_ld"], 16)
                    second_product(old)

            steps(pe, step)

        def et_bank(n):
            a, b = GROUP_OF[n]
            return et[n % 2][:, 0:(b - a) * P].rearrange("p (c t) -> p c t", c=b - a)

        @block.scalar
        def _(act):
            def x_times_rec(i):
                if live(ahead(i, -1)):
                    act.wait_ge(S["xqs_done"], count(i, 1, 0))
                if fixed(i) in range(0, TILES, BT):
                    act.wait_ge(xstep, (fixed(i) // BT + 1) * SCALE_STEPS)
                for k in range(KC):
                    last = act.activation(VX[:, k, :], XB[:, nr(i), k, :], ACT.Copy, scale=xh[:, nr(i), k:k + 1])
                last.then_inc(S["xw_done"], 1)

            def d_times_rec(i):
                r = i[1] % 2
                act.wait_ge(S["dstep"], count(i, SCALE_STEPS, SCALE_STEPS))
                if live(ahead(i, -2)):
                    act.wait_ge(S["dqs_done"], count(i, 3, -3))
                for c in range(IC):
                    last = act.activation(VD[:, r, c, :], DB[:, r, c, :], ACT.Copy, scale=dh[:, r, c:c + 1])
                last.then_inc(S["dw_done"], 1)

            def gelu(i, qs):
                for q in qs:
                    act.wait_ge(S["bias_done"], count(i, 4, q + 1))
                    act.activation(DB[:, i[1] % 2, :, :].rearrange("p c t -> p (c t)")[:, q * NQ:(q + 1) * NQ],
                                   DP[:, q * NQ:(q + 1) * NQ], ACT.Gelu).then_inc(S["gelu_done"], 1)

            def high_x(i):
                act.wait_ge(S["xt_done"], count(i, 1, 1))
                act.activation(XD[:, i[1] % 2, 0, :, :], xt[:, :].rearrange("p (k t) -> p k t", k=KC), ACT.Copy).then_inc(S["xt_hi"], 1)

            def high_e(i, ns):
                for n in ns:
                    a, b = GROUP_OF[n]
                    act.wait_ge(S["et_done"], count(i, 4, n + 1))
                    act.activation(DT[:, 0, a:b, :], et_bank(n), ACT.Copy).then_inc(S["et_hi"], 1)

            def step(i):
                old, hidden, nxt, after = (ahead(i, by) for by in (-2, -1, 1, 2))
                if live(old):
                    high_e(old, (0, 1))
                if live(hidden):
                    d_times_rec(hidden)
                if live(i):
                    gelu(i, (0, 1))
                if live(old):
                    high_e(old, (2,))
                if live(nxt):
                    high_x(nxt)
                if live(after):
                    x_times_rec(after)
                if live(i):
                    gelu(i, (2, 3))
                if live(old):
                    high_e(old, (3,))
                if fixed(i) == X2_STEP:
                    stats_x(act, 2)
                if fixed(i) == X3_STEPS[1]:
                    stats_x(act, 3)

            steps(act, step)

        @block.vector
        def _(dve):
            def quant_x(i):
                to_grid(dve, VX[:, :, :], MX[:, :, :], XB[:, nr(i), :, :], lambda c: xl[:, nr(i), c:c + 1], KC,
                        [S[n] for n in ("xw_done", "xv_done", "xbits", "xm_done", "xsum")], count(i, 1, 1))

            def scales_d(i):
                r = i[1] % 2
                dve.wait_ge(S["gelu_done"], count(i, 4, 4))
                dve.tensor_reduce(da[:, :], DB[:, r, :, :], AX.X, ALU.max, apply_absolute_value=True).then_inc(S["da_done"], 1)
                dve.wait_ge(S["da_done"], count(i, 1, 1))
                quant_scales(dve, da[:, :], ds_[:, r, :], dh[:, r, :], dl[:, r, :], dtmp, S["dstep"], count(i, SCALE_STEPS, 0))

            def add_rest(i):
                r = i[1] % 2
                dve.wait_ge(S["dw_done"], count(i, 1, 1))
                for c in range(IC):
                    last = dve.scalar_tensor_tensor(out=VD[:, r, c, :], in0=DB[:, r, c, :], scalar=dl[:, r, c:c + 1],
                                                    in1=VD[:, r, c, :], op0=ALU.mult, op1=ALU.add)
                last.then_inc(S["dv_done"], 1)

            def grid_d(i):
                V = VD[:, i[1] % 2, :, :]
                if live(ahead(i, -1)):
                    dve.wait_ge(S["dq_done"], count(i, 3, 0))
                dve.wait_ge(S["dv_done"], count(i, 1, 1))
                round_to_grid(dve, V, MD[:, :, :], [S[n] for n in ("dbits", "dm_done", "dsum")], count(i, 1, 1))

            def add_bias(i, qs):
                for q in qs:
                    dve.wait_ge(S["d_done"], count(i, 4, q + 1))
                    dve.scalar_tensor_tensor(out=DP[:, q * NQ:(q + 1) * NQ], in0=db[q][:, 0:NQ], scalar=UNSCALE,
                                             in1=B0[:, q * NQ:(q + 1) * NQ], op0=ALU.mult, op1=ALU.add).then_inc(S["bias_done"], 1)

            def low_x(i):
                dve.wait_ge(S["xt_hi"], count(i, 1, 1))
                dve.tensor_tensor(XD[:, i[1] % 2, 1, :, :], xt[:, :].rearrange("p (k t) -> p k t", k=KC), XD[:, i[1] % 2, 0, :, :],
                                  ALU.subtract).then_inc(S["xt_lo"], 1)

            def low_e(i, ns):
                for n in ns:
                    a, b = GROUP_OF[n]
                    dve.wait_ge(S["et_hi"], count(i, 4, n + 1))
                    dve.tensor_tensor(DT[:, 1, a:b, :], et_bank(n), DT[:, 0, a:b, :], ALU.subtract).then_inc(S["et_lo"], 1)

            def add_bias1(i):
                dve.wait_ge(S["e_done"], count(i, 1, 1))
                dve.scalar_tensor_tensor(out=EB[:, i[1] % 2, :], in0=eb[:, :], scalar=UNSCALE, in1=B1[:, :],
                                         op0=ALU.mult, op1=ALU.add).then_inc(S["eb_done"], 1)

            def step(i):
                older, old, hidden, nxt, after = (ahead(i, by) for by in (-3, -2, -1, 1, 2))
                if live(older):
                    add_bias1(older)
                if live(old):
                    low_e(old, (0, 1))
                if live(i):
                    add_bias(i, (0, 1))
                if live(hidden):
                    add_rest(hidden)
                    grid_d(hidden)
                if live(old):
                    low_e(old, (2,))
                if live(nxt):
                    low_x(nxt)
                if live(i):
                    add_bias(i, (2, 3))
                if live(after):
                    quant_x(after)
                if live(old):
                    low_e(old, (3,))
                for n, piece in enumerate(x_pieces):
                    if fixed(i) == X2_STEP:
                        piece(dve, 2)
                    if fixed(i) == X3_STEPS[n]:
                        piece(dve, 3)
                if live(i):
                    scales_d(i)

            dve.wait_ge(S["b_ld"], 32)
            steps(dve, step)

        @block.gpsimd
        def _(pool):
            def quant_x(i):
                V, M = VX[:, :, :], MX[:, :, :]
                pool.wait_ge(S["xsum"], count(i, 1, 1))
                pool.tensor_tensor(V, V, M, ALU.subtract).then_inc(S["xq_done"], 1)
                if live(ahead(i, -1)):
                    pool.wait_ge(S["xt_lo"], count(i, 1, 0))
                pool.wait_ge(S["xq_done"], count(i, 1, 1))
                pool.tensor_tensor(QX[:, :, :], V, xs[:, nr(i), :].unsqueeze(2).to_broadcast([P, KC, P]),
                                   ALU.mult).then_inc(S["xqs_done"], 1)

            def quant_d(i):
                r = i[1] % 2
                pool.wait_ge(S["dsum"], count(i, 1, 1))
                for n, (a, b) in enumerate(THIRDS):
                    pool.tensor_tensor(VD[:, r, a:b, :], VD[:, r, a:b, :], MD[:, a:b, :], ALU.subtract).then_inc(S["dq_done"], 1)
                    if n == 0 and live(ahead(i, -1)):
                        pool.wait_ge(S["et_done"], count(i, 4, 0))
                    pool.wait_ge(S["dq_done"], count(i, 3, n + 1))
                    pool.tensor_tensor(QD[:, a:b, :], VD[:, r, a:b, :],
                                       ds_[:, r, a:b].unsqueeze(2).to_broadcast([P, b - a, P]), ALU.mult).then_inc(S["dqs_done"], 1)

            def add_x(i):
                pool.wait_ge(S["eb_done"], count(i, 1, 1))
                pool.tensor_tensor(X[:, nr(i), :], X[:, nr(i), :], EB[:, i[1] % 2, :], ALU.add).then_inc(S["x_done"], 1)

            def step(i):
                older, hidden, nxt = (ahead(i, by) for by in (-3, -1, 1))
                if live(nxt):
                    quant_x(nxt)
                if live(older):
                    add_x(older)
                if live(hidden):
                    quant_d(hidden)

            steps(pool, step)


def attention1(nc, sb, pb, sem, X, ident, CT, rstd, nmr, ln, wq, wk, wv, wo):
    exp_scale = float(HEAD1) ** -0.5
    HALF = TILES // 2
    with ExitStack() as ph:
        QT = sb(ph, "QT1", [P, 2, BATCH, REP, SEQ], F16)
        KT = sb(ph, "KT1", [P, 2, TOKENS], F16)
        V = sb(ph, "V1", [P, 2, TILES, P], F16)
        WQ = sb(ph, "WQ1", [P, 2, KC, REP, GROUPS, HEAD1], F16)
        WKV = sb(ph, "WKV1", [P, 2, KC, 2, P], F16)
        WO = sb(ph, "WO1", [P, 2, REP, DIM], F16)
        with ExitStack() as part:
            XT = sb(part, "XT1", [P, 2, KC, TOKENS], F16)
            SQ = sb(part, "SQ1", [P, KC, DIM], F32)
            SKV = sb(part, "SKV1", [P, KC, 2, P], F32)
            SO = sb(part, "SO1", [P, REP, DIM], F32)
            XN = sb(part, "XN1", [P, 2, DIM], F32)
            tp = [pb(part, f"n1_tp{i}") for i in range(2)]
            pj = [pb(part, f"n1_pj{i}") for i in range(2)]
            names = ("sq_ld skv_ld so_ld qkv_hi qkv_lo xn_done tp_done tp_hi tp_lo pj_done pj_hi pj_lo")
            S = {n: sem(part, "n1_" + n) for n in names.split()}
            stats_vector, stats_scalar, stats_ready, parts_before = ln
            block = part.enter_context(nc.Block())

            @block.sync
            def _(sp):
                sp.dma_start(SQ[:, :, :], wq.rearrange("(c p) n -> p c n", p=P)).then_inc(S["sq_ld"], 16)
                for i, w in enumerate((wk, wv)):
                    sp.dma_start(SKV[:, :, i, :], w.rearrange("(c p) n -> p c n", p=P)).then_inc(S["skv_ld"], 16)
                for g in range(GROUPS):
                    sp.dma_start(SO[g * HEAD1:(g + 1) * HEAD1, :, :],
                                 wo[g * REP * HEAD1:(g + 1) * REP * HEAD1, :].rearrange("(j d) n -> d j n", d=HEAD1)).then_inc(S["so_ld"], 16)

            @block.tensor
            def _(pe):
                def transposes(blk):
                    for i in range(BT):
                        pe.wait_ge(S["xn_done"], blk * BT + (i + 1))
                        if not (isinstance(blk, int) and blk == 0 and i < 2):
                            pe.wait_ge(S["tp_lo"], blk * BT + (i - 1))
                        for k in range(KC):
                            last = pe.transpose(tp[i % 2][:, k * P:(k + 1) * P], XN[:, i % 2, k * P:(k + 1) * P], ident[:, :])
                        last.then_inc(S["tp_done"], 1)

                def project(blk, units):
                    for u in units:
                        if not (isinstance(blk, int) and blk == 0 and u < 2):
                            pe.wait_ge(S["pj_lo"], blk * 6 + (u - 1))
                        if u == 0:
                            pe.wait_ge(S["tp_lo"], blk * BT + BT)
                        steps = [(k, ab) for ab in PASSES for k in range(KC)]
                        if u < 5:
                            for n, (k, (a, b)) in enumerate(steps):
                                if u < 4:
                                    w = WQ[:, a, k, u, :, :]
                                else:
                                    w = WKV[:, a, k, 0, :]
                                last = pe.matmul(pj[u % 2][:, :], w, (XT if u < 4 else CT)[:, b, k, bass.ds(blk * BLOCK, BLOCK)],
                                                 start=n == 0, stop=n == len(steps) - 1)
                        else:
                            for i in range(BT):
                                for n, (k, (a, b)) in enumerate(steps):
                                    last = pe.matmul(pj[1][:, i * P:(i + 1) * P], CT[:, a, k, bass.ds(blk * BLOCK + i * P, P)],
                                                     WKV[:, b, k, 1, :], start=n == 0, stop=n == len(steps) - 1)
                        last.then_inc(S["pj_done"], 1)

                transposes(0)
                pe.wait_ge(S["qkv_lo"], 3)
                project(0, range(4))
                transposes(1)
                project(0, (4, 5))
                with pe.Fori(1, BLOCKS - 1) as blk:
                    project(blk, range(4))
                    transposes(blk + 1)
                    project(blk, (4, 5))
                project(BLOCKS - 1, range(6))

            def q_columns(j):
                return SQ[:, :, :].rearrange("p k (g j d) -> p k j g d", g=GROUPS, j=REP)[:, :, j, :, :]

            def tp_bank(i):
                return tp[i % 2][:, :].rearrange("p (k t) -> p k t", k=KC)

            def x_out(part_, blk, i):
                return XT[:, part_, :, bass.ds(blk * BLOCK + i * P, P)]

            def pj_views(part_, blk, u):
                if u < 4:
                    return (QT[:, part_, bass.ds(blk * BB, BB), u, :], pj[u % 2][:, :].rearrange("p (b t) -> p b t", b=BB))
                if u == 4:
                    return KT[:, part_, bass.ds(blk * BLOCK, BLOCK)], pj[0][:, :]
                return V[:, part_, bass.ds(blk * BT, BT), :], pj[1][:, :].rearrange("p (i d) -> p i d", i=BT)

            @block.scalar
            def _(act):
                def high_x(blk):
                    for i in range(BT):
                        act.wait_ge(S["tp_done"], blk * BT + (i + 1))
                        act.activation(x_out(0, blk, i), tp_bank(i), ACT.Copy).then_inc(S["tp_hi"], 1)

                def high(blk, units):
                    for u in units:
                        act.wait_ge(S["pj_done"], blk * 6 + (u + 1))
                        to, bank = pj_views(0, blk, u)
                        act.activation(to, bank, ACT.Copy, scale=UNSCALE).then_inc(S["pj_hi"], 1)

                act.wait_ge(S["sq_ld"], 16)
                for j in range(REP):
                    last = act.activation(WQ[:, 0, :, j, :, :], q_columns(j), ACT.Copy, scale=WEIGHT_SCALE)
                last.then_inc(S["qkv_hi"], 1)
                act.wait_ge(S["skv_ld"], 32)
                act.activation(WKV[:, 0, :, :, :], SKV[:, :, :, :], ACT.Copy, scale=WEIGHT_SCALE).then_inc(S["qkv_hi"], 1)
                act.wait_ge(S["so_ld"], 16 * GROUPS)
                act.activation(WO[:, 0, :, :], SO[:, :, :], ACT.Copy, scale=WEIGHT_SCALE).then_inc(S["qkv_hi"], 1)
                stats_scalar(act, 2, (0,))
                high_x(0)
                with act.Fori(0, BLOCKS - 1) as blk:
                    high(blk, range(4))
                    high_x(blk + 1)
                    high(blk, (4, 5))
                high(BLOCKS - 1, range(6))

            @block.vector
            def _(dve):
                def norm(blk, i):
                    if not (isinstance(blk, int) and blk == 0 and i < 2):
                        dve.wait_ge(S["tp_done"], blk * BT + (i - 1))
                    t = blk * BT + i
                    dve.tensor_scalar(XN[:, i % 2, :], X[:, t, :], rstd[:, bass.ds(t, 1)], nmr[:, bass.ds(t, 1)],
                                      ALU.mult, ALU.add).then_inc(S["xn_done"], 1)

                def low_x(blk, i):
                    dve.wait_ge(S["tp_hi"], blk * BT + (i + 1))
                    dve.tensor_tensor(x_out(1, blk, i), tp_bank(i), x_out(0, blk, i), ALU.subtract).then_inc(S["tp_lo"], 1)

                def low(blk, units):
                    for u in units:
                        dve.wait_ge(S["pj_hi"], blk * 6 + (u + 1))
                        to, bank = pj_views(1, blk, u)
                        dve.scalar_tensor_tensor(out=to, in0=bank, scalar=UNSCALE, in1=pj_views(0, blk, u)[0],
                                                 op0=ALU.mult, op1=ALU.subtract).then_inc(S["pj_lo"], 1)

                def norm_block(blk):
                    norm(blk, 0)
                    norm(blk, 1)
                    for i in range(BT):
                        low_x(blk, i)
                        if i < 2:
                            norm(blk, i + 2)

                stats_vector(dve, 2, (0,))
                dve.wait_ge(stats_ready, parts_before(2) + 1)
                norm_block(0)
                dve.wait_ge(S["qkv_hi"], 1)
                for j in range(REP):
                    for k in range(KC):
                        last = dve.scalar_tensor_tensor(out=WQ[:, 1, k, j, :, :], in0=q_columns(j)[:, k, :, :], scalar=WEIGHT_SCALE,
                                                        in1=WQ[:, 0, k, j, :, :], op0=ALU.mult, op1=ALU.subtract)
                last.then_inc(S["qkv_lo"], 1)
                for n, (w, raw) in enumerate(((WKV, SKV), (WO, SO))):
                    dve.wait_ge(S["qkv_hi"], n + 2)
                    full = (slice(None),) * (len(raw.shape) - 1)
                    dve.scalar_tensor_tensor(out=w[(slice(None), 1) + full], in0=raw[(slice(None),) + full],
                                             scalar=WEIGHT_SCALE, in1=w[(slice(None), 0) + full],
                                             op0=ALU.mult, op1=ALU.subtract).then_inc(S["qkv_lo"], 1)
                with dve.Fori(0, BLOCKS - 1) as blk:
                    low(blk, range(4))
                    norm_block(blk + 1)
                    low(blk, (4, 5))
                low(BLOCKS - 1, range(6))

        with ExitStack() as part:
            mask = sb(part, "mask", [P, GROUPS], F16)
            KM = sb(part, "KM", [P, 2, 2, GROUPS, 2, SEQ], F16)
            VM = sb(part, "VM", [P, 2, 2, 2, 640], F16)
            E = sb(part, "E1", [P, 2, 4, GROUPS, SEQ], F32)
            ST = sb(part, "ST1", [P, 3, 4, GROUPS], F32)
            PT = sb(part, "PT1", [P, 2, 4, 2, 256], F16)
            OT = sb(part, "OT1", [P, 2, 2, REP, P], F16)
            sc = [pb(part, f"sc1_{i}") for i in range(4)]
            tp = [pb(part, f"a1_tp{i}") for i in range(2)]
            ob = pb(part, "ob1")
            xp = pb(part, "a1_xp")
            names = ("mask zeroed km_done vm_done sc_done max_done sub_done exp_done sum_done rcp_done p_done tp_done "
                     "tp_hi tp_lo ot_done ot_hi ot_lo xp_done x_acc")
            S = {n: sem(part, "a1_" + n) for n in names.split()}
            block = part.enter_context(nc.Block())

            def n_of(p, r, per, c):
                return p * (2 * per) + (r * per + c)

            def first(p, r):
                return isinstance(p, int) and p == 0 and r == 0

            @block.gpsimd
            def _(pool):
                pool.memset(mask[:, :], 1.0).then_inc(S["mask"], 1)
                pool.memset(VM[:, :, :, :, :], 0.0).then_inc(S["zeroed"], 1)
                for n, (step, base, cm) in enumerate(((-HEAD1, 0, 1), (HEAD1, HEAD1 - 1, -1))):
                    pool.wait_ge(S["mask"], n + 1)
                    pool.affine_select(out=mask[:, :], in_=mask[:, :], compare_op=ALU.is_ge, fill=0.0, base=base,
                                       pattern=[[step, GROUPS]], channel_multiplier=cm).then_inc(S["mask"], 1)

                def block_keys(p, r, t):
                    if not (isinstance(p, int) and p == 0):
                        pool.wait_ge(S["sc_done"], n_of(p - 1, r, 4, 4))
                    for s in range(2):
                        pool.tensor_tensor(KM[:, r, s, :, :, :].rearrange("p g b k -> p g (b k)"),
                                          KT[:, s, bass.ds(t * P, P)].unsqueeze(1).to_broadcast([P, GROUPS, P]),
                                          mask[:, :].unsqueeze(2).to_broadcast([P, GROUPS, P]), ALU.mult).then_inc(S["km_done"], 1)

                def normalise(p, r, us):
                    for u in us:
                        pool.wait_ge(S["rcp_done"], n_of(p, r, 4, u + 1))
                        e = E[:, r, u, :, :]
                        pool.tensor_tensor(e, e, ST[:, 2, u, :].unsqueeze(2).to_broadcast([P, GROUPS, SEQ]),
                                           ALU.mult).then_inc(S["p_done"], 1)

                pool.wait_ge(S["mask"], 3)
                block_keys(0, 0, 0)
                block_keys(0, 1, 1)
                for r in range(2):
                    normalise(0, r, range(4))
                    block_keys(1, r, 2 + r)
                with pool.Fori(1, HALF - 1) as p:
                    for r in range(2):
                        normalise(p, r, range(4))
                        block_keys(p + 1, r, 2 * p + 2 + r)
                for r in range(2):
                    normalise(HALF - 1, r, range(4))

            @block.tensor
            def _(pe):
                def scores(p, r, t, us):
                    for u in us:
                        b, jp = u // 2, u % 2
                        pe.wait_ge(S["km_done"], n_of(p, r, 2, 2))
                        if not first(p, r):
                            pe.wait_ge(S["sub_done"], n_of(p, r, 4, u - 3))
                        for n, (qa, ka) in enumerate(PASSES):
                            last = pe.matmul(sc[u][:, :], QT[:, qa, 2 * t + b, 2 * jp:2 * jp + 2, :], KM[:, r, ka, :, b, :],
                                             start=n == 0, stop=n == 2)
                        last.then_inc(S["sc_done"], 1)

                def transpose_probs(p, r, b):
                    pe.wait_ge(S["p_done"], n_of(p, r, 4, 2 * b + 2))
                    for h in range(2):
                        u = 2 * b + h
                        if u >= 2:
                            pe.wait_ge(S["tp_lo"], n_of(p, r, 4, u - 1))
                        for q in range(2):
                            for jp in range(2):
                                g = 4 * h + 2 * q
                                last = pe.transpose(tp[h][:, q * 256 + jp * P:q * 256 + (jp + 1) * P],
                                                    E[:, r, 2 * b + jp, g:g + 2, :], ident[:, :])
                        last.then_inc(S["tp_done"], 1)

                def weigh_values(p, r, b):
                    if b == 0:
                        pe.wait_ge(S["vm_done"], n_of(p, r, 1, 1))
                        if not first(p, r):
                            pe.wait_ge(S["ot_lo"], n_of(p, r, 1, 0))
                    n = 0
                    for h in range(2):
                        pe.wait_ge(S["tp_lo"], n_of(p, r, 4, 2 * b + h + 1))
                        for q in range(2):
                            gp = 2 * h + q
                            for va, pa in PASSES:
                                last = pe.matmul(ob[:, b * 256:(b + 1) * 256], VM[:, r, va, b, gp * P:(gp + 1) * P],
                                                 PT[:, pa, 2 * b + h, q, :], start=n == 0, stop=n == 11)
                                n += 1
                    if b == 1:
                        last.then_inc(S["ot_done"], 1)

                def project_out(p, r):
                    pe.wait_ge(S["ot_lo"], n_of(p, r, 1, 1))
                    if not first(p, r):
                        pe.wait_ge(S["x_acc"], n_of(p, r, 1, 0))
                    for n, (j, (a, b)) in enumerate([(j, ab) for j in range(REP) for ab in PASSES]):
                        last = pe.matmul(xp[:, :], OT[:, r, a, j, :], WO[:, b, j, :], start=n == 0, stop=n == 3 * REP - 1)
                    last.then_inc(S["xp_done"], 1)

                def tile(cur, old, out):
                    if old:
                        transpose_probs(*old, 0)
                    if cur:
                        scores(*cur, (0, 1))
                    if old:
                        transpose_probs(*old, 1)
                        weigh_values(*old, 0)
                    if cur:
                        scores(*cur, (2, 3))
                    if old:
                        weigh_values(*old, 1)
                    if out:
                        project_out(*out)

                tile((0, 0, 0), None, None)
                tile((0, 1, 1), (0, 0), None)
                with pe.Fori(1, HALF) as p:
                    tile((p, 0, 2 * p), (p - 1, 1), (p - 1, 0))
                    tile((p, 1, 2 * p + 1), (p, 0), (p - 1, 1))
                tile(None, (HALF - 1, 1), (HALF - 1, 0))
                project_out(HALF - 1, 1)

            def t_bank(u):
                return tp[u % 2][:, :].rearrange("p (q n) -> p q n", q=2)

            def o_bank():
                return ob[:, :].rearrange("p (b j t) -> p b j t", b=2, j=REP)

            def o_out(r, part_):
                return OT[:, r, part_, :, :].rearrange("p j (b t) -> p b j t", b=2)

            @block.scalar
            def _(act):
                def place_values(p, r, t):
                    if not (isinstance(p, int) and p == 0):
                        act.wait_ge(S["ot_done"], n_of(p - 1, r, 1, 1))
                    for b in range(2):
                        for h in range(2):
                            src = V[b * 64:(b + 1) * 64, :, t, :].rearrange("p s (q h d) -> p s q h d", q=4, h=2)[:, :, :, h, :]
                            to = VM[h * 64:(h + 1) * 64, r, :, b, :].rearrange("p s (q c) -> p s q c", q=4)[:, :, :, h * HEAD1:(h + 1) * HEAD1]
                            last = act.activation(to, src, ACT.Copy)
                    last.then_inc(S["vm_done"], 1)

                def exp(p, r, u):
                    act.wait_ge(S["sub_done"], n_of(p, r, 4, u + 1))
                    act.activation(E[:, r, u, :, :], E[:, r, u, :, :], ACT.Exp, scale=exp_scale).then_inc(S["exp_done"], 1)

                def high(p, r, u):
                    act.wait_ge(S["tp_done"], n_of(p, r, 4, u + 1))
                    act.activation(PT[:, 0, u, :, :], t_bank(u), ACT.Copy).then_inc(S["tp_hi"], 1)

                def tile(cur, old, place=None):
                    if old:
                        for u in range(4):
                            high(*old, u)
                    if cur:
                        exp(*cur, 0)
                        exp(*cur, 1)
                    if old:
                        act.wait_ge(S["ot_done"], n_of(*old, 1, 1))
                        act.activation(o_out(old[1], 0), o_bank(), ACT.Copy).then_inc(S["ot_hi"], 1)
                    if cur:
                        exp(*cur, 2)
                        exp(*cur, 3)
                    if place:
                        place_values(*place)

                act.wait_ge(S["zeroed"], 1)
                place_values(0, 0, 0)
                place_values(0, 1, 1)
                tile((0, 0), None)
                tile((0, 1), (0, 0))
                with act.Fori(1, HALF) as p:
                    tile((p, 0), (p - 1, 1), (p, 0, 2 * p))
                    tile((p, 1), (p, 0), (p, 1, 2 * p + 1))
                tile(None, (HALF - 1, 1))

            @block.vector
            def _(dve):
                def scores_less_max(p, r, us):
                    s3 = [sc[u][:, :].rearrange("p (g k) -> p g k", g=GROUPS) for u in range(4)]
                    for u in us:
                        dve.wait_ge(S["sc_done"], n_of(p, r, 4, u + 1))
                        dve.reduce_max(ST[:, 0, u, :], s3[u], AX.X).then_inc(S["max_done"], 1)
                    if not (isinstance(p, int) and p == 0):
                        dve.wait_ge(S["tp_done"], n_of(p - 1, r, 4, 4))
                    for u in us:
                        dve.wait_ge(S["max_done"], n_of(p, r, 4, u + 1))
                        dve.tensor_tensor(E[:, r, u, :, :], s3[u], ST[:, 0, u, :].unsqueeze(2).to_broadcast([P, GROUPS, SEQ]),
                                          ALU.subtract).then_inc(S["sub_done"], 1)

                def sums(p, r, us):
                    for u in us:
                        dve.wait_ge(S["exp_done"], n_of(p, r, 4, u + 1))
                        dve.reduce_sum(ST[:, 1, u, :], E[:, r, u, :, :], AX.X).then_inc(S["sum_done"], 1)
                    for u in us:
                        dve.wait_ge(S["sum_done"], n_of(p, r, 4, u + 1))
                        if not first(p, r):
                            dve.wait_ge(S["p_done"], n_of(p, r, 4, u - 3))
                        dve.reciprocal(ST[:, 2, u, :], ST[:, 1, u, :]).then_inc(S["rcp_done"], 1)

                def low(p, r, u):
                    dve.wait_ge(S["tp_hi"], n_of(p, r, 4, u + 1))
                    dve.tensor_tensor(PT[:, 1, u, :, :], t_bank(u), PT[:, 0, u, :, :], ALU.subtract).then_inc(S["tp_lo"], 1)

                def low_o(p, r):
                    dve.wait_ge(S["ot_hi"], n_of(p, r, 1, 1))
                    dve.tensor_tensor(o_out(r, 1), o_bank(), o_out(r, 0), ALU.subtract).then_inc(S["ot_lo"], 1)

                def add_x(p, r, t):
                    dve.wait_ge(S["xp_done"], n_of(p, r, 1, 1))
                    dve.scalar_tensor_tensor(out=X[:, t, :], in0=xp[:, :], scalar=UNSCALE, in1=X[:, t, :],
                                             op0=ALU.mult, op1=ALU.add).then_inc(S["x_acc"], 1)

                def tile(cur, old, out):
                    if old:
                        low(*old, 0)
                        low(*old, 1)
                    if cur:
                        scores_less_max(*cur, (0, 1))
                    if old:
                        low(*old, 2)
                        low(*old, 3)
                    if cur:
                        sums(*cur, (0, 1))
                        scores_less_max(*cur, (2, 3))
                    if old:
                        low_o(*old)
                    if out:
                        add_x(*out)
                    if cur:
                        sums(*cur, (2, 3))

                tile((0, 0), None, None)
                tile((0, 1), (0, 0), None)
                with dve.Fori(1, HALF) as p:
                    tile((p, 0), (p - 1, 1), (p - 1, 0, 2 * p - 2))
                    tile((p, 1), (p, 0), (p - 1, 1, 2 * p - 1))
                tile(None, (HALF - 1, 1), (HALF - 1, 0, TILES - 2))
                add_x(HALF - 1, 1, TILES - 1)


def ffn1(nc, sb, pb, sem, X, ident, rstd, nmr, ln, weight, bias, centroids, assignments, out):
    OMS = 4
    AHEAD = 2
    ADDS = 4
    with ExitStack() as ph:
        SW = sb(ph, "SW", [P, 4, DIM], F32)
        SC = sb(ph, "SC", [CLUSTERS, DIM], F32)
        WT = sb(ph, "WT", [P, 2, KC, DIM], F16)
        CTT = sb(ph, "CTT", [P, 2, KC, CLUSTERS], F16)
        BI = sb(ph, "BI", [P, DIM], F32)
        AS = sb(ph, "AS", [CLUSTERS, DIM], I32)
        OH = sb(ph, "OH", [CLUSTERS, DIM], F16)
        cid = sb(ph, "cid", [CLUSTERS, 1], F32)
        cidi = sb(ph, "cidi", [CLUSTERS, 1], I32)
        ones = sb(ph, "ones", [P, P], F16)
        XN = sb(ph, "XN2", [P, 2, DIM], F32)
        XT = sb(ph, "XT2", [P, 2, 2, KC, P], F16)
        DN = sb(ph, "DN", [P, TILES, DIM], F32)
        EX = sb(ph, "EX", [P, 2, CLUSTERS], F32)
        cs = sb(ph, "cs", [P, 2, 4], F32)
        HT = sb(ph, "HT", [P, 2, CLUSTERS], F32)
        HA = sb(ph, "HA", [P, CLUSTERS], F16)
        QS = sb(ph, "QS", [P, TILES], F32)
        CSEL = sb(ph, "CSEL", [CLUSTERS, P], F16)
        RSEL = sb(ph, "RSEL", [P, DIM], F32)
        OM = sb(ph, "OM", [P, OMS, DIM], F32)
        tp = [pb(ph, f"t2_{i}") for i in range(2)]
        dn = [pb(ph, f"dn{i}") for i in range(2)]
        lg = [pb(ph, f"lg{i}") for i in range(2)]
        rs = [pb(ph, f"rs{i}") for i in range(2)]
        names = ("w_ld c_ld b_ld a_ld ones_done cid_done oh_done ha_done xn_done tp_done tp_hi tp_lo dn_done lg_done dn_out "
                 "max_done nmax_done exp_done rcp_done hit_done any_done qs_done count_done csel_done row_done rsel_done om_done x_done x_done_v stored")
        S = {n: sem(ph, "f1_" + n) for n in names.split()}
        moments, scales, stats_scalar, stats_ready, parts_before = ln
        block = ph.enter_context(nc.Block())
        HALF = TILES // 2
        FIRST = 5
        LOGIT = UNSCALE / TEMPERATURE

        def w_bank(u):
            if u < 4:
                return tp[u % 2][:, :].rearrange("p (k t) -> p k t", k=KC)
            return tp[0][:, 0:KC * CLUSTERS].rearrange("p (k t) -> p k t", k=KC)

        def w_out(part, u):
            return WT[:, part, :, u * P:(u + 1) * P] if u < 4 else CTT[:, part, :, :]

        def x_bank(r):
            return tp[(FIRST + r) % 2][:, :].rearrange("p (k t) -> p k t", k=KC)

        def live(p):
            return not isinstance(p, int) or p < HALF

        @block.sync
        def _(sp):
            sp.dma_start(SW[:, :, :], weight.rearrange("(t p) k -> p t k", p=P)).then_inc(S["w_ld"], 16)
            sp.dma_start(SC[:, :], centroids).then_inc(S["c_ld"], 16)
            sp.dma_start(BI[:, :], bias.partition_broadcast(P)).then_inc(S["b_ld"], 16)
            sp.dma_start(AS[:, :], assignments.partition_broadcast(CLUSTERS)).then_inc(S["a_ld"], 16)
            for i in range(TILES):
                if i % ADDS == ADDS - 1:
                    sp.wait_ge(S["x_done_v"], i // ADDS + 1)
                else:
                    sp.wait_ge(S["x_done"], i - i // ADDS + 1)
                sp.dma_start(out[i * P:(i + 1) * P, :], X[:, i, :]).then_inc(S["stored"], 16)
            sp.wait_ge(S["stored"], 16 * TILES)

        @block.gpsimd
        def _(pool):
            pool.memset(ones[:, :], 1.0).then_inc(S["ones_done"], 1)
            pool.memset(HA[:, :], 0.0).then_inc(S["ones_done"], 1)
            pool.iota(cidi[:, :], pattern=[[0, 1]], base=0, channel_multiplier=1).then_inc(S["cid_done"], 1)
            pool.wait_ge(S["cid_done"], 1)
            pool.tensor_copy(cid[:, :], cidi[:, :]).then_inc(S["cid_done"], 1)

            for t in range(TILES):
                pool.wait_ge(stats_ready, parts_before(3) + t // 2 + 1)
                if t >= 2:
                    pool.wait_ge(S["tp_done"], FIRST + t - 1)
                pool.tensor_scalar(XN[:, t % 2, :], X[:, t, :], rstd[:, t:t + 1], nmr[:, t:t + 1],
                                   ALU.mult, ALU.add).then_inc(S["xn_done"], 1)
            for i in range(TILES):
                if i % ADDS != ADDS - 1:
                    pool.wait_ge(S["om_done"], i + 1)
                    pool.tensor_tensor(X[:, i, :], X[:, i, :], OM[:, i % OMS, :], ALU.add).then_inc(S["x_done"], 1)

        @block.tensor
        def _(pe):
            pe.wait_ge(S["w_ld"], 16)
            for u in range(4):
                if u >= 2:
                    pe.wait_ge(S["tp_lo"], u - 1)
                for k in range(KC):
                    last = pe.transpose(tp[u % 2][:, k * P:(k + 1) * P], SW[:, u, k * P:(k + 1) * P], ident[:, :])
                last.then_inc(S["tp_done"], 1)
            pe.wait_ge(S["c_ld"], 16)
            pe.wait_ge(S["tp_lo"], 3)
            for k in range(KC):
                last = pe.transpose(tp[0][:, k * CLUSTERS:(k + 1) * CLUSTERS], SC[:, k * P:(k + 1) * P],
                                    ident[0:CLUSTERS, 0:CLUSTERS])
            last.then_inc(S["tp_done"], 1)

            def transposes(p, r):
                pe.wait_ge(S["xn_done"], p * 2 + (r + 1))
                pe.wait_ge(S["tp_lo"], p * 2 + (FIRST + r - 1))
                for k in range(KC):
                    last = pe.transpose(tp[(FIRST + r) % 2][:, k * P:(k + 1) * P], XN[:, r, k * P:(k + 1) * P], ident[:, :])
                last.then_inc(S["tp_done"], 1)

            def products(p, r):
                pe.wait_ge(S["tp_lo"], p * 2 + (FIRST + r + 1))
                if not (isinstance(p, int) and p == 0):
                    pe.wait_ge(S["dn_out"], p * 2 + (r - 1))
                    pe.wait_ge(S["exp_done"], p * 2 + (r - 1))
                for n, (k, (a, b)) in enumerate([(k, ab) for k in range(KC) for ab in PASSES]):
                    last = pe.matmul(lg[r][:, 0:CLUSTERS], XT[:, r, a, k, :], CTT[:, b, k, :], start=n == 0, stop=n == 3 * KC - 1)
                last.then_inc(S["lg_done"], 1)
                for n, (k, (a, b)) in enumerate([(k, ab) for k in range(KC) for ab in PASSES]):
                    last = pe.matmul(dn[r][:, :], XT[:, r, a, k, :], WT[:, b, k, :], start=n == 0, stop=n == 3 * KC - 1)
                last.then_inc(S["dn_done"], 1)

            transposes(0, 0)
            transposes(0, 1)
            products(0, 0)
            transposes(1, 0)
            products(0, 1)
            transposes(1, 1)
            products(1, 0)
            with pe.Fori(2, HALF) as p:
                transposes(p, 0)
                products(p - 1, 1)
                transposes(p, 1)
                products(p, 0)
            products(HALF - 1, 1)
            pe.wait_ge(S["any_done"], TILES)
            pe.matmul(rs[0][0:CLUSTERS, 0:P], HA[:, :], ones[:, :], start=True, stop=True).then_inc(S["count_done"], 1)
            pe.wait_ge(S["csel_done"], 1)
            pe.wait_ge(S["oh_done"], 1)
            pe.matmul(rs[1][:, :], CSEL[:, :], OH[:, :], start=True, stop=True).then_inc(S["row_done"], 1)

        @block.scalar
        def _(act):
            for u in range(FIRST):
                act.wait_ge(S["tp_done"], u + 1)
                act.activation(w_out(0, u), w_bank(u), ACT.Copy, scale=WEIGHT_SCALE).then_inc(S["tp_hi"], 1)
            stats_scalar(act, 3, range(AHEAD))

            def high(p, r):
                act.wait_ge(S["tp_done"], p * 2 + (FIRST + r + 1))
                act.activation(XT[:, r, 0, :, :], x_bank(r), ACT.Copy).then_inc(S["tp_hi"], 1)

            def exps(p, r):
                act.wait_ge(S["nmax_done"], p * 2 + (r + 1))
                act.activation(EX[:, r, :], lg[r][:, 0:CLUSTERS], ACT.Exp, bias=cs[:, r, 1:2], scale=LOGIT,
                               accum_out=cs[:, r, 2:3]).then_inc(S["exp_done"], 1)

            high(0, 0)
            high(0, 1)
            exps(0, 0)
            def step(p):
                high(p, 0)
                exps(p - 1, 1)
                high(p, 1)
                exps(p, 0)
                if live(p + AHEAD):
                    stats_scalar(act, 3, (p + AHEAD,))

            stats_scalar(act, 3, (AHEAD,))
            with act.Fori(1, HALF - AHEAD) as p:
                step(p)
            for p in range(HALF - AHEAD, HALF):
                step(p)
            exps(HALF - 1, 1)

        @block.vector
        def _(dve):
            for u in range(FIRST):
                dve.wait_ge(S["tp_hi"], u + 1)
                dve.scalar_tensor_tensor(out=w_out(1, u), in0=w_bank(u), scalar=WEIGHT_SCALE, in1=w_out(0, u),
                                         op0=ALU.mult, op1=ALU.subtract).then_inc(S["tp_lo"], 1)
            for part in range(AHEAD):
                moments(dve, 3, part)
                scales(dve, 3, part)
            dve.wait_ge(S["ones_done"], 2)
            dve.wait_ge(S["b_ld"], 16)
            dve.wait_ge(S["a_ld"], 16)
            dve.wait_ge(S["cid_done"], 2)
            dve.tensor_scalar(OH[:, :], AS[:, :], cid[:, 0:1], None, ALU.is_equal).then_inc(S["oh_done"], 1)

            def low(p, r):
                dve.wait_ge(S["tp_hi"], p * 2 + (FIRST + r + 1))
                dve.tensor_tensor(XT[:, r, 1, :, :], x_bank(r), XT[:, r, 0, :, :], ALU.subtract).then_inc(S["tp_lo"], 1)

            def maxima(p, r):
                at = p * 2 + (r + 1)
                dve.wait_ge(S["lg_done"], at)
                dve.reduce_max(cs[:, r, 0:1], lg[r][:, 0:CLUSTERS], AX.X).then_inc(S["max_done"], 1)
                dve.wait_ge(S["max_done"], at)
                dve.tensor_scalar(cs[:, r, 1:2], cs[:, r, 0:1], -LOGIT, None, ALU.mult).then_inc(S["nmax_done"], 1)

            def dense_out(p, r):
                dve.wait_ge(S["dn_done"], p * 2 + (r + 1))
                dve.scalar_tensor_tensor(out=DN[:, 2 * p + r, :], in0=dn[r][:, :], scalar=UNSCALE, in1=BI[:, :],
                                         op0=ALU.mult, op1=ALU.add).then_inc(S["dn_out"], 1)

            def hits(p, r):
                at = p * 2 + (r + 1)
                dve.wait_ge(S["exp_done"], at)
                dve.reciprocal(cs[:, r, 3:4], cs[:, r, 2:3]).then_inc(S["rcp_done"], 1)
                dve.wait_ge(S["rcp_done"], at)
                dve.tensor_scalar(HT[:, r, :], EX[:, r, :], cs[:, r, 3:4], THRESHOLD, ALU.mult, ALU.is_gt).then_inc(S["hit_done"], 1)
                dve.wait_ge(S["hit_done"], at)
                dve.reduce_max(QS[:, bass.ds(2 * p + r, 1)], HT[:, r, :], AX.X).then_inc(S["qs_done"], 1)
                dve.tensor_tensor(HA[:, :], HA[:, :], HT[:, r, :], ALU.max).then_inc(S["any_done"], 1)

            def step(p):
                low(p, 0)
                maxima(p - 1, 1)
                hits(p - 1, 0)
                dense_out(p - 1, 0)
                if live(p + AHEAD):
                    moments(dve, 3, p + AHEAD)
                low(p, 1)
                maxima(p, 0)
                hits(p - 1, 1)
                dense_out(p - 1, 1)
                if live(p + AHEAD):
                    scales(dve, 3, p + AHEAD)

            low(0, 0)
            low(0, 1)
            moments(dve, 3, AHEAD)
            maxima(0, 0)
            scales(dve, 3, AHEAD)
            for p in range(1, HALF):
                step(p)
            p = HALF - 1
            maxima(p, 1)
            hits(p, 0)
            dense_out(p, 0)
            hits(p, 1)
            dense_out(p, 1)
            dve.wait_ge(S["count_done"], 1)
            dve.tensor_scalar(CSEL[:, :], rs[0][0:CLUSTERS, 0:P], 0.0, None, ALU.is_gt).then_inc(S["csel_done"], 1)
            dve.wait_ge(S["row_done"], 1)
            dve.tensor_scalar(RSEL[:, :], rs[1][:, :], 0.0, None, ALU.is_gt).then_inc(S["rsel_done"], 1)
            dve.wait_ge(S["rsel_done"], 1)
            dve.wait_ge(S["qs_done"], TILES)
            for i in range(TILES):
                if i >= OMS:
                    if (i - OMS) % ADDS == ADDS - 1:
                        dve.wait_ge(S["x_done_v"], (i - OMS) // ADDS + 1)
                    else:
                        dve.wait_ge(S["x_done"], i - OMS - (i - OMS) // ADDS + 1)
                dve.scalar_tensor_tensor(out=OM[:, i % OMS, :], in0=DN[:, i, :], scalar=QS[:, i:i + 1], in1=RSEL[:, :],
                                         op0=ALU.mult, op1=ALU.mult).then_inc(S["om_done"], 1)
                if i % ADDS == ADDS - 1:
                    dve.wait_ge(S["om_done"], i + 1)
                    dve.tensor_tensor(X[:, i, :], X[:, i, :], OM[:, i % OMS, :], ALU.add).then_inc(S["x_done_v"], 1)


_INS = ["x", "ctx_4096", "L0_xattn_wq", "L0_xattn_wk", "L0_xattn_wv", "L0_xattn_wo",
        "L0_ffn_W0", "L0_ffn_bias0", "L0_ffn_W1", "L0_ffn_bias1",
        "L1_xattn_Wq", "L1_xattn_Wk", "L1_xattn_Wv", "L1_xattn_Wo",
        "L1_ffn_weight", "L1_ffn_bias", "L1_ffn_centroids", "L1_ffn_assignments"]


def kernel(**inputs):
    import numpy as _np
    import concourse.bacc as _bacc
    from concourse import mybir as _mybir
    from concourse.bass_utils import run_bass_kernel_spmd as _run

    nc = _bacc.Bacc("TRN2", target_bir_lowering=False, num_devices=1)
    arrays, args = {}, []
    for name in _INS:
        a = _np.ascontiguousarray(inputs[name])
        if name in ("x", "ctx_4096"):
            a = a.reshape(TOKENS, DIM)
        arrays[f"in_{name}"] = a
        args.append(nc.dram_tensor(f"in_{name}", a.shape, _mybir.dt.from_np(a.dtype), kind="ExternalInput").ap())
    args.append(nc.dram_tensor("out_0", (TOKENS, DIM), _mybir.dt.float32, kind="ExternalOutput").ap())
    fused_decoder_kernel(nc, *args)
    r = _run(nc, [arrays], core_ids=[0])
    return r.results[0]["out_0"].reshape(BATCH, SEQ, DIM)
```

```python
import math

import concourse.bass as bass
from concourse import mybir
from contextlib import ExitStack

F32 = mybir.dt.float32
F16 = mybir.dt.float16
BF16 = mybir.dt.bfloat16
U32 = mybir.dt.uint32
I32 = mybir.dt.int32
ALU = mybir.AluOpType
ACT = mybir.ActivationFunctionType
AX = mybir.AxisListType

P = 128
BATCH, SEQ, DIM = 32, 64, 512
TOKENS = BATCH * SEQ
TILES = TOKENS // P
KC = DIM // P
BLOCK = 512
BLOCKS = TOKENS // BLOCK
BT = BLOCK // P
BB = BLOCK // SEQ
GROUPS, REP = 8, 4
HEAD0 = 128
HEAD1 = 16
INNER = 1792
IC = INNER // P
NQ = 448
CLUSTERS = 64
THRESHOLD, TEMPERATURE = 0.01, 0.1
EPS = 1e-5
FP8_MAX, AMAX_MIN = 448.0, 1e-4
WEIGHT_SCALE = 64.0
UNSCALE = 1.0 / WEIGHT_SCALE
PASSES = ((0, 0), (0, 1), (1, 0))


SCALE_STEPS = 16
SUBNORMAL = 1.5 * 2.0 ** -6
TO_GRID = 2.0 ** 20


def quant_scales(dve, amax, scale, rec_hi, rec_lo, tmp, step, base):
    u = lambda a: a.bitcast(U32)
    clamped, top, rest, rem, s_hi = (tmp[:, i] for i in range(5))
    stt = lambda o, a, c, b, op0, op1: dve.scalar_tensor_tensor(out=o, in0=a, scalar=c, in1=b, op0=op0, op1=op1)
    ops = (
        lambda: dve.tensor_scalar(clamped, amax, AMAX_MIN, None, ALU.max),
        lambda: dve.tensor_scalar(scale, clamped, 1.0 / FP8_MAX, None, ALU.mult),
        lambda: dve.tensor_scalar(u(top), u(scale), 0xFFFFF000, None, ALU.bitwise_and),
        lambda: dve.tensor_tensor(rest, scale, top, ALU.subtract),
        lambda: stt(rem, top, -FP8_MAX, clamped, ALU.mult, ALU.add),
        lambda: stt(rem, rest, -FP8_MAX, rem, ALU.mult, ALU.add),
        lambda: stt(scale, rem, 1.0 / FP8_MAX, scale, ALU.mult, ALU.add),
        lambda: dve.reciprocal(rest, scale),
        lambda: dve.tensor_scalar(u(rec_hi), u(rest), 0xFFFFFF00, None, ALU.bitwise_and),
        lambda: dve.tensor_scalar(u(s_hi), u(scale), 0xFFFF0000, None, ALU.bitwise_and),
        lambda: dve.tensor_tensor(top, s_hi, rec_hi, ALU.mult),
        lambda: dve.tensor_tensor(s_hi, scale, s_hi, ALU.subtract),
        lambda: dve.tensor_scalar(top, top, -1.0, 1.0, ALU.mult, ALU.add),
        lambda: dve.tensor_tensor(s_hi, s_hi, rec_hi, ALU.mult),
        lambda: dve.tensor_tensor(top, top, s_hi, ALU.subtract),
        lambda: dve.tensor_tensor(rec_lo, top, rest, ALU.mult),
    )
    assert len(ops) == SCALE_STEPS
    for n, op in enumerate(ops):
        if n:
            dve.wait_ge(step, base + n)
        op().then_inc(step, 1)


def round_to_grid(dve, V, M, sems, at):
    bits, m_done, done = sems
    dve.tensor_scalar(M.bitcast(U32), V.bitcast(U32), 0x7F800000, 0x00400000,
                      ALU.bitwise_and, ALU.bitwise_or).then_inc(bits, 1)
    dve.wait_ge(bits, at)
    dve.tensor_scalar(M, M, SUBNORMAL, TO_GRID, ALU.max, ALU.mult).then_inc(m_done, 1)
    dve.wait_ge(m_done, at)
    dve.tensor_tensor(V, V, M, ALU.add).then_inc(done, 1)


def to_grid(dve, V, M, src, rec_lo, chunks, sems, at):
    w_done, v_done = sems[:2]
    dve.wait_ge(w_done, at)
    for c in range(chunks):
        last = dve.scalar_tensor_tensor(out=V[:, c, :], in0=src[:, c, :], scalar=rec_lo(c), in1=V[:, c, :],
                                        op0=ALU.mult, op1=ALU.add)
    last.then_inc(v_done, 1)
    dve.wait_ge(v_done, at)
    round_to_grid(dve, V, M, sems[2:], at)


def fused_decoder_kernel(nc, x, ctx, wq0, wk0, wv0, wo0, w0, b0, w1, b1,
                         wq1, wk1, wv1, wo1, weight, bias, centroids, assignments, out):
    stack = ExitStack()
    with stack:
        def sb(where, name, shape, dt):
            return where.enter_context(nc.sbuf_tensor(name, shape, dt))

        def pb(where, name, shape=(P, 512)):
            return where.enter_context(nc.psum_tensor(name, list(shape), F32))

        def sem(where, name):
            return where.enter_context(nc.semaphore(name))

        X = sb(stack, "X", [P, TILES, DIM], F32)
        ident = sb(stack, "ident", [P, P], F32)
        CT = sb(stack, "CT", [P, 2, KC, TOKENS], F16)
        rstd = sb(stack, "rstd", [P, TILES], F32)
        nmr = sb(stack, "nmr", [P, TILES], F32)

        bn = sb(stack, "bn", [P, TILES, 6], F32)
        mv = sb(stack, "mv", [P, TILES, 2], F32)
        var_eps, root, guess, work = (sb(stack, n, [P, TILES], F32) for n in ("var_eps", "root", "guess", "ln_work"))
        stat, var_ready, root_ready, ln_step, stats_ready = (
            sem(stack, n) for n in ("stat", "var_ready", "root_ready", "ln_step", "stats_ready"))
        LN_STEPS = 6
        PARTS = {0: BLOCKS, 1: BLOCKS, 2: BLOCKS, 3: TILES // 2}

        def parts_before(use):
            return sum(PARTS[u] for u in range(use))

        def ln_part(use, part):
            per = TILES // PARTS[use]
            return per, bass.ds(part * per, per), part + parts_before(use)

        def ln_moments(dve, use, part):
            per, s, at = ln_part(use, part)
            for i in range(per):
                dve.bn_stats(bn[:, i, :], X[:, part * per + i, :]).then_inc(stat, 1)
            if not (isinstance(at, int) and at == 0):
                dve.wait_ge(stats_ready, at)
            for i in range(per):
                dve.wait_ge(stat, part * per + (use * TILES + i + 1))
                last = dve.bn_aggr(mv[:, i, :], bn[:, i, :])
            last.then_inc(ln_step, 1)
            dve.wait_ge(ln_step, at * LN_STEPS + 1)
            dve.tensor_scalar(var_eps[:, s], mv[:, 0:per, 1], EPS, None, ALU.add).then_inc(var_ready, 1)

        def ln_scales(dve, use, part):
            per, s, at = ln_part(use, part)
            dve.wait_ge(root_ready, at + 1)
            dve.reciprocal(guess[:, s], root[:, s]).then_inc(ln_step, 1)
            for n, op in enumerate((
                    lambda: dve.tensor_tensor(work[:, s], guess[:, s], guess[:, s], ALU.mult),
                    lambda: dve.tensor_tensor(work[:, s], work[:, s], var_eps[:, s], ALU.mult),
                    lambda: dve.tensor_scalar(work[:, s], work[:, s], -0.5, 1.5, ALU.mult, ALU.add),
                    lambda: dve.tensor_tensor(rstd[:, s], work[:, s], guess[:, s], ALU.mult))):
                dve.wait_ge(ln_step, at * LN_STEPS + (n + 2))
                op().then_inc(ln_step, 1)
            dve.wait_ge(ln_step, at * LN_STEPS + LN_STEPS)
            dve.scalar_tensor_tensor(out=nmr[:, s], in0=mv[:, 0:per, 0], scalar=-1.0, in1=rstd[:, s],
                                     op0=ALU.mult, op1=ALU.mult).then_inc(stats_ready, 1)

        def ln_stats_vector(dve, use, parts, loaded=None):
            for part in parts:
                if loaded is not None:
                    dve.wait_ge(loaded[part], 16)
                ln_moments(dve, use, part)
                ln_scales(dve, use, part)

        def ln_stats_scalar(act, use, parts):
            for part in parts:
                per, s, at = ln_part(use, part)
                act.wait_ge(var_ready, at + 1)
                act.activation(root[:, s], var_eps[:, s], ACT.Sqrt).then_inc(root_ready, 1)

        ln = (ln_stats_vector, ln_stats_scalar, stats_ready, parts_before)

        w0t_scope = stack.enter_context(ExitStack())
        ffn0_scope = stack.enter_context(ExitStack())
        W0T = sb(w0t_scope, "W0T", [P, 2, KC, INNER], F16)
        XB = sb(ffn0_scope, "XB", [P, TILES, KC, P], BF16)
        xa = sb(ffn0_scope, "xamax", [P, TILES, KC], F32)
        xs, xh, xl = (sb(ffn0_scope, "x" + n, [P, TILES, KC], F32) for n in ("scale", "rec_hi", "rec_lo"))
        xtmp = sb(ffn0_scope, "xtmp", [P, 5, BT, KC], F32)
        xb_done, xa_done, xstep, w0_ld = (sem(stack, n) for n in ("xb_done", "xa_done", "xstep", "w0_ld"))

        def norm_x(dve, part):
            dve.wait_ge(stats_ready, parts_before(1) + part + 1)
            for i in range(part * BT, (part + 1) * BT):
                dve.tensor_scalar(XB[:, i, :, :].rearrange("p c t -> p (c t)"), X[:, i, :], rstd[:, i:i + 1], nmr[:, i:i + 1],
                                  ALU.mult, ALU.add).then_inc(xb_done, 1)

        def amax_x(dve, part):
            for i in range(part * BT, (part + 1) * BT):
                dve.wait_ge(xb_done, i + 1)
                last = dve.tensor_reduce(xa[:, i, :], XB[:, i, :, :], AX.X, ALU.max, apply_absolute_value=True)
            last.then_inc(xa_done, 1)

        def scales_x(dve, part):
            dve.wait_ge(xa_done, part + 1)
            s = slice(part * BT, (part + 1) * BT)
            quant_scales(dve, xa[:, s, :], xs[:, s, :], xh[:, s, :], xl[:, s, :], xtmp, xstep, part * SCALE_STEPS)

        x_pieces = (lambda dve, part: ln_moments(dve, 1, part), lambda dve, part: ln_scales(dve, 1, part), norm_x, amax_x, scales_x)
        VW = sb(ffn0_scope, "VW", [P, 2, 8, P], F32)
        VX, MX, QX = VW[:, 0, 0:KC, :], VW[:, 0, KC:2 * KC, :], VW[:, 1, 0:KC, :]
        x_sems = {n: sem(stack, "f0_" + n) for n in "xw_done xv_done xbits xm_done xsum xq_done xqs_done".split()}

        def first_x_scalar(act):
            act.wait_ge(xstep, SCALE_STEPS)
            for k in range(KC):
                last = act.activation(VX[:, k, :], XB[:, 0, k, :], ACT.Copy, scale=xh[:, 0, k:k + 1])
            last.then_inc(x_sems["xw_done"], 1)

        def first_x_vector(dve):
            to_grid(dve, VX, MX, XB[:, 0, :, :], lambda c: xl[:, 0, c:c + 1], KC,
                    [x_sems[n] for n in ("xw_done", "xv_done", "xbits", "xm_done", "xsum")], 1)

        def first_x_pool(pool):
            pool.wait_ge(x_sems["xsum"], 1)
            pool.tensor_tensor(VX, VX, MX, ALU.subtract).then_inc(x_sems["xq_done"], 1)
            pool.wait_ge(x_sems["xq_done"], 1)
            pool.tensor_tensor(QX, VX, xs[:, 0, :].unsqueeze(2).to_broadcast([P, KC, P]), ALU.mult).then_inc(x_sems["xqs_done"], 1)

        first_x = (first_x_scalar, first_x_vector, first_x_pool)
        ahead_of_ffn0 = (W0T, XB, w0_ld, x_pieces, lambda act, part: ln_stats_scalar(act, 1, (part,)))

        NQH = REP * HEAD0

        def bits16(buffer):
            return buffer[:, :, :, :].rearrange("p a b c -> p (a b c)")

        def piece(memory, at, shape, dt):
            size = math.prod(shape) * mybir.dt.size(dt) // 2
            names = "abcd"[:len(shape)]
            flat = memory[:, at:at + size].bitcast(dt)
            return flat.rearrange(f"p ({' '.join(names)}) -> p {' '.join(names)}", **dict(zip(names, shape))), at + size

        xt_scope = stack.enter_context(ExitStack())
        SQ, at = piece(bits16(W0T), 0, (KC, NQH), F32)
        SKV, at = piece(bits16(W0T), at, (KC, 2, HEAD0), F32)
        SO, at = piece(bits16(W0T), at, (REP, DIM), F32)
        WS1, at = piece(bits16(W0T), at, (2, 2, DIM), F16)
        WQ = sb(xt_scope, "WQ", [P, 2, KC, NQH], F16)
        WKV = sb(xt_scope, "WKV", [P, 2, KC, 2, HEAD0], F16)
        weights0 = (SQ, SKV, SO, WQ, WKV, WS1)
        weight_sems0 = {n: sem(stack, "a0_" + n) for n in "sq_ld skv_ld so_ld qkv_hi qkv_lo".split()}

        def load_qkv(sp, g):
            sp.dma_start(SQ[:, :, :], wq0[:, bass.ds(g * NQH, NQH)].rearrange("(c p) n -> p c n", p=P)).then_inc(weight_sems0["sq_ld"], 16)
            for i, w in enumerate((wk0, wv0)):
                sp.dma_start(SKV[:, :, i, :], w[:, bass.ds(g * HEAD0, HEAD0)].rearrange("(c p) n -> p c n", p=P)).then_inc(weight_sems0["skv_ld"], 16)

        def load_o(sp, g):
            sp.dma_start(SO[:, :, :], wo0[bass.ds(g * NQH, NQH), :].rearrange("(j p) n -> p j n", p=P)).then_inc(weight_sems0["so_ld"], 16)

        def high_q(act, g):
            act.wait_ge(weight_sems0["sq_ld"], g * 16 + 16)
            act.activation(WQ[:, 0, :, :], SQ[:, :, :], ACT.Copy, scale=WEIGHT_SCALE).then_inc(weight_sems0["qkv_hi"], 1)

        def high_kv(act, g):
            act.wait_ge(weight_sems0["skv_ld"], g * 32 + 32)
            act.activation(WKV[:, 0, :, :, :], SKV[:, :, :, :], ACT.Copy, scale=WEIGHT_SCALE).then_inc(weight_sems0["qkv_hi"], 1)

        def low_q(dve, g):
            dve.wait_ge(weight_sems0["qkv_hi"], g * 2 + 1)
            dve.scalar_tensor_tensor(out=WQ[:, 1, :, :], in0=SQ[:, :, :], scalar=WEIGHT_SCALE, in1=WQ[:, 0, :, :],
                                     op0=ALU.mult, op1=ALU.subtract).then_inc(weight_sems0["qkv_lo"], 1)

        def low_kv(dve, g):
            dve.wait_ge(weight_sems0["qkv_hi"], g * 2 + 2)
            dve.scalar_tensor_tensor(out=WKV[:, 1, :, :, :], in0=SKV[:, :, :, :], scalar=WEIGHT_SCALE, in1=WKV[:, 0, :, :, :],
                                     op0=ALU.mult, op1=ALU.subtract).then_inc(weight_sems0["qkv_lo"], 1)

        SQ1, at = piece(bits16(W0T), 0, (KC, DIM), F32)
        SKV1, at = piece(bits16(W0T), at, (KC, 2, P), F32)
        SO1, at = piece(bits16(W0T), at, (REP, DIM), F32)
        ld1 = {n: sem(stack, "n1_" + n) for n in "sq_ld skv_ld so_ld".split()}

        SW, at = piece(bits16(W0T), 0, (4, DIM), F32)
        SC, at = piece(bits16(W0T), at, (DIM,), F32)
        BI, at = piece(bits16(W0T), at, (DIM,), F32)
        AS, at = piece(bits16(W0T), at, (DIM,), I32)
        SC, AS = SC[0:CLUSTERS, :], AS[0:CLUSTERS, :]
        ld2 = {n: sem(stack, "f1_" + n) for n in "w_ld c_ld b_ld a_ld".split()}

        def load_weights2(sp):
            sp.dma_start(SW[:, :, :], weight.rearrange("(t p) k -> p t k", p=P)).then_inc(ld2["w_ld"], 16)
            sp.dma_start(SC[:, :], centroids).then_inc(ld2["c_ld"], 16)
            sp.dma_start(BI[:, :], bias.partition_broadcast(P)).then_inc(ld2["b_ld"], 16)
            sp.dma_start(AS[:, :], assignments.partition_broadcast(CLUSTERS)).then_inc(ld2["a_ld"], 16)

        def load_weights1(sp):
            sp.dma_start(SQ1[:, :, :], wq1.rearrange("(c p) n -> p c n", p=P)).then_inc(ld1["sq_ld"], 16)
            for i, w in enumerate((wk1, wv1)):
                sp.dma_start(SKV1[:, :, i, :], w.rearrange("(c p) n -> p c n", p=P)).then_inc(ld1["skv_ld"], 16)
            for g in range(GROUPS):
                sp.dma_start(SO1[g * HEAD1:(g + 1) * HEAD1, :, :],
                             wo1[g * REP * HEAD1:(g + 1) * REP * HEAD1, :].rearrange("(j d) n -> d j n", d=HEAD1)).then_inc(ld1["so_ld"], 16)

        XT = sb(xt_scope, "XT", [P, 2, KC, TOKENS], F16)
        w0t = nc.dram_tensor("w0t", [P, 2 * KC * INNER], F16, kind="Internal").ap()
        w1t = nc.dram_tensor("w1t", [P, 2 * IC * DIM], F16, kind="Internal").ap()
        with ExitStack() as ph:
            CS = sb(ph, "CS", [P, TILES, DIM], F32)
            XN = sb(ph, "XN", [P, 2, DIM], F32)
            tp = [pb(ph, f"p0_tp{i}") for i in range(4)]
            x_ld = [sem(ph, f"x_ld{i}") for i in range(BLOCKS)]
            c_ld = [sem(ph, f"c_ld{i}") for i in range(BLOCKS)]
            ident_ready = sem(ph, "ident_ready")
            xn_ready = sem(ph, "xn_ready")
            tp_done = sem(ph, "p0_tp_done")
            hi_done = sem(ph, "p0_hi_done")
            lo_done = sem(ph, "p0_lo_done")
            UNITS = [(x_too, i * BT + j) for i in range(BLOCKS) for x_too in range(2) for j in range(BT)]
            block = ph.enter_context(nc.Block())

            @block.sync
            def _(sp):
                for i in range(BLOCKS):
                    rows = slice(i * BLOCK, (i + 1) * BLOCK)
                    sp.dma_start(CS[:, i * BT:(i + 1) * BT, :],
                                 ctx[rows, :].rearrange("(t p) d -> p t d", p=P)).then_inc(c_ld[i], 16)
                    sp.dma_start(X[:, i * BT:(i + 1) * BT, :],
                                 x[rows, :].rearrange("(t p) d -> p t d", p=P)).then_inc(x_ld[i], 16)
                    if i == 1:
                        load_qkv(sp, 0)
                load_o(sp, 0)

            @block.gpsimd
            def _(pool):
                pool.memset(ident[:, :], 0.0).then_inc(ident_ready, 1)
                pool.wait_ge(ident_ready, 1)
                pool.affine_select(out=ident[:, :], in_=ident[:, :], compare_op=ALU.not_equal, fill=1.0,
                                   base=0, pattern=[[-1, P]], channel_multiplier=1).then_inc(ident_ready, 1)
                for i in range(TILES):
                    pool.wait_ge(stats_ready, i // BT + 1)
                    if i >= 2:
                        pool.wait_ge(tp_done, UNITS.index((1, i - 2)) + 1)
                    pool.tensor_scalar(XN[:, i % 2, :], X[:, i, :], rstd[:, i:i + 1], nmr[:, i:i + 1],
                                       ALU.mult, ALU.add).then_inc(xn_ready, 1)

            @block.tensor
            def _(pe):
                pe.wait_ge(ident_ready, 2)
                for n, (x_too, i) in enumerate(UNITS):
                    if not x_too:
                        if i % BT == 0:
                            pe.wait_ge(c_ld[i // BT], 16)
                        src = CS[:, i, :]
                    else:
                        pe.wait_ge(xn_ready, i + 1)
                        src = XN[:, i % 2, :]
                    if n >= 4:
                        pe.wait_ge(lo_done, n - 3)
                    for k in range(KC):
                        last = pe.transpose(tp[n % 4][:, k * P:(k + 1) * P], src[:, k * P:(k + 1) * P], ident[:, :])
                    last.then_inc(tp_done, 1)

            def dst(n, part):
                x_too, i = UNITS[n]
                return (CT, XT)[x_too][:, part, :, i * P:(i + 1) * P]

            def bank(n):
                return tp[n % 4][:, :].rearrange("p (k t) -> p k t", k=KC)

            @block.scalar
            def _(act):
                for n in range(2 * TILES):
                    if n % (2 * BT) == 0:
                        ln_stats_scalar(act, 0, (n // (2 * BT),))
                    act.wait_ge(tp_done, n + 1)
                    act.activation(dst(n, 0), bank(n), ACT.Copy).then_inc(hi_done, 1)
                high_q(act, 0)
                high_kv(act, 0)

            @block.vector
            def _(dve):
                for n in range(2 * TILES):
                    if n % (2 * BT) == 0:
                        ln_stats_vector(dve, 0, (n // (2 * BT),), x_ld)
                    dve.wait_ge(hi_done, n + 1)
                    dve.tensor_tensor(dst(n, 1), bank(n), dst(n, 0), ALU.subtract).then_inc(lo_done, 1)
                low_q(dve, 0)
                low_kv(dve, 0)

        attention0(nc, sb, pb, sem, X, ident, XT, CT, w0, w1, w0t, w1t, ahead_of_ffn0,
                   weights0, weight_sems0, (load_qkv, load_o), (high_q, high_kv, low_q, low_kv), piece, bits16, VW, first_x)
        xt_scope.close()
        ffn0(nc, sb, pb, sem, X, ident, ahead_of_ffn0, (xs, xh, xl, xstep), (VX, MX, QX), x_sems, w1t, b0, b1,
             load_weights1, ln[:2])
        ffn0_scope.close()
        attention1(nc, sb, pb, sem, X, ident, CT, rstd, nmr, ln, (SQ1, SKV1, SO1), ld1, load_weights2)
        ffn1(nc, sb, pb, sem, X, ident, rstd, nmr, (ln_moments, ln_scales) + ln[1:], (SW, SC, BI, AS), ld2, out)


def attention0(nc, sb, pb, sem, X, ident, XT, CT, w0, w1, w0t_dram, w1t_dram, ahead_of_ffn0,
               weights, weight_sems, loads, splits, piece, bits16, VW, first_x):
    exp_scale = float(HEAD0) ** -0.5
    with ExitStack() as ph:
        W0T, XB, w0_ld, x_pieces, stats_x = ahead_of_ffn0
        SQ, SKV, SO, WQ, WKV, WS1 = weights
        load_qkv, load_o = loads
        high_q, high_kv, low_q, low_kv = splits
        WO = sb(ph, "WO", [P, 2, REP, DIM], F16)
        QT = sb(ph, "QT", [P, 2, BB, REP, SEQ], F16)
        KT = sb(ph, "KT", [P, 2, BB, SEQ], F16)
        V = sb(ph, "V", [P, 2, BT, 2, HEAD0], F16)
        E = sb(ph, "E", [P, 2, BB, SEQ], F32)
        ST = sb(ph, "ST", [P, 3, 2, BB], F32)
        PT = sb(ph, "PT", [P, 2, BT, REP * SEQ], F16)
        OT = sb(ph, "OT", [P, 2, REP, BLOCK], F16)
        words = bits16(XB)
        WB, at = piece(words, 0, (16, P), BF16)
        MW, at = piece(words, at, (8, P), F32)
        WS0, at = piece(words, at, (2, KC, 2 * P), F16)
        wa, ws, wh, wl = (sb(ph, "w" + n, [P, 16], F32) for n in ("amax", "scale", "rec_hi", "rec_lo"))
        wtmp = sb(ph, "wtmp", [P, 5, 16], F32)
        sc = [pb(ph, f"sc{i}") for i in range(2)]
        pj = [pb(ph, f"pj{i}") for i in range(2)]
        tv = [pb(ph, f"tv{i}") for i in range(2)]
        xp = [pb(ph, f"xp{i}") for i in range(2)]
        names = ("zeroed o_hi o_lo sc_done pj_done tp_done pv_done xp_done "
                 "exp_done pj_hi tp_hi ot_hi max_done sub_done sum_done rcp_done p_done pj_lo tp_lo ot_lo x_acc "
                 "wb_ld wa_done wstep ww_done wv_done wbits wm_done wsum wqs_done wq_done wt_done wt_hi wt_lo w_st")
        S = {n: sem(ph, "a0_" + n) for n in names.split()} | weight_sems
        block = ph.enter_context(nc.Block())
        SPG = BLOCKS
        PREP = ((1, 0, 8), (2, 8, 16))

        def prepared(t, last):
            return [] if last else [(n, lo, hi) for n, (at, lo, hi) in enumerate(PREP) if at == t]

        def n_of(g, t, per, c):
            return g * (SPG * per) + (t * per + c)

        @block.sync
        def _(sp):
            with sp.Fori(0, GROUPS - 1) as g:
                sp.dma_start(WB[:, 0:8, :].rearrange("p (t c) k -> p t (c k)", t=2),
                             w0[bass.ds(g * 256, 256), :].rearrange("(t p) k -> p t k", p=P)).then_inc(S["wb_ld"], 16)
                sp.dma_start(WB[:, 8:16, :].rearrange("p (t c) k -> p t (c k)", t=4),
                             w1[:, bass.ds(g * 256, 256)].rearrange("(t p) k -> p t k", p=P)).then_inc(S["wb_ld"], 16)
                sp.wait_ge(S["qkv_lo"], g * 2 + 2)
                load_qkv(sp, g + 1)
                sp.wait_ge(S["wt_lo"], g * 4 + 4)
                sp.dma_start(w0t_dram.rearrange("p (s c n) -> p s c n", s=2, c=KC)[:, :, :, bass.ds(g * 256, 256)],
                             WS0[:, :, :, :]).then_inc(S["w_st"], 16)
                sp.dma_start(w1t_dram.rearrange("p (s c n) -> p s c n", s=2, c=IC)[:, :, bass.ds(g * 2, 2), :],
                             WS1[:, :, :, :]).then_inc(S["w_st"], 16)
                sp.wait_ge(S["w_st"], g * 32 + 32)
                sp.wait_ge(S["o_lo"], g + 1)
                load_o(sp, g + 1)
            sp.wait_ge(S["qkv_lo"], 2 * GROUPS)
            sp.wait_ge(S["o_lo"], GROUPS)
            sp.dma_start(W0T[:, :, :, :], w0t_dram.rearrange("p (s c n) -> p s c n", s=2, c=KC)).then_inc(w0_ld, 16)

        @block.gpsimd
        def _(pool):
            pool.memset(V[:, :, :, :, :], 0.0).then_inc(S["zeroed"], 1)
            with pool.Fori(0, GROUPS - 1) as g:
                for n, (t, lo, hi) in enumerate(PREP):
                    v = VW[:, n, 0:hi - lo, :]
                    pool.wait_ge(S["wsum"], g * 2 + (n + 1))
                    pool.tensor_tensor(v, v, MW[:, 0:hi - lo, :], ALU.subtract).then_inc(S["wq_done"], 1)
                    pool.wait_ge(S["wq_done"], g * 2 + (n + 1))
                    pool.tensor_tensor(v, v, ws[:, lo:hi].unsqueeze(2).to_broadcast([P, hi - lo, P]), ALU.mult).then_inc(S["wqs_done"], 1)
            first_x[2](pool)

        @block.tensor
        def _(pe):
            def project(g, t, units):
                for u in units:
                    bank = pj[u % 2]
                    if u == 0:
                        pe.wait_ge(S["qkv_lo"], g * 2 + 2)
                    if not (isinstance(g, int) and g == 0 and t == 0 and u < 2):
                        pe.wait_ge(S["pj_lo"], n_of(g, t, 6, u - 1))
                    tokens = slice(t * BLOCK, (t + 1) * BLOCK)
                    if u < 5:
                        for n, (k, (a, b)) in enumerate([(k, ab) for ab in PASSES for k in range(KC)]):
                            w = WQ[:, a, k, u * HEAD0:(u + 1) * HEAD0] if u < 4 else WKV[:, a, k, 0, :]
                            src = XT if u < 4 else CT
                            last = pe.matmul(bank[:, :], w, src[:, b, k, tokens], start=n == 0, stop=n == 3 * KC - 1)
                    else:
                        for i in range(BT):
                            for n, (k, (a, b)) in enumerate([(k, ab) for ab in PASSES for k in range(KC)]):
                                own = slice(t * BLOCK + i * P, t * BLOCK + (i + 1) * P)
                                last = pe.matmul(bank[:, i * P:(i + 1) * P], CT[:, a, k, own], WKV[:, b, k, 1, :],
                                                 start=n == 0, stop=n == 3 * KC - 1)
                    last.then_inc(S["pj_done"], 1)

            def scores(g, t):
                pe.wait_ge(S["pj_lo"], n_of(g, t, 6, 5))
                for jp in range(2):
                    for b in range(BB):
                        for n, (qa, ka) in enumerate(PASSES):
                            last = pe.matmul(sc[jp][:, b * SEQ:(b + 1) * SEQ], QT[:, qa, b, 2 * jp:2 * jp + 2, :],
                                             KT[:, ka, b, :], start=n == 0, stop=n == 2)
                    last.then_inc(S["sc_done"], 1)

            def transpose_probs(g, t):
                pe.wait_ge(S["p_done"], n_of(g, t, 2, 2))
                for i in range(BT):
                    for jp in range(2):
                        at = (i % 2) * 256 + jp * P
                        last = pe.transpose(tv[i // 2][:, at:at + P],
                                            E[:, jp, 2 * i:2 * i + 2, :], ident[:, :])
                    if i % 2:
                        last.then_inc(S["tp_done"], 1)

            def weigh_values(g, t):
                pe.wait_ge(S["pj_lo"], n_of(g, t, 6, 6))
                for i in range(BT):
                    if i < 2:
                        pe.wait_ge(S["tp_lo"], n_of(g, t, 2, 2))
                    else:
                        pe.wait_ge(S["ot_lo"], n_of(g, t, 4, i - 1))
                    for h in range(2):
                        for n, (a, b) in enumerate(PASSES):
                            last = pe.matmul(tv[i % 2][:, h * 256:(h + 1) * 256], V[:, a, i, h, :], PT[:, b, i, :],
                                             start=n == 0, stop=n == 2)
                    last.then_inc(S["pv_done"], 1)

            def project_out(g, t):
                pe.wait_ge(S["o_lo"], g + 1)
                for i in range(BT):
                    pe.wait_ge(S["ot_lo"], n_of(g, t, 4, i + 1))
                    if i >= 2:
                        pe.wait_ge(S["x_acc"], n_of(g, t, 4, i - 1))
                    for n, (j, (a, b)) in enumerate([(j, ab) for j in range(REP) for ab in PASSES]):
                        last = pe.matmul(xp[i % 2][:, :], OT[:, a, j, i * P:(i + 1) * P], WO[:, b, j, :],
                                         start=n == 0, stop=n == 3 * REP - 1)
                    last.then_inc(S["xp_done"], 1)

            def transpose_weights(g, n, lo, hi):
                pe.wait_ge(S["wqs_done"], g * 2 + (n + 1))
                for u in range(lo // 4, hi // 4):
                    pe.wait_ge(S["x_acc"], n_of(g, PREP[n][0], 4, 3 + u - lo // 4))
                    for i in range(4):
                        slot = i if u < 2 else (i % 2) * 2 + i // 2
                        last = pe.transpose(xp[u - lo // 4][:, slot * P:(slot + 1) * P], VW[:, n, 4 * u + i - lo, :], ident[:, :])
                    last.then_inc(S["wt_done"], 1)

            def group(g, last):
                for t in range(SPG):
                    nxt = (g, t + 1) if t < SPG - 1 else (g + 1, 0)
                    more = not (last and t == SPG - 1)
                    scores(g, t)
                    if more:
                        project(*nxt, range(4))
                    transpose_probs(g, t)
                    split = prepared(t - 1, last)
                    for p in split:
                        transpose_weights(g, *p)
                    if more:
                        project(*nxt, (4,))
                    weigh_values(g, t)
                    if more:
                        project(*nxt, (5,))
                    for n, lo, hi in split:
                        pe.wait_ge(S["wt_lo"], g * 4 + hi // 4)
                    project_out(g, t)

            pe.sem_inc(S["xp_done"], 1)
            pe.wait_ge(S["zeroed"], 1)
            project(0, 0, range(6))
            with pe.Fori(0, GROUPS - 1) as g:
                group(g, False)
            group(GROUPS - 1, True)

        def q_bank(u):
            return pj[u % 2][:, :].rearrange("p (b t) -> p b t", b=BB)

        def v_bank(h):
            return pj[1][h * 64:(h + 1) * 64, :].rearrange("p (i d) -> p i d", i=BT)

        def o_bank(i):
            return tv[i % 2][:, :].rearrange("p (b j t) -> p b j t", b=2, j=REP)

        def o_out(part, i):
            return OT[:, part, :, i * P:(i + 1) * P].rearrange("p j (b t) -> p b j t", b=2)

        def w_bank(u, lo):
            return xp[u - lo // 4][:, :].rearrange("p (c n) -> p c n", c=4 if u < 2 else 2)

        def w_out(part, u):
            return WS0[:, part, :, u * P:(u + 1) * P] if u < 2 else WS1[:, part, :, (u - 2) * 256:(u - 1) * 256]

        @block.scalar
        def _(act):
            def weights_times_rec(g, n, lo, hi):
                act.wait_ge(S["wstep"], g * SCALE_STEPS + SCALE_STEPS)
                for c in range(lo, hi):
                    last = act.activation(VW[:, n, c - lo, :], WB[:, c, :], ACT.Copy, scale=wh[:, c:c + 1])
                last.then_inc(S["ww_done"], 1)

            def high_weights(g, n, lo, hi):
                for u in range(lo // 4, hi // 4):
                    act.wait_ge(S["wt_done"], g * 4 + (u + 1))
                    act.activation(w_out(0, u), w_bank(u, lo), ACT.Copy, scale=WEIGHT_SCALE).then_inc(S["wt_hi"], 1)

            def high(g, t, units):
                for u in units:
                    act.wait_ge(S["pj_done"], n_of(g, t, 6, u + 1))
                    if u < 4:
                        act.activation(QT[:, 0, :, u, :], q_bank(u), ACT.Copy, scale=UNSCALE).then_inc(S["pj_hi"], 1)
                    elif u == 4:
                        act.activation(KT[:, 0, :, :], q_bank(u), ACT.Copy, scale=UNSCALE).then_inc(S["pj_hi"], 1)
                    else:
                        act.activation(V[0:64, 0, :, 0, :], v_bank(0), ACT.Copy, scale=UNSCALE)
                        act.activation(V[64:128, 0, :, 1, :], v_bank(1), ACT.Copy, scale=UNSCALE).then_inc(S["pj_hi"], 1)

            def group(g, last):
                for t in range(SPG):
                    nxt = (g, t + 1) if t < SPG - 1 else (g + 1, 0)
                    more = not (last and t == SPG - 1)
                    for jp in range(2):
                        act.wait_ge(S["sub_done"], n_of(g, t, 2, jp + 1))
                        act.activation(E[:, jp, :, :], E[:, jp, :, :], ACT.Exp, scale=exp_scale).then_inc(S["exp_done"], 1)
                    if more:
                        high(*nxt, range(2))
                    for p in prepared(t, last):
                        weights_times_rec(g, *p)
                    if more:
                        high(*nxt, range(2, 4))
                    if last and t in (1, 2):
                        stats_x(act, t - 1)
                    for i in range(2):
                        act.wait_ge(S["tp_done"], n_of(g, t, 2, i + 1))
                        act.activation(PT[:, 0, 2 * i:2 * i + 2, :], tv[i][:, :].rearrange("p (i n) -> p i n", i=2),
                                       ACT.Copy).then_inc(S["tp_hi"], 1)
                    for p in prepared(t - 1, last):
                        high_weights(g, *p)
                    if t == SPG - 2 and not last:
                        high_q(act, g + 1)
                    if t == 0:
                        act.wait_ge(S["so_ld"], g * 16 + 16)
                        act.wait_ge(S["xp_done"], g * (SPG * 4) + 1)
                        act.activation(WO[:, 0, :, :], SO[:, :, :], ACT.Copy, scale=WEIGHT_SCALE).then_inc(S["o_hi"], 1)
                    if more:
                        high(*nxt, (4,))
                    for i in range(BT):
                        act.wait_ge(S["pv_done"], n_of(g, t, 4, i + 1))
                        act.activation(o_out(0, i), o_bank(i), ACT.Copy).then_inc(S["ot_hi"], 1)
                    if more:
                        high(*nxt, (5,))
                    if t == SPG - 2 and not last:
                        high_kv(act, g + 1)
                    if last and t == SPG - 1:
                        first_x[0](act)

            high(0, 0, range(5))
            act.wait_ge(S["zeroed"], 1)
            high(0, 0, (5,))
            with act.Fori(0, GROUPS - 1) as g:
                group(g, False)
            group(GROUPS - 1, True)

        @block.vector
        def _(dve):
            def low(g, t, u):
                dve.wait_ge(S["pj_hi"], n_of(g, t, 6, u + 1))
                if u < 5:
                    to = (QT[:, 1, :, u, :], QT[:, 0, :, u, :]) if u < 4 else (KT[:, 1, :, :], KT[:, 0, :, :])
                    dve.scalar_tensor_tensor(out=to[0], in0=q_bank(u), scalar=UNSCALE, in1=to[1],
                                             op0=ALU.mult, op1=ALU.subtract).then_inc(S["pj_lo"], 1)
                else:
                    for h in range(2):
                        rows = slice(h * 64, (h + 1) * 64)
                        last = dve.scalar_tensor_tensor(out=V[rows, 1, :, h, :], in0=v_bank(h), scalar=UNSCALE,
                                                        in1=V[rows, 0, :, h, :], op0=ALU.mult, op1=ALU.subtract)
                    last.then_inc(S["pj_lo"], 1)

            def scale_weights(g):
                dve.wait_ge(S["wb_ld"], g * 32 + 32)
                dve.tensor_reduce(wa[:, :], WB[:, :, :], AX.X, ALU.max, apply_absolute_value=True).then_inc(S["wa_done"], 1)
                dve.wait_ge(S["wa_done"], g + 1)
                quant_scales(dve, wa[:, :], ws[:, :], wh[:, :], wl[:, :], wtmp, S["wstep"], g * SCALE_STEPS)

            def weights_add_rest(g, n, lo, hi):
                dve.wait_ge(S["ww_done"], g * 2 + (n + 1))
                for c in range(hi - lo):
                    last = dve.scalar_tensor_tensor(out=VW[:, n, c, :], in0=WB[:, lo + c, :], scalar=wl[:, lo + c:lo + c + 1],
                                                    in1=VW[:, n, c, :], op0=ALU.mult, op1=ALU.add)
                last.then_inc(S["wv_done"], 1)

            def weights_to_grid(g, n, lo, hi):
                dve.wait_ge(S["wv_done"], g * 2 + (n + 1))
                round_to_grid(dve, VW[:, n, 0:hi - lo, :], MW[:, 0:hi - lo, :],
                              [S[x] for x in ("wbits", "wm_done", "wsum")], g * 2 + (n + 1))

            def low_weights(g, n, lo, hi):
                for u in range(lo // 4, hi // 4):
                    dve.wait_ge(S["wt_hi"], g * 4 + (u + 1))
                    dve.scalar_tensor_tensor(out=w_out(1, u), in0=w_bank(u, lo), scalar=WEIGHT_SCALE, in1=w_out(0, u),
                                             op0=ALU.mult, op1=ALU.subtract).then_inc(S["wt_lo"], 1)

            def scores_less_max(g, t, jp):
                s3 = sc[jp][:, :].rearrange("p (b k) -> p b k", b=BB)
                dve.wait_ge(S["sc_done"], n_of(g, t, 2, jp + 1))
                dve.reduce_max(ST[:, 0, jp, :], s3, AX.X).then_inc(S["max_done"], 1)
                dve.wait_ge(S["max_done"], n_of(g, t, 2, jp + 1))
                dve.tensor_tensor(E[:, jp, :, :], s3, ST[:, 0, jp, :].unsqueeze(2).to_broadcast([P, BB, SEQ]),
                                  ALU.subtract).then_inc(S["sub_done"], 1)

            def normalise(g, t, jp):
                at = n_of(g, t, 2, jp + 1)
                dve.wait_ge(S["exp_done"], at)
                dve.reduce_sum(ST[:, 1, jp, :], E[:, jp, :, :], AX.X).then_inc(S["sum_done"], 1)
                dve.wait_ge(S["sum_done"], at)
                dve.reciprocal(ST[:, 2, jp, :], ST[:, 1, jp, :]).then_inc(S["rcp_done"], 1)
                dve.wait_ge(S["rcp_done"], at)
                dve.tensor_tensor(E[:, jp, :, :], E[:, jp, :, :], ST[:, 2, jp, :].unsqueeze(2).to_broadcast([P, BB, SEQ]),
                                  ALU.mult).then_inc(S["p_done"], 1)

            def group(g, last):
                for t in range(SPG):
                    nxt = (g, t + 1) if t < SPG - 1 else (g + 1, 0)
                    more = not (last and t == SPG - 1)

                    def x_ahead(n):
                        if last and t in (1, 2):
                            x_pieces[n](dve, t - 1)

                    scores_less_max(g, t, 0)
                    scores_less_max(g, t, 1)
                    if more:
                        low(*nxt, 0)
                    normalise(g, t, 0)
                    if more:
                        low(*nxt, 1)
                    normalise(g, t, 1)
                    if more:
                        low(*nxt, 2)
                    x_ahead(0)
                    if more:
                        low(*nxt, 3)
                    x_ahead(1)
                    for i in range(2):
                        dve.wait_ge(S["tp_hi"], n_of(g, t, 2, i + 1))
                        dve.tensor_tensor(PT[:, 1, 2 * i:2 * i + 2, :], tv[i][:, :].rearrange("p (i n) -> p i n", i=2),
                                          PT[:, 0, 2 * i:2 * i + 2, :], ALU.subtract).then_inc(S["tp_lo"], 1)
                    for p in prepared(t - 1, last):
                        low_weights(g, *p)
                    if more:
                        low(*nxt, 4)
                    x_ahead(2)
                    for i in range(BT):
                        dve.wait_ge(S["ot_hi"], n_of(g, t, 4, i + 1))
                        dve.tensor_tensor(o_out(1, i), o_bank(i), o_out(0, i), ALU.subtract).then_inc(S["ot_lo"], 1)
                    if t == 0:
                        dve.wait_ge(S["o_hi"], g + 1)
                        dve.scalar_tensor_tensor(out=WO[:, 1, :, :], in0=SO[:, :, :], scalar=WEIGHT_SCALE, in1=WO[:, 0, :, :],
                                                 op0=ALU.mult, op1=ALU.subtract).then_inc(S["o_lo"], 1)
                    if t == SPG - 2 and not last:
                        low_q(dve, g + 1)
                    for p in prepared(t, last):
                        weights_add_rest(g, *p)
                    x_ahead(3)
                    if more:
                        low(*nxt, 5)
                    for p in prepared(t, last):
                        weights_to_grid(g, *p)
                    for i in range(BT):
                        if t == 0 and i == 2 and not last:
                            scale_weights(g)
                        dve.wait_ge(S["xp_done"], n_of(g, t, 4, i + 2))
                        xt = X[:, t * BT + i, :]
                        dve.scalar_tensor_tensor(out=xt, in0=xp[i % 2][:, :], scalar=UNSCALE, in1=xt,
                                                 op0=ALU.mult, op1=ALU.add).then_inc(S["x_acc"], 1)
                        if i == 0:
                            x_ahead(4)
                            if last and t == SPG - 1:
                                first_x[1](dve)
                        if i == 1 and t == SPG - 2 and not last:
                            low_kv(dve, g + 1)

            for u in range(6):
                low(0, 0, u)
            with dve.Fori(0, GROUPS - 1) as g:
                group(g, False)
            group(GROUPS - 1, True)


def ffn0(nc, sb, pb, sem, X, ident, ahead_of_ffn0, x_scales, x_buffers, x_sems, w1t_dram, b0, b1,
         load_weights1, ln_stats):
    with ExitStack() as ph:
        W0T, XB, w0_ld, x_pieces, stats_x = ahead_of_ffn0
        xs, xh, xl, xstep = x_scales
        stats_vector, stats_scalar = ln_stats
        W1T = sb(ph, "W1T", [P, 2, IC, DIM], F16)
        B0, B1 = sb(ph, "B0", [1, INNER], BF16), sb(ph, "B1", [1, DIM], BF16)
        B0S, B1S = sb(ph, "B0S", [1, INNER], BF16), sb(ph, "B1S", [1, DIM], BF16)
        ones = sb(ph, "ones0", [1, P], BF16)
        VX, MX, QX = x_buffers
        XD = sb(ph, "XD", [P, 2, 2, KC, P], F16)
        DB = sb(ph, "DB", [P, 2, IC, P], BF16)
        da = sb(ph, "damax", [P, IC], F32)
        ds_, dh, dl = (sb(ph, "d" + n, [P, 2, IC], F32) for n in ("scale", "rec_hi", "rec_lo"))
        dtmp = sb(ph, "dtmp", [P, 5, IC], F32)
        VD = sb(ph, "VD", [P, 2, IC, P], F32)
        MD = sb(ph, "MD", [P, IC, P], F32)
        QD = sb(ph, "QD", [P, IC, P], F32)
        DT = sb(ph, "DT", [P, 2, IC, P], F16)
        EB = sb(ph, "EB", [P, 2, DIM], BF16)
        db = [pb(ph, f"db{i}") for i in range(4)]
        et = [pb(ph, f"et{i}") for i in range(2)]
        xt = pb(ph, "xt")
        eb = pb(ph, "eb")
        names = ("w1_ld b_ld "
                 "xt_done xt_hi xt_lo d_done ones_done bias_ready gelu_done da_done dstep dw_done dv_done dbits dm_done dsum "
                 "dq_done dqs_done et_done et_hi et_lo e_done eb_done x_done")
        S = {n: sem(ph, "f0_" + n) for n in names.split()} | x_sems
        block = ph.enter_context(nc.Block())
        X2_STEPS, X3_STEPS = (0, 0, 1, 1, 1), (2, 3, 3, 4, 5)
        STATS_STEPS = {TILES: (0, 1), TILES + 1: (2,)}
        THIRDS = [(0, 4), (4, 8), (8, 14)]
        GROUP_OF = [(0, 4), (4, 8), (8, 12), (12, 14)]

        def ahead(tile, by):
            return tile[0], tile[1] + by

        def fixed(tile):
            return 2 * tile[0] + tile[1] if isinstance(tile[0], int) else None

        def live(tile):
            return fixed(tile) is None or 0 <= fixed(tile) < TILES

        def nr(tile):
            return 2 * tile[0] + tile[1]

        def count(tile, per, c):
            return tile[0] * (2 * per) + (tile[1] * per + c)

        def steps(engine, step):
            for i in range(-1, 6):
                step((0, i))
            with engine.Fori(3, TILES // 2 - 1) as p:
                step((p, 0))
                step((p, 1))
            for i in range(TILES - 2, TILES + 3):
                step((0, i))

        @block.sync
        def _(sp):
            sp.dma_start(B0[:, :], b0.partition_broadcast(1)).then_inc(S["b_ld"], 16)
            sp.dma_start(B1[:, :], b1.partition_broadcast(1)).then_inc(S["b_ld"], 16)
            sp.dma_start(W1T[:, :, :, :], w1t_dram.rearrange("p (s c n) -> p s c n", s=2, c=IC)).then_inc(S["w1_ld"], 16)
            sp.wait_ge(S["d_done"], 4 * TILES)
            load_weights1(sp)

        @block.tensor
        def _(pe):
            def first_product(i, qs):
                for q in qs:
                    if q == 0:
                        pe.wait_ge(S["xt_lo"], count(i, 1, 1))
                    if live(ahead(i, -1)):
                        pe.wait_ge(S["gelu_done"], count(i, 4, q - 3))
                    pe.matmul(db[q][:, 0:NQ], ones[:, :], B0S[:, q * NQ:(q + 1) * NQ], start=True, stop=False)
                    for n, (k, (a, b)) in enumerate([(k, ab) for ab in PASSES for k in range(KC)]):
                        last = pe.matmul(db[q][:, 0:NQ], XD[:, i[1] % 2, a, k, :], W0T[:, b, k, q * NQ:(q + 1) * NQ],
                                         start=False, stop=n == 3 * KC - 1)
                    last.then_inc(S["d_done"], 1)

            def transpose_x(i):
                pe.wait_ge(S["xqs_done"], count(i, 1, 1))
                for k in range(KC):
                    last = pe.transpose(xt[:, k * P:(k + 1) * P], QX[:, k, :], ident[:, :])
                last.then_inc(S["xt_done"], 1)

            def transpose_hidden(i, n):
                if n < 3:
                    pe.wait_ge(S["dqs_done"], count(i, 3, n + 1))
                if n >= 2 or live(ahead(i, -1)):
                    pe.wait_ge(S["et_lo"], count(i, 4, n - 1))
                for c in range(*GROUP_OF[n]):
                    last = pe.transpose(et[n % 2][:, (c % 4) * P:(c % 4 + 1) * P], QD[:, c, :], ident[:, :])
                last.then_inc(S["et_done"], 1)

            def second_product(i):
                if live(ahead(i, -1)):
                    pe.wait_ge(S["eb_done"], count(i, 1, 0))
                pe.matmul(eb[:, :], ones[:, :], B1S[:, :], start=True, stop=False)
                for n in range(4):
                    pe.wait_ge(S["et_lo"], count(i, 4, n + 1))
                    for c in range(*GROUP_OF[n]):
                        for a, b in PASSES:
                            last = pe.matmul(eb[:, :], DT[:, a, c, :], W1T[:, b, c, :],
                                             start=False, stop=c == IC - 1 and (a, b) == PASSES[-1])
                    if n == 0:
                        transpose_hidden(i, 3)
                last.then_inc(S["e_done"], 1)

            def step(i):
                old, nxt = ahead(i, -2), ahead(i, 1)
                if live(old):
                    transpose_hidden(old, 0)
                    transpose_hidden(old, 1)
                if fixed(i) == 0:
                    pe.wait_ge(w0_ld, 16)
                    pe.wait_ge(S["ones_done"], 1)
                    pe.wait_ge(S["bias_ready"], 2)
                if live(i):
                    first_product(i, (0, 1, 2))
                if live(old):
                    transpose_hidden(old, 2)
                if live(nxt):
                    transpose_x(nxt)
                if live(i):
                    first_product(i, (3,))
                if live(old):
                    if fixed(i) == 2:
                        pe.wait_ge(S["w1_ld"], 16)
                    second_product(old)

            steps(pe, step)

        def et_bank(n):
            a, b = GROUP_OF[n]
            return et[n % 2][:, 0:(b - a) * P].rearrange("p (c t) -> p c t", c=b - a)

        @block.scalar
        def _(act):
            def x_times_rec(i):
                if live(ahead(i, -1)):
                    act.wait_ge(S["xqs_done"], count(i, 1, 0))
                if fixed(i) in range(0, TILES, BT):
                    act.wait_ge(xstep, (fixed(i) // BT + 1) * SCALE_STEPS)
                for k in range(KC):
                    last = act.activation(VX[:, k, :], XB[:, nr(i), k, :], ACT.Copy, scale=xh[:, nr(i), k:k + 1])
                last.then_inc(S["xw_done"], 1)

            def d_times_rec(i):
                r = i[1] % 2
                act.wait_ge(S["dstep"], count(i, SCALE_STEPS, SCALE_STEPS))
                if live(ahead(i, -2)):
                    act.wait_ge(S["dqs_done"], count(i, 3, -3))
                for c in range(IC):
                    last = act.activation(VD[:, r, c, :], DB[:, r, c, :], ACT.Copy, scale=dh[:, r, c:c + 1])
                last.then_inc(S["dw_done"], 1)

            def gelu(i, qs):
                for q in qs:
                    act.wait_ge(S["d_done"], count(i, 4, q + 1))
                    act.activation(DB[:, i[1] % 2, :, :].rearrange("p c t -> p (c t)")[:, q * NQ:(q + 1) * NQ],
                                   db[q][:, 0:NQ], ACT.Gelu, scale=UNSCALE).then_inc(S["gelu_done"], 1)

            def out_e(i):
                act.wait_ge(S["e_done"], count(i, 1, 1))
                act.activation(EB[:, i[1] % 2, :], eb[:, :], ACT.Copy, scale=UNSCALE).then_inc(S["eb_done"], 1)

            def high_x(i):
                act.wait_ge(S["xt_done"], count(i, 1, 1))
                act.activation(XD[:, i[1] % 2, 0, :, :], xt[:, :].rearrange("p (k t) -> p k t", k=KC), ACT.Copy).then_inc(S["xt_hi"], 1)

            def high_e(i, ns):
                for n in ns:
                    a, b = GROUP_OF[n]
                    act.wait_ge(S["et_done"], count(i, 4, n + 1))
                    act.activation(DT[:, 0, a:b, :], et_bank(n), ACT.Copy).then_inc(S["et_hi"], 1)

            def step(i):
                older, old, hidden, nxt, after = (ahead(i, by) for by in (-3, -2, -1, 1, 2))
                if live(older):
                    out_e(older)
                if live(old):
                    high_e(old, (0, 1))
                if live(hidden):
                    d_times_rec(hidden)
                if live(i):
                    gelu(i, (0, 1))
                if live(old):
                    high_e(old, (2,))
                if live(nxt):
                    high_x(nxt)
                if live(after):
                    x_times_rec(after)
                if live(i):
                    gelu(i, (2, 3))
                if live(old):
                    high_e(old, (3,))
                if fixed(i) == X2_STEPS[1]:
                    stats_x(act, 2)
                if fixed(i) == X3_STEPS[1]:
                    stats_x(act, 3)
                if fixed(i) in STATS_STEPS:
                    stats_scalar(act, 2, STATS_STEPS[fixed(i)])

            steps(act, step)

        @block.vector
        def _(dve):
            def quant_x(i):
                to_grid(dve, VX[:, :, :], MX[:, :, :], XB[:, nr(i), :, :], lambda c: xl[:, nr(i), c:c + 1], KC,
                        [S[n] for n in ("xw_done", "xv_done", "xbits", "xm_done", "xsum")], count(i, 1, 1))

            def scales_d(i):
                r = i[1] % 2
                dve.wait_ge(S["gelu_done"], count(i, 4, 4))
                dve.tensor_reduce(da[:, :], DB[:, r, :, :], AX.X, ALU.max, apply_absolute_value=True).then_inc(S["da_done"], 1)
                dve.wait_ge(S["da_done"], count(i, 1, 1))
                quant_scales(dve, da[:, :], ds_[:, r, :], dh[:, r, :], dl[:, r, :], dtmp, S["dstep"], count(i, SCALE_STEPS, 0))

            def add_rest(i):
                r = i[1] % 2
                dve.wait_ge(S["dw_done"], count(i, 1, 1))
                for c in range(IC):
                    last = dve.scalar_tensor_tensor(out=VD[:, r, c, :], in0=DB[:, r, c, :], scalar=dl[:, r, c:c + 1],
                                                    in1=VD[:, r, c, :], op0=ALU.mult, op1=ALU.add)
                last.then_inc(S["dv_done"], 1)

            def grid_d(i):
                V = VD[:, i[1] % 2, :, :]
                if live(ahead(i, -1)):
                    dve.wait_ge(S["dq_done"], count(i, 3, 0))
                dve.wait_ge(S["dv_done"], count(i, 1, 1))
                round_to_grid(dve, V, MD[:, :, :], [S[n] for n in ("dbits", "dm_done", "dsum")], count(i, 1, 1))

            def low_x(i):
                dve.wait_ge(S["xt_hi"], count(i, 1, 1))
                dve.tensor_tensor(XD[:, i[1] % 2, 1, :, :], xt[:, :].rearrange("p (k t) -> p k t", k=KC), XD[:, i[1] % 2, 0, :, :],
                                  ALU.subtract).then_inc(S["xt_lo"], 1)

            def low_e(i, ns):
                for n in ns:
                    a, b = GROUP_OF[n]
                    dve.wait_ge(S["et_hi"], count(i, 4, n + 1))
                    dve.tensor_tensor(DT[:, 1, a:b, :], et_bank(n), DT[:, 0, a:b, :], ALU.subtract).then_inc(S["et_lo"], 1)

            def step(i):
                old, hidden, nxt, after = (ahead(i, by) for by in (-2, -1, 1, 2))
                if live(old):
                    low_e(old, (0, 1))
                if live(hidden):
                    add_rest(hidden)
                if live(old):
                    low_e(old, (2,))
                if live(hidden):
                    grid_d(hidden)
                if live(nxt):
                    low_x(nxt)
                if live(after):
                    quant_x(after)
                if live(old):
                    low_e(old, (3,))
                if live(i):
                    scales_d(i)
                for n, piece in enumerate(x_pieces):
                    if fixed(i) == X2_STEPS[n]:
                        piece(dve, 2)
                    if fixed(i) == X3_STEPS[n]:
                        piece(dve, 3)
                for part in STATS_STEPS.get(fixed(i), ()):
                    dve.wait_ge(S["x_done"], (part + 1) * BT)
                    stats_vector(dve, 2, (part,))

            dve.wait_ge(S["b_ld"], 32)
            for scaled, bias in ((B0S, B0), (B1S, B1)):
                dve.tensor_scalar(scaled[:, :], bias[:, :], WEIGHT_SCALE, None, ALU.mult).then_inc(S["bias_ready"], 1)
            steps(dve, step)

        @block.gpsimd
        def _(pool):
            def quant_x(i):
                V, M = VX[:, :, :], MX[:, :, :]
                pool.wait_ge(S["xsum"], count(i, 1, 1))
                pool.tensor_tensor(V, V, M, ALU.subtract).then_inc(S["xq_done"], 1)
                if live(ahead(i, -1)):
                    pool.wait_ge(S["xt_lo"], count(i, 1, 0))
                pool.wait_ge(S["xq_done"], count(i, 1, 1))
                pool.tensor_tensor(QX[:, :, :], V, xs[:, nr(i), :].unsqueeze(2).to_broadcast([P, KC, P]),
                                   ALU.mult).then_inc(S["xqs_done"], 1)

            def quant_d(i):
                r = i[1] % 2
                pool.wait_ge(S["dsum"], count(i, 1, 1))
                for n, (a, b) in enumerate(THIRDS):
                    pool.tensor_tensor(VD[:, r, a:b, :], VD[:, r, a:b, :], MD[:, a:b, :], ALU.subtract).then_inc(S["dq_done"], 1)
                    if n == 0 and live(ahead(i, -1)):
                        pool.wait_ge(S["et_done"], count(i, 4, 0))
                    pool.wait_ge(S["dq_done"], count(i, 3, n + 1))
                    pool.tensor_tensor(QD[:, a:b, :], VD[:, r, a:b, :],
                                       ds_[:, r, a:b].unsqueeze(2).to_broadcast([P, b - a, P]), ALU.mult).then_inc(S["dqs_done"], 1)

            def add_x(i):
                pool.wait_ge(S["eb_done"], count(i, 1, 1))
                pool.tensor_tensor(X[:, nr(i), :], X[:, nr(i), :], EB[:, i[1] % 2, :], ALU.add).then_inc(S["x_done"], 1)

            def step(i):
                older, hidden, nxt = (ahead(i, by) for by in (-3, -1, 1))
                if live(nxt) and fixed(nxt) != 0:
                    quant_x(nxt)
                if live(older):
                    add_x(older)
                if live(hidden):
                    quant_d(hidden)

            pool.memset(ones[:, :], 1.0).then_inc(S["ones_done"], 1)
            steps(pool, step)


def attention1(nc, sb, pb, sem, X, ident, CT, rstd, nmr, ln, staged, loaded, load_weights2):
    exp_scale = float(HEAD1) ** -0.5
    HALF = TILES // 2
    with ExitStack() as ph:
        QT = sb(ph, "QT1", [P, 2, BATCH, REP, SEQ], F16)
        KT = sb(ph, "KT1", [P, 2, TOKENS], F16)
        V = sb(ph, "V1", [P, 2, TILES, P], F16)
        WO = sb(ph, "WO1", [P, 2, REP, DIM], F16)
        mask = sb(ph, "mask", [P, GROUPS], F16)
        KM = sb(ph, "KM", [P, 2, 2, GROUPS, 2, SEQ], F16)
        km_done = sem(ph, "km_done")

        def block_keys(pool, r, t):
            for s in range(2):
                pool.tensor_tensor(KM[:, r, s, :, :, :].rearrange("p g b k -> p g (b k)"),
                                   KT[:, s, bass.ds(t * P, P)].unsqueeze(1).to_broadcast([P, GROUPS, P]),
                                   mask[:, :].unsqueeze(2).to_broadcast([P, GROUPS, P]), ALU.mult).then_inc(km_done, 1)

        with ExitStack() as part:
            WQ = sb(part, "WQ1", [P, 2, KC, REP, GROUPS, HEAD1], F16)
            WKV = sb(part, "WKV1", [P, 2, KC, 2, P], F16)
            XT = sb(part, "XT1", [P, 2, KC, TOKENS], F16)
            SQ, SKV, SO = staged
            XN = sb(part, "XN1", [P, 2, DIM], F32)
            tp = [pb(part, f"n1_tp{i}") for i in range(2)]
            pj = [pb(part, f"n1_pj{i}") for i in range(2)]
            names = ("mask_done qkv_hi qkv_lo xn_done tp_done tp_hi tp_lo pj_done pj_hi pj_lo")
            S = {n: sem(part, "n1_" + n) for n in names.split()} | loaded
            stats_vector, stats_scalar, stats_ready, parts_before = ln
            block = part.enter_context(nc.Block())

            @block.gpsimd
            def _(pool):
                pool.memset(mask[:, :], 1.0).then_inc(S["mask_done"], 1)
                for n, (step, base, cm) in enumerate(((-HEAD1, 0, 1), (HEAD1, HEAD1 - 1, -1))):
                    pool.wait_ge(S["mask_done"], n + 1)
                    pool.affine_select(out=mask[:, :], in_=mask[:, :], compare_op=ALU.is_ge, fill=0.0, base=base,
                                       pattern=[[step, GROUPS]], channel_multiplier=cm).then_inc(S["mask_done"], 1)
                for t in range(TILES):
                    pool.wait_ge(stats_ready, parts_before(2) + t // BT + 1)
                    if t >= 2:
                        pool.wait_ge(S["tp_done"], t - 1)
                    pool.tensor_scalar(XN[:, t % 2, :], X[:, t, :], rstd[:, t:t + 1], nmr[:, t:t + 1],
                                       ALU.mult, ALU.add).then_inc(S["xn_done"], 1)
                pool.wait_ge(S["mask_done"], 3)
                pool.wait_ge(S["pj_lo"], 5)
                block_keys(pool, 0, 0)
                block_keys(pool, 1, 1)

            @block.tensor
            def _(pe):
                def transposes(blk):
                    for i in range(BT):
                        pe.wait_ge(S["xn_done"], blk * BT + (i + 1))
                        if not (isinstance(blk, int) and blk == 0 and i < 2):
                            pe.wait_ge(S["tp_lo"], blk * BT + (i - 1))
                        for k in range(KC):
                            last = pe.transpose(tp[i % 2][:, k * P:(k + 1) * P], XN[:, i % 2, k * P:(k + 1) * P], ident[:, :])
                        last.then_inc(S["tp_done"], 1)

                def project(blk, units):
                    for u in units:
                        if not (isinstance(blk, int) and blk == 0 and u < 2):
                            pe.wait_ge(S["pj_lo"], blk * 6 + (u - 1))
                        if u == 0:
                            pe.wait_ge(S["tp_lo"], blk * BT + BT)
                        steps = [(k, ab) for ab in PASSES for k in range(KC)]
                        if u < 5:
                            for n, (k, (a, b)) in enumerate(steps):
                                if u < 4:
                                    w = WQ[:, a, k, u, :, :]
                                else:
                                    w = WKV[:, a, k, 0, :]
                                last = pe.matmul(pj[u % 2][:, :], w, (XT if u < 4 else CT)[:, b, k, bass.ds(blk * BLOCK, BLOCK)],
                                                 start=n == 0, stop=n == len(steps) - 1)
                        else:
                            for i in range(BT):
                                for n, (k, (a, b)) in enumerate(steps):
                                    last = pe.matmul(pj[1][:, i * P:(i + 1) * P], CT[:, a, k, bass.ds(blk * BLOCK + i * P, P)],
                                                     WKV[:, b, k, 1, :], start=n == 0, stop=n == len(steps) - 1)
                        last.then_inc(S["pj_done"], 1)

                transposes(0)
                pe.wait_ge(S["qkv_lo"], 1)
                project(0, range(4))
                transposes(1)
                pe.wait_ge(S["qkv_lo"], 3)
                project(0, (4, 5))
                with pe.Fori(1, BLOCKS - 1) as blk:
                    project(blk, range(4))
                    transposes(blk + 1)
                    project(blk, (4, 5))
                project(BLOCKS - 1, range(6))

            def q_columns(j):
                return SQ[:, :, :].rearrange("p k (g j d) -> p k j g d", g=GROUPS, j=REP)[:, :, j, :, :]

            def tp_bank(i):
                return tp[i % 2][:, :].rearrange("p (k t) -> p k t", k=KC)

            def x_out(part_, blk, i):
                return XT[:, part_, :, bass.ds(blk * BLOCK + i * P, P)]

            def pj_views(part_, blk, u):
                if u < 4:
                    return (QT[:, part_, bass.ds(blk * BB, BB), u, :], pj[u % 2][:, :].rearrange("p (b t) -> p b t", b=BB))
                if u == 4:
                    return KT[:, part_, bass.ds(blk * BLOCK, BLOCK)], pj[0][:, :]
                return V[:, part_, bass.ds(blk * BT, BT), :], pj[1][:, :].rearrange("p (i d) -> p i d", i=BT)

            @block.scalar
            def _(act):
                def high_x(blk):
                    for i in range(BT):
                        act.wait_ge(S["tp_done"], blk * BT + (i + 1))
                        act.activation(x_out(0, blk, i), tp_bank(i), ACT.Copy).then_inc(S["tp_hi"], 1)

                def high(blk, units):
                    for u in units:
                        act.wait_ge(S["pj_done"], blk * 6 + (u + 1))
                        to, bank = pj_views(0, blk, u)
                        act.activation(to, bank, ACT.Copy, scale=UNSCALE).then_inc(S["pj_hi"], 1)

                act.wait_ge(S["sq_ld"], 16)
                for j in range(REP):
                    last = act.activation(WQ[:, 0, :, j, :, :], q_columns(j), ACT.Copy, scale=WEIGHT_SCALE)
                last.then_inc(S["qkv_hi"], 1)
                high_x(0)
                stats_scalar(act, 2, (BLOCKS - 1,))
                act.wait_ge(S["skv_ld"], 32)
                act.activation(WKV[:, 0, :, :, :], SKV[:, :, :, :], ACT.Copy, scale=WEIGHT_SCALE).then_inc(S["qkv_hi"], 1)
                act.wait_ge(S["so_ld"], 16 * GROUPS)
                act.activation(WO[:, 0, :, :], SO[:, :, :], ACT.Copy, scale=WEIGHT_SCALE).then_inc(S["qkv_hi"], 1)
                with act.Fori(0, BLOCKS - 1) as blk:
                    high(blk, range(4))
                    high_x(blk + 1)
                    high(blk, (4, 5))
                high(BLOCKS - 1, range(6))

            @block.vector
            def _(dve):
                def low_x(blk, i):
                    dve.wait_ge(S["tp_hi"], blk * BT + (i + 1))
                    dve.tensor_tensor(x_out(1, blk, i), tp_bank(i), x_out(0, blk, i), ALU.subtract).then_inc(S["tp_lo"], 1)

                def low(blk, units):
                    for u in units:
                        dve.wait_ge(S["pj_hi"], blk * 6 + (u + 1))
                        to, bank = pj_views(1, blk, u)
                        dve.scalar_tensor_tensor(out=to, in0=bank, scalar=UNSCALE, in1=pj_views(0, blk, u)[0],
                                                 op0=ALU.mult, op1=ALU.subtract).then_inc(S["pj_lo"], 1)

                dve.wait_ge(S["qkv_hi"], 1)
                for j in range(REP):
                    for k in range(KC):
                        last = dve.scalar_tensor_tensor(out=WQ[:, 1, k, j, :, :], in0=q_columns(j)[:, k, :, :], scalar=WEIGHT_SCALE,
                                                        in1=WQ[:, 0, k, j, :, :], op0=ALU.mult, op1=ALU.subtract)
                last.then_inc(S["qkv_lo"], 1)
                for i in range(BT):
                    low_x(0, i)
                stats_vector(dve, 2, (BLOCKS - 1,))
                for n, (w, raw) in enumerate(((WKV, SKV), (WO, SO))):
                    dve.wait_ge(S["qkv_hi"], n + 2)
                    full = (slice(None),) * (len(raw.shape) - 1)
                    dve.scalar_tensor_tensor(out=w[(slice(None), 1) + full], in0=raw[(slice(None),) + full],
                                             scalar=WEIGHT_SCALE, in1=w[(slice(None), 0) + full],
                                             op0=ALU.mult, op1=ALU.subtract).then_inc(S["qkv_lo"], 1)
                with dve.Fori(0, BLOCKS - 1) as blk:
                    low(blk, range(4))
                    for i in range(BT):
                        low_x(blk + 1, i)
                    low(blk, (4, 5))
                low(BLOCKS - 1, range(6))

        with ExitStack() as part:
            VM = sb(part, "VM", [P, 2, 2, 2, 640], F16)
            E = sb(part, "E1", [P, 2, 4, GROUPS, SEQ], F32)
            ST = sb(part, "ST1", [P, 3, 4, GROUPS], F32)
            PT = sb(part, "PT1", [P, 2, 4, 2, 256], F16)
            OT = sb(part, "OT1", [P, 2, 2, REP, P], F16)
            XO = sb(part, "XO", [P, 2, DIM], F32)
            sc = [pb(part, f"sc1_{i}") for i in range(4)]
            tp = [pb(part, f"a1_tp{i}") for i in range(2)]
            ob = pb(part, "ob1")
            xp = pb(part, "a1_xp")
            names = ("zeroed vm_done sc_done max_done sub_done exp_done sum_done rcp_done p_done tp_done "
                     "tp_hi tp_lo ot_done ot_hi ot_lo xp_done xp_out x_acc")
            S = {n: sem(part, "a1_" + n) for n in names.split()}
            block = part.enter_context(nc.Block())

            def n_of(p, r, per, c):
                return p * (2 * per) + (r * per + c)

            def first(p, r):
                return isinstance(p, int) and p == 0 and r == 0

            @block.sync
            def _(sp):
                load_weights2(sp)

            @block.gpsimd
            def _(pool):
                pool.memset(VM[:, :, :, :, :], 0.0).then_inc(S["zeroed"], 1)

                def next_keys(p, r, t):
                    pool.wait_ge(S["sc_done"], n_of(p - 1, r, 4, 4))
                    block_keys(pool, r, t)

                def normalise(p, r, us):
                    for u in us:
                        pool.wait_ge(S["rcp_done"], n_of(p, r, 2, u // 2 + 1))
                        e = E[:, r, u, :, :]
                        pool.tensor_tensor(e, e, ST[:, 2, u, :].unsqueeze(2).to_broadcast([P, GROUPS, SEQ]),
                                           ALU.mult).then_inc(S["p_done"], 1)

                def add_x(p, r, t):
                    pool.wait_ge(S["xp_out"], n_of(p, r, 1, 1))
                    pool.tensor_tensor(X[:, t, :], X[:, t, :], XO[:, r, :], ALU.add).then_inc(S["x_acc"], 1)

                for r in range(2):
                    normalise(0, r, range(4))
                    next_keys(1, r, 2 + r)
                with pool.Fori(1, HALF - 1) as p:
                    for r in range(2):
                        normalise(p, r, range(4))
                        next_keys(p + 1, r, 2 * p + 2 + r)
                        add_x(p - 1, r, 2 * p - 2 + r)
                for r in range(2):
                    normalise(HALF - 1, r, range(4))
                    add_x(HALF - 2, r, TILES - 4 + r)
                for r in range(2):
                    add_x(HALF - 1, r, TILES - 2 + r)

            @block.tensor
            def _(pe):
                def scores(p, r, t, us):
                    for u in us:
                        b, jp = u // 2, u % 2
                        pe.wait_ge(km_done, n_of(p, r, 2, 2))
                        if not first(p, r):
                            pe.wait_ge(S["sub_done"], n_of(p, r, 4, u - 3))
                        for n, (qa, ka) in enumerate(PASSES):
                            last = pe.matmul(sc[u][:, :], QT[:, qa, 2 * t + b, 2 * jp:2 * jp + 2, :], KM[:, r, ka, :, b, :],
                                             start=n == 0, stop=n == 2)
                        last.then_inc(S["sc_done"], 1)

                def transpose_probs(p, r, b):
                    pe.wait_ge(S["p_done"], n_of(p, r, 4, 2 * b + 2))
                    for h in range(2):
                        u = 2 * b + h
                        if u >= 2:
                            pe.wait_ge(S["tp_lo"], n_of(p, r, 4, u - 1))
                        for q in range(2):
                            for jp in range(2):
                                g = 4 * h + 2 * q
                                last = pe.transpose(tp[h][:, q * 256 + jp * P:q * 256 + (jp + 1) * P],
                                                    E[:, r, 2 * b + jp, g:g + 2, :], ident[:, :])
                        last.then_inc(S["tp_done"], 1)

                def weigh_values(p, r, b):
                    if b == 0:
                        pe.wait_ge(S["vm_done"], n_of(p, r, 1, 1))
                        if not first(p, r):
                            pe.wait_ge(S["ot_lo"], n_of(p, r, 1, 0))
                    n = 0
                    for h in range(2):
                        pe.wait_ge(S["tp_lo"], n_of(p, r, 4, 2 * b + h + 1))
                        for q in range(2):
                            gp = 2 * h + q
                            for va, pa in PASSES:
                                last = pe.matmul(ob[:, b * 256:(b + 1) * 256], VM[:, r, va, b, gp * P:(gp + 1) * P],
                                                 PT[:, pa, 2 * b + h, q, :], start=n == 0, stop=n == 11)
                                n += 1
                    if b == 1:
                        last.then_inc(S["ot_done"], 1)

                def project_out(p, r):
                    pe.wait_ge(S["ot_lo"], n_of(p, r, 1, 1))
                    if not first(p, r):
                        pe.wait_ge(S["xp_out"], n_of(p, r, 1, 0))
                    for n, (j, (a, b)) in enumerate([(j, ab) for j in range(REP) for ab in PASSES]):
                        last = pe.matmul(xp[:, :], OT[:, r, a, j, :], WO[:, b, j, :], start=n == 0, stop=n == 3 * REP - 1)
                    last.then_inc(S["xp_done"], 1)

                def tile(cur, old, out):
                    if old:
                        transpose_probs(*old, 0)
                    if cur:
                        scores(*cur, (0, 1))
                    if old:
                        transpose_probs(*old, 1)
                        weigh_values(*old, 0)
                    if cur:
                        scores(*cur, (2, 3))
                    if old:
                        weigh_values(*old, 1)
                    if out:
                        project_out(*out)

                tile((0, 0, 0), None, None)
                tile((0, 1, 1), (0, 0), None)
                with pe.Fori(1, HALF) as p:
                    tile((p, 0, 2 * p), (p - 1, 1), (p - 1, 0))
                    tile((p, 1, 2 * p + 1), (p, 0), (p - 1, 1))
                tile(None, (HALF - 1, 1), (HALF - 1, 0))
                project_out(HALF - 1, 1)

            def t_bank(u):
                return tp[u % 2][:, :].rearrange("p (q n) -> p q n", q=2)

            def o_bank():
                return ob[:, :].rearrange("p (b j t) -> p b j t", b=2, j=REP)

            def o_out(r, part_):
                return OT[:, r, part_, :, :].rearrange("p j (b t) -> p b j t", b=2)

            @block.scalar
            def _(act):
                def place_values(p, r, t):
                    if not (isinstance(p, int) and p == 0):
                        act.wait_ge(S["ot_done"], n_of(p - 1, r, 1, 1))
                    for b in range(2):
                        for h in range(2):
                            src = V[b * 64:(b + 1) * 64, :, t, :].rearrange("p s (q h d) -> p s q h d", q=4, h=2)[:, :, :, h, :]
                            to = VM[h * 64:(h + 1) * 64, r, :, b, :].rearrange("p s (q c) -> p s q c", q=4)[:, :, :, h * HEAD1:(h + 1) * HEAD1]
                            last = act.activation(to, src, ACT.Copy)
                    last.then_inc(S["vm_done"], 1)

                def exp(p, r, u):
                    act.wait_ge(S["sub_done"], n_of(p, r, 4, u + 1))
                    act.activation(E[:, r, u, :, :], E[:, r, u, :, :], ACT.Exp, scale=exp_scale).then_inc(S["exp_done"], 1)

                def high(p, r, u):
                    act.wait_ge(S["tp_done"], n_of(p, r, 4, u + 1))
                    act.activation(PT[:, 0, u, :, :], t_bank(u), ACT.Copy).then_inc(S["tp_hi"], 1)

                def out_x(p, r):
                    act.wait_ge(S["xp_done"], n_of(p, r, 1, 1))
                    if not (isinstance(p, int) and p == 0):
                        act.wait_ge(S["x_acc"], n_of(p, r, 1, -1))
                    act.activation(XO[:, r, :], xp[:, :], ACT.Copy, scale=UNSCALE).then_inc(S["xp_out"], 1)

                def tile(cur, old, out, place=None):
                    if old:
                        for u in range(4):
                            high(*old, u)
                    if cur:
                        exp(*cur, 0)
                        exp(*cur, 1)
                    if old:
                        act.wait_ge(S["ot_done"], n_of(*old, 1, 1))
                        act.activation(o_out(old[1], 0), o_bank(), ACT.Copy).then_inc(S["ot_hi"], 1)
                    if cur:
                        exp(*cur, 2)
                        exp(*cur, 3)
                    if place:
                        place_values(*place)
                    if out:
                        out_x(*out)

                act.wait_ge(S["zeroed"], 1)
                place_values(0, 0, 0)
                place_values(0, 1, 1)
                tile((0, 0), None, None)
                tile((0, 1), (0, 0), None)
                tile((1, 0), (0, 1), (0, 0), (1, 0, 2))
                tile((1, 1), (1, 0), (0, 1), (1, 1, 3))
                with act.Fori(2, HALF) as p:
                    tile((p, 0), (p - 1, 1), (p - 1, 0), (p, 0, 2 * p))
                    tile((p, 1), (p, 0), (p - 1, 1), (p, 1, 2 * p + 1))
                tile(None, (HALF - 1, 1), (HALF - 1, 0))
                out_x(HALF - 1, 1)

            @block.vector
            def _(dve):
                def scores_less_max(p, r, us):
                    s3 = [sc[u][:, :].rearrange("p (g k) -> p g k", g=GROUPS) for u in range(4)]
                    for u in us:
                        dve.wait_ge(S["sc_done"], n_of(p, r, 4, u + 1))
                        dve.reduce_max(ST[:, 0, u, :], s3[u], AX.X).then_inc(S["max_done"], 1)
                    if not (isinstance(p, int) and p == 0):
                        dve.wait_ge(S["tp_done"], n_of(p - 1, r, 4, 4))
                    for u in us:
                        dve.wait_ge(S["max_done"], n_of(p, r, 4, u + 1))
                        dve.tensor_tensor(E[:, r, u, :, :], s3[u], ST[:, 0, u, :].unsqueeze(2).to_broadcast([P, GROUPS, SEQ]),
                                          ALU.subtract).then_inc(S["sub_done"], 1)

                def sums(p, r, b):
                    us = slice(2 * b, 2 * b + 2)
                    dve.wait_ge(S["exp_done"], n_of(p, r, 4, 2 * b + 2))
                    dve.reduce_sum(ST[:, 1, us, :], E[:, r, us, :, :], AX.X).then_inc(S["sum_done"], 1)
                    dve.wait_ge(S["sum_done"], n_of(p, r, 2, b + 1))
                    if not first(p, r):
                        dve.wait_ge(S["p_done"], n_of(p, r, 4, 2 * b - 2))
                    dve.reciprocal(ST[:, 2, us, :], ST[:, 1, us, :]).then_inc(S["rcp_done"], 1)

                def low(p, r, u):
                    dve.wait_ge(S["tp_hi"], n_of(p, r, 4, u + 1))
                    dve.tensor_tensor(PT[:, 1, u, :, :], t_bank(u), PT[:, 0, u, :, :], ALU.subtract).then_inc(S["tp_lo"], 1)

                def low_o(p, r):
                    dve.wait_ge(S["ot_hi"], n_of(p, r, 1, 1))
                    dve.tensor_tensor(o_out(r, 1), o_bank(), o_out(r, 0), ALU.subtract).then_inc(S["ot_lo"], 1)

                def tile(cur, old):
                    if old:
                        low(*old, 0)
                        low(*old, 1)
                    if cur:
                        scores_less_max(*cur, (0, 1))
                    if old:
                        low(*old, 2)
                        low(*old, 3)
                    if cur:
                        sums(*cur, 0)
                        scores_less_max(*cur, (2, 3))
                    if old:
                        low_o(*old)
                    if cur:
                        sums(*cur, 1)

                tile((0, 0), None)
                tile((0, 1), (0, 0))
                with dve.Fori(1, HALF) as p:
                    tile((p, 0), (p - 1, 1))
                    tile((p, 1), (p, 0))
                tile(None, (HALF - 1, 1))


def ffn1(nc, sb, pb, sem, X, ident, rstd, nmr, ln, staged, loaded, out):
    OMS = 4
    AHEAD = 2
    ADDS = 4
    with ExitStack() as ph:
        SW, SC, BI, AS = staged
        WT = sb(ph, "WT", [P, 2, KC, DIM], F16)
        CTT = sb(ph, "CTT", [P, 2, KC, CLUSTERS], F16)
        OH = sb(ph, "OH", [CLUSTERS, DIM], F16)
        cid = sb(ph, "cid", [CLUSTERS, 1], F32)
        cidi = sb(ph, "cidi", [CLUSTERS, 1], I32)
        ones = sb(ph, "ones", [P, P], F16)
        XN = sb(ph, "XN2", [P, 2, DIM], F32)
        XT = sb(ph, "XT2", [P, 2, 2, KC, P], F16)
        DN = sb(ph, "DN", [P, TILES, DIM], F32)
        EX = sb(ph, "EX", [P, 2, CLUSTERS], F32)
        cs = sb(ph, "cs", [P, 2, 4], F32)
        HT = sb(ph, "HT", [P, 2, CLUSTERS], F32)
        HA = sb(ph, "HA", [P, CLUSTERS], F16)
        QS = sb(ph, "QS", [P, TILES], F32)
        CSEL = sb(ph, "CSEL", [CLUSTERS, P], F16)
        RSEL = sb(ph, "RSEL", [P, DIM], F32)
        OM = sb(ph, "OM", [P, OMS, DIM], F32)
        tp = [pb(ph, f"t2_{i}") for i in range(2)]
        dn = [pb(ph, f"dn{i}") for i in range(2)]
        lg = [pb(ph, f"lg{i}") for i in range(2)]
        rs = [pb(ph, f"rs{i}") for i in range(2)]
        names = ("ones_done cid_done oh_done xn_done tp_done tp_hi tp_lo dn_done lg_done dn_out "
                 "max_done nmax_done exp_done rcp_done hit_done any_done qs_done count_done csel_done row_done rsel_done om_done x_done x_done_v stored")
        S = {n: sem(ph, "f1_" + n) for n in names.split()} | loaded
        moments, scales, stats_scalar, stats_ready, parts_before = ln
        block = ph.enter_context(nc.Block())
        HALF = TILES // 2
        FIRST = 5
        LOGIT = UNSCALE / TEMPERATURE

        def w_bank(u):
            if u < 4:
                return tp[u % 2][:, :].rearrange("p (k t) -> p k t", k=KC)
            return tp[0][:, 0:KC * CLUSTERS].rearrange("p (k t) -> p k t", k=KC)

        def w_out(part, u):
            return WT[:, part, :, u * P:(u + 1) * P] if u < 4 else CTT[:, part, :, :]

        def x_bank(r):
            return tp[(FIRST + r) % 2][:, :].rearrange("p (k t) -> p k t", k=KC)

        def live(p):
            return not isinstance(p, int) or p < HALF

        @block.sync
        def _(sp):
            for i in range(TILES):
                if i % ADDS == ADDS - 1:
                    sp.wait_ge(S["x_done_v"], i // ADDS + 1)
                else:
                    sp.wait_ge(S["x_done"], i - i // ADDS + 1)
                sp.dma_start(out[i * P:(i + 1) * P, :], X[:, i, :]).then_inc(S["stored"], 16)
            sp.wait_ge(S["stored"], 16 * TILES)

        @block.gpsimd
        def _(pool):
            pool.memset(ones[:, :], 1.0).then_inc(S["ones_done"], 1)
            pool.memset(HA[:, :], 0.0).then_inc(S["ones_done"], 1)
            pool.iota(cidi[:, :], pattern=[[0, 1]], base=0, channel_multiplier=1).then_inc(S["cid_done"], 1)
            pool.wait_ge(S["cid_done"], 1)
            pool.tensor_copy(cid[:, :], cidi[:, :]).then_inc(S["cid_done"], 1)

            for t in range(TILES):
                pool.wait_ge(stats_ready, parts_before(3) + t // 2 + 1)
                if t >= 2:
                    pool.wait_ge(S["tp_done"], FIRST + t - 1)
                pool.tensor_scalar(XN[:, t % 2, :], X[:, t, :], rstd[:, t:t + 1], nmr[:, t:t + 1],
                                   ALU.mult, ALU.add).then_inc(S["xn_done"], 1)
            for i in range(TILES):
                if i % ADDS != ADDS - 1:
                    pool.wait_ge(S["om_done"], i + 1)
                    pool.tensor_tensor(X[:, i, :], X[:, i, :], OM[:, i % OMS, :], ALU.add).then_inc(S["x_done"], 1)

        @block.tensor
        def _(pe):
            pe.wait_ge(S["w_ld"], 16)
            for u in range(4):
                if u >= 2:
                    pe.wait_ge(S["tp_lo"], u - 1)
                for k in range(KC):
                    last = pe.transpose(tp[u % 2][:, k * P:(k + 1) * P], SW[:, u, k * P:(k + 1) * P], ident[:, :])
                last.then_inc(S["tp_done"], 1)
            pe.wait_ge(S["c_ld"], 16)
            pe.wait_ge(S["tp_lo"], 3)
            for k in range(KC):
                last = pe.transpose(tp[0][:, k * CLUSTERS:(k + 1) * CLUSTERS], SC[:, k * P:(k + 1) * P],
                                    ident[0:CLUSTERS, 0:CLUSTERS])
            last.then_inc(S["tp_done"], 1)

            def transposes(p, r):
                pe.wait_ge(S["xn_done"], p * 2 + (r + 1))
                pe.wait_ge(S["tp_lo"], p * 2 + (FIRST + r - 1))
                for k in range(KC):
                    last = pe.transpose(tp[(FIRST + r) % 2][:, k * P:(k + 1) * P], XN[:, r, k * P:(k + 1) * P], ident[:, :])
                last.then_inc(S["tp_done"], 1)

            def products(p, r):
                pe.wait_ge(S["tp_lo"], p * 2 + (FIRST + r + 1))
                if not (isinstance(p, int) and p == 0):
                    pe.wait_ge(S["dn_out"], p * 2 + (r - 1))
                    pe.wait_ge(S["exp_done"], p * 2 + (r - 1))
                for n, (k, (a, b)) in enumerate([(k, ab) for k in range(KC) for ab in PASSES]):
                    last = pe.matmul(lg[r][:, 0:CLUSTERS], XT[:, r, a, k, :], CTT[:, b, k, :], start=n == 0, stop=n == 3 * KC - 1)
                last.then_inc(S["lg_done"], 1)
                for n, (k, (a, b)) in enumerate([(k, ab) for k in range(KC) for ab in PASSES]):
                    last = pe.matmul(dn[r][:, :], XT[:, r, a, k, :], WT[:, b, k, :], start=n == 0, stop=n == 3 * KC - 1)
                last.then_inc(S["dn_done"], 1)

            transposes(0, 0)
            transposes(0, 1)
            products(0, 0)
            transposes(1, 0)
            products(0, 1)
            transposes(1, 1)
            products(1, 0)
            with pe.Fori(2, HALF) as p:
                transposes(p, 0)
                products(p - 1, 1)
                transposes(p, 1)
                products(p, 0)
            products(HALF - 1, 1)
            pe.wait_ge(S["any_done"], TILES)
            pe.matmul(rs[0][0:CLUSTERS, 0:P], HA[:, :], ones[:, :], start=True, stop=True).then_inc(S["count_done"], 1)
            pe.wait_ge(S["csel_done"], 1)
            pe.wait_ge(S["oh_done"], 1)
            pe.matmul(rs[1][:, :], CSEL[:, :], OH[:, :], start=True, stop=True).then_inc(S["row_done"], 1)

        @block.scalar
        def _(act):
            for u in range(FIRST):
                act.wait_ge(S["tp_done"], u + 1)
                act.activation(w_out(0, u), w_bank(u), ACT.Copy, scale=WEIGHT_SCALE).then_inc(S["tp_hi"], 1)
                if u == 1:
                    stats_scalar(act, 3, (0,))
            stats_scalar(act, 3, (1,))

            def high(p, r):
                act.wait_ge(S["tp_done"], p * 2 + (FIRST + r + 1))
                act.activation(XT[:, r, 0, :, :], x_bank(r), ACT.Copy).then_inc(S["tp_hi"], 1)

            def exps(p, r):
                act.wait_ge(S["nmax_done"], p * 2 + (r + 1))
                act.activation(EX[:, r, :], lg[r][:, 0:CLUSTERS], ACT.Exp, bias=cs[:, r, 1:2], scale=LOGIT,
                               accum_out=cs[:, r, 2:3]).then_inc(S["exp_done"], 1)

            high(0, 0)
            high(0, 1)
            exps(0, 0)
            def step(p):
                high(p, 0)
                exps(p - 1, 1)
                high(p, 1)
                exps(p, 0)
                if live(p + AHEAD):
                    stats_scalar(act, 3, (p + AHEAD,))

            stats_scalar(act, 3, (AHEAD,))
            with act.Fori(1, HALF - AHEAD) as p:
                step(p)
            for p in range(HALF - AHEAD, HALF):
                step(p)
            exps(HALF - 1, 1)

        @block.vector
        def _(dve):
            moments(dve, 3, 0)
            for u in range(FIRST):
                dve.wait_ge(S["tp_hi"], u + 1)
                dve.scalar_tensor_tensor(out=w_out(1, u), in0=w_bank(u), scalar=WEIGHT_SCALE, in1=w_out(0, u),
                                         op0=ALU.mult, op1=ALU.subtract).then_inc(S["tp_lo"], 1)
                if u == 1:
                    scales(dve, 3, 0)
                    moments(dve, 3, 1)
            scales(dve, 3, 1)
            dve.wait_ge(S["ones_done"], 2)
            dve.wait_ge(S["b_ld"], 16)
            dve.wait_ge(S["a_ld"], 16)
            dve.wait_ge(S["cid_done"], 2)
            dve.tensor_scalar(OH[:, :], AS[:, :], cid[:, 0:1], None, ALU.is_equal).then_inc(S["oh_done"], 1)

            def low(p, r):
                dve.wait_ge(S["tp_hi"], p * 2 + (FIRST + r + 1))
                dve.tensor_tensor(XT[:, r, 1, :, :], x_bank(r), XT[:, r, 0, :, :], ALU.subtract).then_inc(S["tp_lo"], 1)

            def maxima(p, r):
                at = p * 2 + (r + 1)
                dve.wait_ge(S["lg_done"], at)
                dve.reduce_max(cs[:, r, 0:1], lg[r][:, 0:CLUSTERS], AX.X).then_inc(S["max_done"], 1)
                dve.wait_ge(S["max_done"], at)
                dve.tensor_scalar(cs[:, r, 1:2], cs[:, r, 0:1], -LOGIT, None, ALU.mult).then_inc(S["nmax_done"], 1)

            def dense_out(p, r):
                dve.wait_ge(S["dn_done"], p * 2 + (r + 1))
                dve.scalar_tensor_tensor(out=DN[:, 2 * p + r, :], in0=dn[r][:, :], scalar=UNSCALE, in1=BI[:, :],
                                         op0=ALU.mult, op1=ALU.add).then_inc(S["dn_out"], 1)

            def hits(p, r):
                at = p * 2 + (r + 1)
                dve.wait_ge(S["exp_done"], at)
                dve.reciprocal(cs[:, r, 3:4], cs[:, r, 2:3]).then_inc(S["rcp_done"], 1)
                dve.wait_ge(S["rcp_done"], at)
                dve.tensor_scalar(HT[:, r, :], EX[:, r, :], cs[:, r, 3:4], THRESHOLD, ALU.mult, ALU.is_gt).then_inc(S["hit_done"], 1)
                dve.wait_ge(S["hit_done"], at)
                dve.reduce_max(QS[:, bass.ds(2 * p + r, 1)], HT[:, r, :], AX.X).then_inc(S["qs_done"], 1)
                dve.tensor_tensor(HA[:, :], HA[:, :], HT[:, r, :], ALU.max).then_inc(S["any_done"], 1)

            def step(p):
                low(p, 0)
                maxima(p - 1, 1)
                hits(p - 1, 0)
                dense_out(p - 1, 0)
                if live(p + AHEAD):
                    moments(dve, 3, p + AHEAD)
                low(p, 1)
                maxima(p, 0)
                hits(p - 1, 1)
                dense_out(p - 1, 1)
                if live(p + AHEAD):
                    scales(dve, 3, p + AHEAD)

            low(0, 0)
            low(0, 1)
            moments(dve, 3, AHEAD)
            maxima(0, 0)
            scales(dve, 3, AHEAD)
            for p in range(1, HALF):
                step(p)
            p = HALF - 1
            maxima(p, 1)
            hits(p, 0)
            dense_out(p, 0)
            hits(p, 1)
            dense_out(p, 1)
            dve.wait_ge(S["count_done"], 1)
            dve.tensor_scalar(CSEL[:, :], rs[0][0:CLUSTERS, 0:P], 0.0, None, ALU.is_gt).then_inc(S["csel_done"], 1)
            dve.wait_ge(S["row_done"], 1)
            dve.tensor_scalar(RSEL[:, :], rs[1][:, :], 0.0, None, ALU.is_gt).then_inc(S["rsel_done"], 1)
            dve.wait_ge(S["rsel_done"], 1)
            dve.wait_ge(S["qs_done"], TILES)
            for i in range(TILES):
                if i >= OMS:
                    if (i - OMS) % ADDS == ADDS - 1:
                        dve.wait_ge(S["x_done_v"], (i - OMS) // ADDS + 1)
                    else:
                        dve.wait_ge(S["x_done"], i - OMS - (i - OMS) // ADDS + 1)
                dve.scalar_tensor_tensor(out=OM[:, i % OMS, :], in0=DN[:, i, :], scalar=QS[:, i:i + 1], in1=RSEL[:, :],
                                         op0=ALU.mult, op1=ALU.mult).then_inc(S["om_done"], 1)
                if i % ADDS == ADDS - 1:
                    dve.wait_ge(S["om_done"], i + 1)
                    dve.tensor_tensor(X[:, i, :], X[:, i, :], OM[:, i % OMS, :], ALU.add).then_inc(S["x_done_v"], 1)


_INS = ["x", "ctx_4096", "L0_xattn_wq", "L0_xattn_wk", "L0_xattn_wv", "L0_xattn_wo",
        "L0_ffn_W0", "L0_ffn_bias0", "L0_ffn_W1", "L0_ffn_bias1",
        "L1_xattn_Wq", "L1_xattn_Wk", "L1_xattn_Wv", "L1_xattn_Wo",
        "L1_ffn_weight", "L1_ffn_bias", "L1_ffn_centroids", "L1_ffn_assignments"]


def kernel(**inputs):
    import numpy as _np
    import concourse.bacc as _bacc
    from concourse import mybir as _mybir
    from concourse.bass_utils import run_bass_kernel_spmd as _run

    nc = _bacc.Bacc("TRN2", target_bir_lowering=False, num_devices=1)
    arrays, args = {}, []
    for name in _INS:
        a = _np.ascontiguousarray(inputs[name])
        if name in ("x", "ctx_4096"):
            a = a.reshape(TOKENS, DIM)
        arrays[f"in_{name}"] = a
        args.append(nc.dram_tensor(f"in_{name}", a.shape, _mybir.dt.from_np(a.dtype), kind="ExternalInput").ap())
    args.append(nc.dram_tensor("out_0", (TOKENS, DIM), _mybir.dt.float32, kind="ExternalOutput").ap())
    fused_decoder_kernel(nc, *args)
    r = _run(nc, [arrays], core_ids=[0])
    return r.results[0]["out_0"].reshape(BATCH, SEQ, DIM)
```
